# Optimizing a Trainium2 kernel written in Bass

```python
import numpy as np
import jax
import jax.numpy as jnp

def _softmax(x, axis=-1):
    return jax.nn.softmax(x, axis=axis)
def _gelu(x):
    return jax.nn.gelu(x, approximate=True)
def _silu(x):
    return jax.nn.silu(x)
def _sigmoid(x):
    return jax.nn.sigmoid(x)
def _layernorm(x, axis=-1, eps=1e-5):
    m = jnp.mean(x, axis=axis, keepdims=True)
    v = jnp.var(x, axis=axis, keepdims=True)
    return (x - m) / jnp.sqrt(v + eps)
def _scatter_add(tgt, idx, src, axis=0):
    return tgt.at[idx].add(src)
def _segment_sum(src, seg, n):
    return jax.ops.segment_sum(src, seg, n)

kernel_name = 'mk_adj_preln_d4_adj_128_f2ca2a'

def setup_inputs(seed: int = 0):
    np.random.seed(seed)
    _w = jnp.asarray
    def _rec_inputs():
        import jax
        import jax.numpy as jnp
        _gk = jax.random.key(seed)
        x = -0.0005207 + 1.001 * jax.random.normal(jax.random.fold_in(_gk, 1), (64, 256, 128), jnp.float32)
        _a = jax.random.bernoulli(jax.random.fold_in(_gk, 2), 0.015625, (64, 256, 256))
        _a = jnp.logical_or(_a, jnp.swapaxes(_a, -1, -2))
        _a = jnp.logical_or(_a, jnp.eye(256, dtype=bool))
        _af = _a.astype(jnp.float32)
        _af = _af * jax.random.uniform(jax.random.fold_in(_gk, 3), (64, 256, 256), jnp.float32, 0.05, 5.41998)
        adj = _af
        return x, adj
    x, adj = _rec_inputs()
    def _L0_gnn_setup():
        import jax, jax.numpy as jnp
        import numpy as np
        B, N, H = (2, 8192, 128)
        EPS = 1e-06
        key = jax.random.key(seed)
        k1, k2, k3, k4 = jax.random.split(key, 4)
        x = jax.random.normal(k1, (B, N, H), dtype=jnp.float32)
        adj = jax.random.normal(k2, (B, N, N), dtype=jnp.float32)
        W = jax.random.normal(k3, (H, H), dtype=jnp.float32)
        b = jax.random.normal(k4, (H,), dtype=jnp.float32)
        return {'x': x, 'adj': adj, 'W': W, 'b': b}
    _L0_gnn_all = _L0_gnn_setup()
    _L0_gnn_in = {k: v for k, v in _L0_gnn_all.items() if k in ('W', 'b', )}
    del _L0_gnn_all

    def _L1_gnn_setup():
        import jax, jax.numpy as jnp
        import numpy as np
        C = 1.0
        MIN_NORM = 1e-15
        EPS = 1e-07

        def _sqnorm(x):
            return jnp.sum(x * x, axis=-1, keepdims=True)

        def _norm(x):
            return jnp.sqrt(jnp.maximum(_sqnorm(x), MIN_NORM))

        def _atanh(u):
            return jnp.arctanh(jnp.clip(u, -1.0 + EPS, 1.0 - EPS))

        def mobius_add(x, y, c):
            x2 = _sqnorm(x)
            y2 = _sqnorm(y)
            xy = jnp.sum(x * y, axis=-1, keepdims=True)
            num = (1.0 + 2.0 * c * xy + c * y2) * x + (1.0 - c * x2) * y
            den = 1.0 + 2.0 * c * xy + c * c * x2 * y2
            return num / jnp.maximum(den, MIN_NORM)

        def logmap0(p, c):
            sc = jnp.sqrt(c)
            pn = _norm(p)
            return p / pn / sc * _atanh(sc * pn)

        def logmap(p1, p2, c):
            sub = mobius_add(-p1, p2, c)
            sn = _norm(sub)
            lam = 2.0 / jnp.maximum(1.0 - c * _sqnorm(p1), MIN_NORM)
            sc = jnp.sqrt(c)
            return 2.0 / sc / lam * _atanh(sc * sn) * sub / sn

        def expmap(p, u, c):
            un = _norm(u)
            lam = 2.0 / jnp.maximum(1.0 - c * _sqnorm(p), MIN_NORM)
            sc = jnp.sqrt(c)
            second = jnp.tanh(sc * lam * un / 2.0) * u / (sc * un)
            return mobius_add(p, second, c)
        key = jax.random.key(seed)
        k1, k2, k3 = jax.random.split(key, 3)
        B, N, D = (1, 1024, 128)
        x = jax.random.normal(k1, (B, N, D), jnp.float32) * 0.02
        adj = (jax.random.uniform(k2, (B, N, N)) < 0.05).astype(jnp.float32)
        att_w = jax.random.normal(k3, (2 * D,), jnp.float32) * 0.1
        att_b = jnp.zeros((), jnp.float32)
        return {'x': x, 'adj': adj, 'att_w': att_w, 'att_b': att_b}
    _L1_gnn_all = _L1_gnn_setup()
    _L1_gnn_in = {k: v for k, v in _L1_gnn_all.items() if k in ('att_w', 'att_b', )}
    del _L1_gnn_all

    def _L2_gnn_setup():
        import jax, jax.numpy as jnp
        import numpy as np
        LN_EPS = 1e-05

        def _layernorm(x, gamma, beta):
            mu = jnp.mean(x, axis=-1, keepdims=True)
            var = jnp.mean(jnp.square(x - mu), axis=-1, keepdims=True)
            return (x - mu) * jax.lax.rsqrt(var + LN_EPS) * gamma + beta
        key = jax.random.key(seed)
        ks = jax.random.split(key, 10)
        B, N, D, O = (2, 512, 128, 128)
        node_features = jax.random.normal(ks[0], (B, N, D), dtype=jnp.float32)
        adjacency = jax.random.uniform(ks[1], (B, N, N), dtype=jnp.float32)
        s1 = 1.0 / np.sqrt(2 * D)
        s2 = 1.0 / np.sqrt(D + O)
        W1 = jax.random.uniform(ks[2], (2 * D, O), jnp.float32, -s1, s1)
        b1 = jax.random.uniform(ks[3], (O,), jnp.float32, -s1, s1)
        g1 = jnp.ones((O,), jnp.float32)
        be1 = jnp.zeros((O,), jnp.float32)
        W2 = jax.random.uniform(ks[4], (D + O, O), jnp.float32, -s2, s2)
        b2 = jax.random.uniform(ks[5], (O,), jnp.float32, -s2, s2)
        g2 = jnp.ones((O,), jnp.float32)
        be2 = jnp.zeros((O,), jnp.float32)
        return {'node_features': node_features, 'adjacency': adjacency, 'W1': W1, 'b1': b1, 'g1': g1, 'be1': be1, 'W2': W2, 'b2': b2, 'g2': g2, 'be2': be2}
    _L2_gnn_all = _L2_gnn_setup()
    _L2_gnn_in = {k: v for k, v in _L2_gnn_all.items() if k in ('W1', 'b1', 'g1', 'be1', 'W2', 'b2', 'g2', 'be2', )}
    del _L2_gnn_all

    def _L3_gnn_setup():
        import jax, jax.numpy as jnp
        import numpy as np
        B, N = (2, 4096)
        IN_DIMS = [128, 128, 256, 384]
        REP = 128
        OUT = 128
        NUM_LAYERS = 4
        EPS = 1e-12

        def _l2norm(x, axis):
            n = jnp.sqrt(jnp.sum(x * x, axis=axis, keepdims=True))
            return x / jnp.maximum(n, EPS)

        def _layer(nodes, adj, ws, bs, wd, bd, wn, bn, wu, bu):
            src = nodes @ ws + bs
            src_agg = jnp.einsum('bjv,bij->biv', src, _l2norm(adj, 2))
            dst = nodes @ wd + bd
            dst_agg = jnp.einsum('bjv,bji->biv', dst, _l2norm(adj, 1))
            self_rep = nodes @ wn + bn
            upd = jnp.concatenate([src_agg, self_rep, dst_agg], axis=2)
            return jnp.tanh(upd @ wu + bu)
        key = jax.random.key(seed)
        ks = jax.random.split(key, 2 + 8 * NUM_LAYERS)
        inp = {'nodes': jax.random.normal(ks[0], (B, N, IN_DIMS[0]), dtype=jnp.float32), 'adj': jax.random.uniform(ks[1], (B, N, N), dtype=jnp.float32)}
        ki = 2
        for i, din in enumerate(IN_DIMS):
            s = 1.0 / np.sqrt(din)
            su = 1.0 / np.sqrt(3 * REP)
            inp[f'ws{i}'] = jax.random.uniform(ks[ki + 0], (din, REP), minval=-s, maxval=s)
            inp[f'bs{i}'] = jax.random.uniform(ks[ki + 1], (REP,), minval=-s, maxval=s)
            inp[f'wd{i}'] = jax.random.uniform(ks[ki + 2], (din, REP), minval=-s, maxval=s)
            inp[f'bd{i}'] = jax.random.uniform(ks[ki + 3], (REP,), minval=-s, maxval=s)
            inp[f'wn{i}'] = jax.random.uniform(ks[ki + 4], (din, REP), minval=-s, maxval=s)
            inp[f'bn{i}'] = jax.random.uniform(ks[ki + 5], (REP,), minval=-s, maxval=s)
            inp[f'wu{i}'] = jax.random.uniform(ks[ki + 6], (3 * REP, OUT), minval=-su, maxval=su)
            inp[f'bu{i}'] = jax.random.uniform(ks[ki + 7], (OUT,), minval=-su, maxval=su)
            ki += 8
        return inp
    _L3_gnn_all = _L3_gnn_setup()
    _L3_gnn_in = {k: v for k, v in _L3_gnn_all.items() if k in ('ws0', 'bs0', 'wd0', 'bd0', 'wn0', 'bn0', 'wu0', 'bu0', 'ws1', 'bs1', 'wd1', 'bd1', 'wn1', 'bn1', 'wu1', 'bu1', 'ws2', 'bs2', 'wd2', 'bd2', 'wn2', 'bn2', 'wu2', 'bu2', 'ws3', 'bs3', 'wd3', 'bd3', 'wn3', 'bn3', 'wu3', 'bu3', )}
    del _L3_gnn_all

    return {
        "x": x,
        "adj": adj,
        "L0_gnn_W": _L0_gnn_in["W"],
        "L0_gnn_b": _L0_gnn_in["b"],
        "L1_gnn_att_w": _L1_gnn_in["att_w"],
        "L1_gnn_att_b": _L1_gnn_in["att_b"],
        "L2_gnn_W1": _L2_gnn_in["W1"],
        "L2_gnn_b1": _L2_gnn_in["b1"],
        "L2_gnn_g1": _L2_gnn_in["g1"],
        "L2_gnn_be1": _L2_gnn_in["be1"],
        "L2_gnn_W2": _L2_gnn_in["W2"],
        "L2_gnn_b2": _L2_gnn_in["b2"],
        "L2_gnn_g2": _L2_gnn_in["g2"],
        "L2_gnn_be2": _L2_gnn_in["be2"],
        "L3_gnn_ws0": _L3_gnn_in["ws0"],
        "L3_gnn_bs0": _L3_gnn_in["bs0"],
        "L3_gnn_wd0": _L3_gnn_in["wd0"],
        "L3_gnn_bd0": _L3_gnn_in["bd0"],
        "L3_gnn_wn0": _L3_gnn_in["wn0"],
        "L3_gnn_bn0": _L3_gnn_in["bn0"],
        "L3_gnn_wu0": _L3_gnn_in["wu0"],
        "L3_gnn_bu0": _L3_gnn_in["bu0"],
        "L3_gnn_ws1": _L3_gnn_in["ws1"],
        "L3_gnn_bs1": _L3_gnn_in["bs1"],
        "L3_gnn_wd1": _L3_gnn_in["wd1"],
        "L3_gnn_bd1": _L3_gnn_in["bd1"],
        "L3_gnn_wn1": _L3_gnn_in["wn1"],
        "L3_gnn_bn1": _L3_gnn_in["bn1"],
        "L3_gnn_wu1": _L3_gnn_in["wu1"],
        "L3_gnn_bu1": _L3_gnn_in["bu1"],
        "L3_gnn_ws2": _L3_gnn_in["ws2"],
        "L3_gnn_bs2": _L3_gnn_in["bs2"],
        "L3_gnn_wd2": _L3_gnn_in["wd2"],
        "L3_gnn_bd2": _L3_gnn_in["bd2"],
        "L3_gnn_wn2": _L3_gnn_in["wn2"],
        "L3_gnn_bn2": _L3_gnn_in["bn2"],
        "L3_gnn_wu2": _L3_gnn_in["wu2"],
        "L3_gnn_bu2": _L3_gnn_in["bu2"],
        "L3_gnn_ws3": _L3_gnn_in["ws3"],
        "L3_gnn_bs3": _L3_gnn_in["bs3"],
        "L3_gnn_wd3": _L3_gnn_in["wd3"],
        "L3_gnn_bd3": _L3_gnn_in["bd3"],
        "L3_gnn_wn3": _L3_gnn_in["wn3"],
        "L3_gnn_bn3": _L3_gnn_in["bn3"],
        "L3_gnn_wu3": _L3_gnn_in["wu3"],
        "L3_gnn_bu3": _L3_gnn_in["bu3"],
    }

def reference(x, adj, L0_gnn_W, L0_gnn_b, L1_gnn_att_w, L1_gnn_att_b, L2_gnn_W1, L2_gnn_b1, L2_gnn_g1, L2_gnn_be1, L2_gnn_W2, L2_gnn_b2, L2_gnn_g2, L2_gnn_be2, L3_gnn_ws0, L3_gnn_bs0, L3_gnn_wd0, L3_gnn_bd0, L3_gnn_wn0, L3_gnn_bn0, L3_gnn_wu0, L3_gnn_bu0, L3_gnn_ws1, L3_gnn_bs1, L3_gnn_wd1, L3_gnn_bd1, L3_gnn_wn1, L3_gnn_bn1, L3_gnn_wu1, L3_gnn_bu1, L3_gnn_ws2, L3_gnn_bs2, L3_gnn_wd2, L3_gnn_bd2, L3_gnn_wn2, L3_gnn_bn2, L3_gnn_wu2, L3_gnn_bu2, L3_gnn_ws3, L3_gnn_bs3, L3_gnn_wd3, L3_gnn_bd3, L3_gnn_wn3, L3_gnn_bn3, L3_gnn_wu3, L3_gnn_bu3):
    import jax
    import jax.numpy as jnp
    def _L0_gnn_ref(x, adj, W, b):
        import jax, jax.numpy as jnp
        import numpy as np
        B, N, H = (2, 8192, 128)
        EPS = 1e-06
        in_degrees = jnp.sum(jnp.abs(adj), axis=-1)
        norm = jnp.power(in_degrees + EPS, -0.5)[..., None]
        support = jnp.matmul(x, W)
        out = jnp.einsum('bmn,bnh->bmh', adj, support * norm) * norm
        return jax.nn.elu(out + b)

    def _L1_gnn_ref(x, adj, att_w, att_b):
        import jax, jax.numpy as jnp
        import numpy as np
        C = 1.0
        MIN_NORM = 1e-15
        EPS = 1e-07

        def _sqnorm(x):
            return jnp.sum(x * x, axis=-1, keepdims=True)

        def _norm(x):
            return jnp.sqrt(jnp.maximum(_sqnorm(x), MIN_NORM))

        def _atanh(u):
            return jnp.arctanh(jnp.clip(u, -1.0 + EPS, 1.0 - EPS))

        def mobius_add(x, y, c):
            x2 = _sqnorm(x)
            y2 = _sqnorm(y)
            xy = jnp.sum(x * y, axis=-1, keepdims=True)
            num = (1.0 + 2.0 * c * xy + c * y2) * x + (1.0 - c * x2) * y
            den = 1.0 + 2.0 * c * xy + c * c * x2 * y2
            return num / jnp.maximum(den, MIN_NORM)

        def logmap0(p, c):
            sc = jnp.sqrt(c)
            pn = _norm(p)
            return p / pn / sc * _atanh(sc * pn)

        def logmap(p1, p2, c):
            sub = mobius_add(-p1, p2, c)
            sn = _norm(sub)
            lam = 2.0 / jnp.maximum(1.0 - c * _sqnorm(p1), MIN_NORM)
            sc = jnp.sqrt(c)
            return 2.0 / sc / lam * _atanh(sc * sn) * sub / sn

        def expmap(p, u, c):
            un = _norm(u)
            lam = 2.0 / jnp.maximum(1.0 - c * _sqnorm(p), MIN_NORM)
            sc = jnp.sqrt(c)
            second = jnp.tanh(sc * lam * un / 2.0) * u / (sc * un)
            return mobius_add(p, second, c)
        B, N, D = x.shape
        x_t = logmap0(x, C)
        left = x_t @ att_w[:D]
        right = x_t @ att_w[D:]
        att = jax.nn.sigmoid(left[:, :, None] + right[:, None, :] + att_b) * adj
        x_local = logmap(x[:, :, None, :], x[:, None, :, :], C)
        support_t = jnp.einsum('bij,bijd->bid', att, x_local)
        return expmap(x, support_t, C)

    def _L2_gnn_ref(node_features, adjacency, W1, b1, g1, be1, W2, b2, g2, be2):
        import jax, jax.numpy as jnp
        import numpy as np
        LN_EPS = 1e-05

        def _layernorm(x, gamma, beta):
            mu = jnp.mean(x, axis=-1, keepdims=True)
            var = jnp.mean(jnp.square(x - mu), axis=-1, keepdims=True)
            return (x - mu) * jax.lax.rsqrt(var + LN_EPS) * gamma + beta
        B, N, D = node_features.shape
        m_j = jnp.einsum('bnd,do->bno', node_features, W1[:D])
        m_i = jnp.einsum('bnd,do->bno', node_features, W1[D:])
        pre = m_j[:, None, :, :] + m_i[:, :, None, :] + b1
        msg = jax.nn.gelu(_layernorm(pre, g1, be1), approximate=False)
        agg = jnp.einsum('bijo,bij->bio', msg, adjacency)
        upd_in = jnp.concatenate([node_features, agg], axis=-1)
        updated = _layernorm(upd_in @ W2 + b2, g2, be2)
        return updated

    def _L3_gnn_ref(nodes, adj, ws0, bs0, wd0, bd0, wn0, bn0, wu0, bu0, ws1, bs1, wd1, bd1, wn1, bn1, wu1, bu1, ws2, bs2, wd2, bd2, wn2, bn2, wu2, bu2, ws3, bs3, wd3, bd3, wn3, bn3, wu3, bu3):
        import jax, jax.numpy as jnp
        import numpy as np
        B, N = (2, 4096)
        IN_DIMS = [128, 128, 256, 384]
        REP = 128
        OUT = 128
        NUM_LAYERS = 4
        EPS = 1e-12

        def _l2norm(x, axis):
            n = jnp.sqrt(jnp.sum(x * x, axis=axis, keepdims=True))
            return x / jnp.maximum(n, EPS)

        def _layer(nodes, adj, ws, bs, wd, bd, wn, bn, wu, bu):
            src = nodes @ ws + bs
            src_agg = jnp.einsum('bjv,bij->biv', src, _l2norm(adj, 2))
            dst = nodes @ wd + bd
            dst_agg = jnp.einsum('bjv,bji->biv', dst, _l2norm(adj, 1))
            self_rep = nodes @ wn + bn
            upd = jnp.concatenate([src_agg, self_rep, dst_agg], axis=2)
            return jnp.tanh(upd @ wu + bu)
        params = [(ws0, bs0, wd0, bd0, wn0, bn0, wu0, bu0), (ws1, bs1, wd1, bd1, wn1, bn1, wu1, bu1), (ws2, bs2, wd2, bd2, wn2, bn2, wu2, bu2), (ws3, bs3, wd3, bd3, wn3, bn3, wu3, bu3)]
        fpass = nodes
        stashed = []
        half = NUM_LAYERS // 2
        for i in range(NUM_LAYERS):
            if i < half:
                stashed.append(fpass)
            elif i == half:
                fpass = jnp.concatenate([fpass, stashed[NUM_LAYERS - i - 1]], axis=2)
            else:
                fpass = jnp.concatenate([fpass, stashed[NUM_LAYERS - i], stashed[NUM_LAYERS - i - 1]], axis=2)
            fpass = _layer(fpass, adj, *params[i])
        return fpass

    h = jnp.maximum(_layernorm(x, axis=-1), 0.0)
    x = x + _L0_gnn_ref(h, adj, L0_gnn_W, L0_gnn_b)
    h = jnp.maximum(_layernorm(x, axis=-1), 0.0)
    x = x + _L1_gnn_ref(h, adj, L1_gnn_att_w, L1_gnn_att_b)
    h = jnp.maximum(_layernorm(x, axis=-1), 0.0)
    x = x + _L2_gnn_ref(h, adj, L2_gnn_W1, L2_gnn_b1, L2_gnn_g1, L2_gnn_be1, L2_gnn_W2, L2_gnn_b2, L2_gnn_g2, L2_gnn_be2)
    h = jnp.maximum(_layernorm(x, axis=-1), 0.0)
    x = x + _L3_gnn_ref(h, adj, L3_gnn_ws0, L3_gnn_bs0, L3_gnn_wd0, L3_gnn_bd0, L3_gnn_wn0, L3_gnn_bn0, L3_gnn_wu0, L3_gnn_bu0, L3_gnn_ws1, L3_gnn_bs1, L3_gnn_wd1, L3_gnn_bd1, L3_gnn_wn1, L3_gnn_bn1, L3_gnn_wu1, L3_gnn_bu1, L3_gnn_ws2, L3_gnn_bs2, L3_gnn_wd2, L3_gnn_bd2, L3_gnn_wn2, L3_gnn_bn2, L3_gnn_wu2, L3_gnn_bu2, L3_gnn_ws3, L3_gnn_bs3, L3_gnn_wd3, L3_gnn_bd3, L3_gnn_wn3, L3_gnn_bn3, L3_gnn_wu3, L3_gnn_bu3)
    return x


_drawn_inputs = setup_inputs


def setup_inputs(seed=0):
    import zlib

    import numpy as np

    out = dict(_drawn_inputs(seed))
    spreads = {'L2_gnn_g1': (1.0, 0.2),
     'L2_gnn_be1': (0.0, 0.28),
     'L2_gnn_g2': (1.0, 0.2),
     'L2_gnn_be2': (0.0, 0.377)}
    factors = {'L1_gnn_att_w': 200.0,
     'L2_gnn_b1': 3.024,
     'L2_gnn_b2': 29.007,
     'L3_gnn_bs0': 8.0,
     'L3_gnn_bd0': 8.0,
     'L3_gnn_wn0': 4.773,
     'L3_gnn_bn0': 21.651,
     'L3_gnn_bu0': 8.0,
     'L3_gnn_ws1': 8.0,
     'L3_gnn_bs1': 8.0,
     'L3_gnn_wd1': 8.0,
     'L3_gnn_bd1': 23.294,
     'L3_gnn_wn1': 8.0,
     'L3_gnn_bn1': 47.798,
     'L3_gnn_wu1': 4.406,
     'L3_gnn_bu1': 200.0,
     'L3_gnn_ws2': 4.899,
     'L3_gnn_bs2': 37.742,
     'L3_gnn_wd2': 3.599,
     'L3_gnn_bd2': 34.504,
     'L3_gnn_wn2': 8.0,
     'L3_gnn_bn2': 64.0,
     'L3_gnn_wu2': 3.223,
     'L3_gnn_bu2': 64.0,
     'L3_gnn_bs3': 8.0,
     'L3_gnn_bd3': 8.0,
     'L3_gnn_wn3': 3.111,
     'L3_gnn_bn3': 37.574,
     'L3_gnn_bu3': 8.0}
    for name, (base, spread) in spreads.items():
        noise = np.random.default_rng([zlib.crc32(name.encode()), seed]).standard_normal(out[name].shape)
        drawn = base * np.exp(spread * noise) if base else spread * noise
        out[name] = jnp.asarray(drawn.astype(out[name].dtype))
    for name, factor in factors.items():
        out[name] = (out[name] * factor).astype(out[name].dtype)
    return out
```

```python
from contextlib import ExitStack

import concourse.bass as bass
from concourse import mybir

P = 128
ALU = mybir.AluOpType
ACT = mybir.ActivationFunctionType
AX = mybir.AxisListType
F32 = mybir.dt.float32
BF16 = mybir.dt.bfloat16
I32 = mybir.dt.int32
U32 = mybir.dt.uint32

B, N, D = 64, 256, 128
NB = N // P
GB = 4
GROUPS = B // GB
LN_EPS = 1e-5
L3_IN = (1, 1, 2, 3)
L3_ORDER = ((0,), (1,), (2, 1), (3, 1, 0))


class Scope:

    def __init__(self, nc, stack, prefix):
        self.nc, self.stack, self.prefix = nc, stack, prefix

    def sb(self, name, shape, dtype=F32):
        return self.stack.enter_context(self.nc.sbuf_tensor(self.prefix + name, shape, dtype))

    def psum(self, name, shape, dtype=F32):
        return self.stack.enter_context(self.nc.psum_tensor(self.prefix + name, shape, dtype))

    def sem(self, name):
        return self.stack.enter_context(self.nc.semaphore(self.prefix + name))


def prepare(nc, w, keep):
    with ExitStack() as stack:
        s = Scope(nc, stack, "w_")
        kinds = ("s", "d", "n")
        tiles = [(l, k, t) for l in range(4) for k in range(3) for t in range(L3_IN[l])]
        raw = s.sb("raw", [P, len(tiles), D])
        wu = s.sb("wu", [P, 4, 3, D])
        bcol = s.sb("bcol", [P, 4, 4])
        bwide = s.sb("bwide", [P, 8, P])
        rawT = s.sb("rawT", [P, 2, P])
        loaded, consts, turned, copied, folded, kept, widened, biased, stored = (
            s.sem(n) for n in ("loaded", "consts", "turned", "copied", "folded", "kept", "widened", "biased", "stored"))
        ps_turn = [s.psum(f"ps_turn{i}", [P, 512]) for i in range(2)]
        ps_fold = [s.psum(f"ps_fold{i}", [P, 512]) for i in range(2)]
        ps_bias = [s.psum(f"ps_bias{i}", [P, 512]) for i in range(2)]
        n_loads = 0
        third = {"s": 0, "n": 1, "d": 2}
        block = stack.enter_context(nc.Block())

        def wide(l, kt):
            return sum(L3_IN[:l]) + kt

        @block.sync
        def _(sp):
            n = 0

            def load(dst, src):
                sp.dma_start(dst, src).then_inc(loaded, 16)

            for i, (l, k, t) in enumerate(tiles):
                if t == 0:
                    src = w[f"L3_gnn_w{kinds[k]}{l}"].rearrange("(t p) d -> p t d", p=P)
                    load(raw[:, i:i + L3_IN[l], :], src)
                    n += 1
            for l in range(4):
                load(wu[:, l], w[f"L3_gnn_wu{l}"].rearrange("(t p) d -> p t d", p=P))
                for c, name in enumerate(("bs", "bd", "bn", "bu")):
                    load(bcol[:, l, c:c + 1], w[f"L3_gnn_{name}{l}"].rearrange("(p a) -> p a", a=1))
                n += 5

            for name, dst in keep["broadcast"].items():
                load(dst[:], w[name].partition_broadcast(P))
                n += 1
            load(keep["W0"][:], w["L0_gnn_W"])
            for c in range(2):
                load(keep["att2"][:, c:c + 1], w["L1_gnn_att_w"][c * D:(c + 1) * D].rearrange("(p a) -> p a", a=1))
            load(keep["attb"][:], w["L1_gnn_att_b"].partition_broadcast(P))
            load(keep["W1"][:], w["L2_gnn_W1"].rearrange("(t p) d -> p t d", p=P))
            load(keep["W2"][:], w["L2_gnn_W2"].rearrange("(t p) d -> p t d", p=P))
            n += 6
            for g in range(GROUPS):
                load(keep["x"][:, g * GB:(g + 1) * GB],
                     w["x"][g * GB:(g + 1) * GB].rearrange("b (k p) d -> p b k d", p=P))
                n += 1
            sp.wait_ge(loaded, 16 * n)
            sp.sem_inc(stored, 1)
            sp.sem_inc(keep["ready"], 1)

        ident, ones, neg_half = keep["ident"], keep["ones"], keep["neg_half"]

        @block.gpsimd
        def _(pool):
            nc.gpsimd.memset(ident[:], 0.0).then_inc(consts, 1)
            pool.wait_ge(consts, 1)
            nc.gpsimd.affine_select(out=ident[:], in_=ident[:], compare_op=ALU.not_equal, fill=1.0, base=0,
                                    pattern=[[-1, P]], channel_multiplier=1).then_inc(consts, 1)
            nc.gpsimd.memset(ones[:], 1.0).then_inc(consts, 1)
            nc.gpsimd.memset(neg_half[:], -0.5).then_inc(consts, 1)

        @block.tensor
        def _(pe):
            pe.wait_ge(stored, 1)
            pe.wait_ge(consts, 4)
            for i, (l, k, t) in enumerate(tiles):
                if i >= 2:
                    pe.wait_ge(copied, i - 1)
                nc.tensor.transpose(ps_turn[i % 2][:, 0:P], raw[:, i, :], ident[:]).then_inc(turned, 1)
                pe.wait_ge(copied, i + 1)
                if i >= 2:
                    pe.wait_ge(kept, i - 1)
                nc.tensor.matmul(ps_fold[i % 2][:, 0:P], rawT[:, i % 2, :], wu[:, l, third[kinds[k]], :],
                                 start=True, stop=True).then_inc(folded, 1)
            pe.wait_ge(widened, 8)
            for l in range(4):
                if l >= 2:
                    pe.wait_ge(biased, l - 1)
                bank = ps_bias[l % 2]
                nc.tensor.matmul(bank[:, 0:D], bwide[:, 2 * l, :], wu[:, l, 0, :], start=True, stop=True)
                nc.tensor.matmul(bank[:, D:2 * D], bwide[:, 2 * l + 1, :], wu[:, l, 2, :], start=True, stop=True)
                nc.tensor.matmul(bank[:, 2 * D:2 * D + 1], wu[:, l, 1, :], bcol[:, l, 2:3],
                                 start=True, stop=True).then_inc(folded, 1)

        @block.scalar
        def _(act):
            for i in range(len(tiles)):
                act.wait_ge(turned, i + 1)
                if i >= 2:
                    act.wait_ge(folded, i - 1)
                nc.scalar.activation(rawT[:, i % 2, :], ps_turn[i % 2][:, 0:P], ACT.Copy).then_inc(copied, 1)

        @block.vector
        def _(dve):
            dve.wait_ge(stored, 1)
            dve.wait_ge(consts, 4)
            for l in range(4):
                for c in range(2):
                    nc.vector.tensor_scalar(bwide[:, 2 * l + c, :], ones[:], bcol[:, l, c:c + 1], None,
                                            ALU.mult).then_inc(widened, 1)
            for i, (l, k, t) in enumerate(tiles):
                dve.wait_ge(folded, i + 1)
                kt = wide(l, t)
                dst = keep["l3_wn"][:, kt, :] if kinds[k] == "n" else keep["l3_wsd"][:, kt, (k == 1) * D:(k == 1) * D + D]
                nc.vector.tensor_copy(dst, ps_fold[i % 2][:, 0:P]).then_inc(kept, 1)
            for l in range(4):
                dve.wait_ge(folded, len(tiles) + l + 1)
                nc.vector.tensor_copy(keep["l3_bsd"][:, l, :], ps_bias[l % 2][:, 0:2 * D])
                nc.vector.tensor_tensor(keep["l3_c"][:, l:l + 1], ps_bias[l % 2][:, 2 * D:2 * D + 1], bcol[:, l, 3:4],
                                        ALU.add).then_inc(biased, 1)





MIN_NORM = 1e-15
MAX_TANH = 1.0 - 1e-7
L0_EPS = 1e-6


def layers01(nc, w, keep):
    with ExitStack() as stack:
        s = Scope(nc, stack, "l01_")
        x, ident, bc = keep["x"], keep["ident"], keep["broadcast"]
        units = GB * NB
        adj = s.sb("adj", [P, units, N])
        adjT = s.sb("adjT", [P, GB, NB, N])
        junk = s.sb("junk", [P, 2, N], BF16)
        degree = s.sb("degree", [P, units])
        degree_eps = s.sb("degree_eps", [P, units])
        norm = s.sb("norm", [P, units])
        stats = s.sb("stats", [P, units, 6])
        mv = s.sb("mv", [P, units, 2])
        var = s.sb("var", [P, units])
        rstd = s.sb("rstd", [P, units])
        normed = s.sb("normed", [P, units, D])
        hn = s.sb("hn", [P, units, D])
        sumT = s.sb("sumT", [P, GB, N])
        z0 = s.sb("z0", [P, units, D])
        z0_low = s.sb("z0_low", [P, units, D])
        h = s.sb("h", [P, units, D + 1])
        hT = s.sb("hT", [P, GB, N])
        hT_m2 = s.sb("hT_m2", [P, GB, N])
        cols = s.sb("cols", [P, units, 16])
        rows = s.sb("rows", [4, GB, 4, N])
        pair = s.sb("pair", [P, GB, 2, NB * N])
        diff = s.sb("diff", [P, GB, NB * N])
        total = s.sb("total", [P, GB, NB * N])
        gate = s.sb("gate", [P, GB, NB * N])
        tangent = s.sb("tangent", [P, units, D])
        half = s.sb("half", [P, units])
        small = {n: s.sb("s_" + n, [P, units]) for n in (
            "p", "pc", "pn", "rpn", "u", "ln_a", "ln_b", "at", "scale", "one_p", "lam", "dot", "alpha", "kb", "ka",
            "norm2", "norm2c", "norm1", "rlam", "targ", "th", "rnorm", "f", "f2", "y2", "hu", "hu2", "xy2", "num",
            "py2", "den", "denc", "rden", "ch", "cu0", "cu", "b1")}
        names = ("consts", "degree_ready", "eps_ready", "norm_ready", "var_ready", "rstd_ready", "hn_ready", "adj_turned", "adjT_kept",
                 "sum_made", "sum_kept", "out_made", "z0_low_ready", "exp_ready", "x_ready", "var1_ready", "rstd1_ready",
                 "h_ready", "h_turned", "hT_kept", "hT_m2_kept", "lr_made", "pc_ready", "pn_ready", "rpn_ready", "u_ready",
                 "lns_ready", "cols_ready", "cols_turned", "rows_kept", "pair_made", "gate_made", "pair_clamped", "ln_ready",
                 "diff_ready", "total_ready", "s_ready", "coef_ready", "u_clipped", "artanh_ready", "sigmoid_ready",
                 "gated", "c_ready", "s_made", "norm2_ready", "norm1_ready", "targ_ready", "th_ready", "group_done",
                 "abs_step", "out_used")
        sem = {n: s.sem(n) for n in names}
        adj_in = [s.sem(f"adj_in{b}") for b in range(GB)]
        ps_pair = [s.psum(f"ps_pair{i}", [P, 2, NB * N]) for i in range(2)]
        ps_gate = [s.psum(f"ps_gate{i}", [P, NB * N]) for i in range(2)]
        ps_work = [s.psum(f"ps_work{i}", [P, NB * N]) for i in range(2)]
        ps_s = ps_work + ps_gate
        block = stack.enter_context(nc.Block())

        def of(b):
            return slice(b * NB, (b + 1) * NB)

        @block.sync
        def _(sp):
            with sp.Fori(0, GROUPS) as g:
                done = sp.snap(g * GB)
                for b in range(GB):
                    sp.dma_start(adj[:, of(b)], w["adj"][bass.ds(done + b, 1)].rearrange(
                        "b (k p) j -> p (b k) j", p=P)).then_inc(adj_in[b], 16)
                sp.wait_ge(sem["degree_ready"], g + 1)
                sp.sem_inc(keep["held"], 1)
                sp.wait_ge(sem["adj_turned"], done + GB)
                sp.sem_inc(keep["held"], 1)

        @block.gpsimd
        def _(pool):
            nc.gpsimd.memset(half[:], 0.5)
            nc.gpsimd.memset(cols[:], 0.0)
            pool.drain()
            for c in (1, 3, 4, 9, 14):
                nc.gpsimd.memset(cols[:, :, c:c + 1], 1.0)
            pool.drain().then_inc(sem["consts"], 1)
            minus_half = keep["neg_half"][:, 0:units]
            with pool.Fori(0, GROUPS) as g:
                done = pool.snap(g * GB)
                pool.wait_ge(sem["var_ready"], g + 1)
                nc.gpsimd.tensor_tensor(rstd[:], var[:], minus_half, ALU.pow).then_inc(sem["rstd_ready"], 1)
                pool.wait_ge(sem["eps_ready"], g + 1)
                nc.gpsimd.tensor_tensor(norm[:], degree_eps[:], minus_half, ALU.pow).then_inc(sem["norm_ready"], 1)
                pool.wait_ge(sem["var1_ready"], g + 1)
                nc.gpsimd.tensor_tensor(rstd[:], var[:], minus_half, ALU.pow).then_inc(sem["rstd1_ready"], 1)
                pool.wait_ge(sem["pc_ready"], g + 1)
                nc.gpsimd.tensor_tensor(small["pn"][:], small["pc"][:], half[:], ALU.pow).then_inc(sem["pn_ready"], 1)
                nc.gpsimd.tensor_tensor(small["rpn"][:], small["pc"][:], minus_half, ALU.pow).then_inc(sem["rpn_ready"], 1)
                for b in range(GB):
                    pool.wait_ge(sem["ln_ready"], done + (b + 1))
                    nc.gpsimd.tensor_tensor(total[:, b], pair[:, b, 0], pair[:, b, 1], ALU.add).then_inc(sem["total_ready"], 1)
                for b in range(GB):
                    pool.wait_ge(sem["sigmoid_ready"], done + (b + 1))
                    nc.gpsimd.tensor_tensor(gate[:, b], gate[:, b], adjT[:, b].rearrange("p k n -> p (k n)"),
                                            ALU.mult).then_inc(sem["gated"], 1)
                pool.wait_ge(sem["norm2_ready"], g + 1)
                nc.gpsimd.tensor_tensor(small["norm1"][:], small["norm2c"][:], half[:], ALU.pow).then_inc(sem["norm1_ready"], 1)

        @block.scalar
        def _(act):
            with act.Fori(0, GROUPS) as g:
                done = act.snap(g * GB)
                for b in range(GB):
                    act.wait_ge(adj_in[b], g * 16 + 16)
                    for k in range(NB):
                        u = b * NB + k
                        if u >= 2:
                            act.wait_ge(sem["abs_step"], g * units + (u - 1))
                        nc.scalar.activation(junk[:, u % 2], adj[:, u], ACT.Abs,
                                             accum_out=degree[:, u:u + 1]).then_inc(sem["abs_step"], 1)
                act.wait_ge(sem["abs_step"], g * units + units)
                act.sem_inc(sem["degree_ready"], 1)
                for b in range(GB):
                    act.wait_ge(sem["adj_turned"], done + (b + 1))
                    nc.scalar.activation(adjT[:, b].rearrange("p k n -> p (k n)"), ps_pair[b // 2][:, b % 2], ACT.Copy)\
                        .then_inc(sem["adjT_kept"], 1)
                for b in range(GB):
                    act.wait_ge(sem["sum_made"], done + (b + 1))
                    nc.scalar.activation(sumT[:, b], ps_work[b % 2][:, 0:N], ACT.Copy).then_inc(sem["sum_kept"], 1)
                for b in range(GB):
                    act.wait_ge(sem["z0_low_ready"], done + (b + 1))
                    nc.scalar.activation(z0_low[:, of(b)], z0_low[:, of(b)], ACT.Exp).then_inc(sem["exp_ready"], 1)
                for b in range(GB):
                    act.wait_ge(sem["h_turned"], done + (b + 1))
                    nc.scalar.activation(hT[:, b], ps_work[b % 2][:, 0:N], ACT.Copy).then_inc(sem["hT_kept"], 1)
                act.wait_ge(sem["u_ready"], g + 1)
                nc.scalar.activation(small["ln_a"][:], small["u"][:], ACT.Ln, bias=1.0)
                nc.scalar.activation(small["ln_b"][:], small["u"][:], ACT.Ln, bias=1.0, scale=-1.0).then_inc(sem["lns_ready"], 1)
                for b in range(GB):
                    act.wait_ge(sem["cols_turned"], done + (b + 1))
                    nc.scalar.activation(rows[:, b], ps_pair[b % 2][0:4].rearrange("p a (c n) -> p (a c) n", c=2),
                                         ACT.Copy).then_inc(sem["rows_kept"], 1)
                for b in range(GB):
                    act.wait_ge(sem["pair_clamped"], done + (b + 1))
                    nc.scalar.activation(pair[:, b], pair[:, b], ACT.Ln).then_inc(sem["ln_ready"], 1)
                for b in range(GB):
                    act.wait_ge(sem["diff_ready"], done + (b + 1))
                    nc.scalar.activation(diff[:, b], diff[:, b], ACT.Exp, scale=0.5).then_inc(sem["s_ready"], 1)
                    act.wait_ge(sem["total_ready"], done + (b + 1))
                    nc.scalar.activation(total[:, b], total[:, b], ACT.Exp, scale=-0.5).then_inc(sem["coef_ready"], 1)
                for b in range(GB):
                    act.wait_ge(sem["u_clipped"], done + (b + 1))
                    act.wait_ge(sem["total_ready"], done + (b + 1))
                    nc.scalar.activation(pair[:, b, 0], diff[:, b], ACT.Ln, bias=1.0)
                    nc.scalar.activation(pair[:, b, 1], diff[:, b], ACT.Ln, bias=1.0, scale=-1.0)\
                        .then_inc(sem["artanh_ready"], 1)
                for b in range(GB):
                    act.wait_ge(sem["gate_made"], done + (b + 1))
                    nc.scalar.activation(gate[:, b], ps_s[b][:], ACT.Sigmoid).then_inc(sem["sigmoid_ready"], 1)
                act.wait_ge(sem["targ_ready"], g + 1)
                nc.scalar.activation(small["th"][:], small["targ"][:], ACT.Tanh).then_inc(sem["th_ready"], 1)

        @block.tensor
        def _(pe):
            pe.wait_ge(sem["consts"], 1)
            with pe.Fori(0, GROUPS) as g:
                done = pe.snap(g * GB)
                for b in range(GB):
                    pe.wait_ge(adj_in[b], g * 16 + 16)
                    for ki in range(NB):
                        for kj in range(NB):
                            ins = nc.tensor.transpose(ps_pair[b // 2][:, b % 2, kj * N + ki * P:kj * N + (ki + 1) * P],
                                                      adj[:, b * NB + ki, kj * P:(kj + 1) * P], ident[:])
                    ins.then_inc(sem["adj_turned"], 1)
                for b in range(GB):
                    pe.wait_ge(sem["adjT_kept"], done + (b + 1))
                    pe.wait_ge(sem["hn_ready"], done + (b + 1))
                    if b >= 2:
                        pe.wait_ge(sem["sum_kept"], done + (b - 1))
                    for k in range(NB):
                        ins = nc.tensor.matmul(ps_work[b % 2][:, 0:N], hn[:, b * NB + k], adjT[:, b, k],
                                               start=k == 0, stop=k == NB - 1)
                    ins.then_inc(sem["sum_made"], 1)
                for b in range(GB):
                    pe.wait_ge(sem["sum_kept"], done + (b + 1))
                    for k in range(NB):
                        ins = nc.tensor.matmul(ps_pair[b // 2][:, b % 2, k * P:(k + 1) * P],
                                               sumT[:, b, k * P:(k + 1) * P], keep["W0"][:], start=True, stop=True)
                    ins.then_inc(sem["out_made"], 1)
                pe.wait_ge(sem["sum_kept"], done + GB)
                for b in range(GB):
                    pe.wait_ge(sem["h_ready"], done + (b + 1))
                    if b >= 2:
                        pe.wait_ge(sem["hT_kept"], done + (b - 1))
                    for k in range(NB):
                        ins = nc.tensor.transpose(ps_work[b % 2][:, k * P:(k + 1) * P], h[:, b * NB + k, 0:D], ident[:])
                    ins.then_inc(sem["h_turned"], 1)
                for b in range(GB):
                    pe.wait_ge(sem["hT_kept"], done + (b + 1))
                    for k in range(NB):
                        u = b * NB + k
                        ins = nc.tensor.matmul(ps_gate[0][:, 2 * u:2 * u + 2], hT[:, b, k * P:(k + 1) * P],
                                               keep["att2"][:], start=True, stop=True)
                ins.then_inc(sem["lr_made"], 1)
                pe.wait_ge(sem["cols_ready"], g + 1)
                pe.wait_ge(sem["hT_m2_kept"], done + GB)

                def turn_cols(b):
                    for q in range(4):
                        for k in range(NB):
                            ins = nc.tensor.transpose(ps_pair[b % 2][0:4, q // 2, (q % 2) * N + k * P:(q % 2) * N + (k + 1) * P],
                                                      cols[:, b * NB + k, 4 * q:4 * q + 4], ident[:])
                    ins.then_inc(sem["cols_turned"], 1)

                turn_cols(0)
                turn_cols(1)
                for b in range(GB):
                    pe.wait_ge(sem["rows_kept"], done + (b + 1))
                    for kj in range(NB):
                        left = rows[:, b, 0, kj * P:(kj + 1) * P]
                        for q in range(2):
                            out = ps_pair[b % 2][:, q, kj * N:(kj + 1) * N]
                            nc.tensor.matmul(out, hT_m2[:, b, kj * P:(kj + 1) * P], hT[:, b], start=True, stop=False)
                            ins = nc.tensor.matmul(out, left, rows[:, b, 1 + q], start=False, stop=True)
                    ins.then_inc(sem["pair_made"], 1)
                    for kj in range(NB):
                        ins = nc.tensor.matmul(ps_s[b][:, kj * N:(kj + 1) * N], rows[:, b, 0, kj * P:(kj + 1) * P],
                                               rows[:, b, 3], start=True, stop=True)
                    ins.then_inc(sem["gate_made"], 1)
                    if b + 2 < GB:
                        pe.wait_ge(sem["pair_clamped"], done + (b + 1))
                        turn_cols(b + 2)
                pe.wait_ge(sem["sigmoid_ready"], done + GB)
                for b in range(GB):
                    pe.wait_ge(sem["c_ready"], done + (b + 1))
                    for ki in range(NB):
                        for kj in range(NB):
                            ins = nc.tensor.matmul(ps_s[b][:, ki * (D + 1):(ki + 1) * (D + 1)],
                                                   pair[:, b, 0, kj * N + ki * P:kj * N + (ki + 1) * P],
                                                   h[:, b * NB + kj], start=kj == 0, stop=kj == NB - 1)
                    ins.then_inc(sem["s_made"], 1)
                pe.wait_ge(sem["group_done"], g + 1)
                pe.sem_inc(keep["held"], 1)

        @block.vector
        def _(dve):
            v = nc.vector
            dve.wait_ge(sem["consts"], 1)
            sm = {n: t[:] for n, t in small.items()}

            def layernorm_sums(xg, then):
                for u in range(units):
                    v.bn_stats(stats[:, u], xg[:, u])
                dve.drain()
                for u in range(units):
                    v.bn_aggr(mv[:, u], stats[:, u])
                dve.drain()
                v.tensor_scalar(var[:], mv[:, :, 1], LN_EPS, None, ALU.add).then_inc(then, 1)

            with dve.Fori(0, GROUPS) as g:
                done = dve.snap(g * GB)
                xg = x[:, bass.ds(done, GB)].rearrange("p b k d -> p (b k) d")
                layernorm_sums(xg, sem["var_ready"])
                dve.wait_ge(sem["degree_ready"], g + 1)
                v.tensor_scalar(degree_eps[:], degree[:], L0_EPS, None, ALU.add).then_inc(sem["eps_ready"], 1)
                dve.wait_ge(sem["rstd_ready"], g + 1)
                for u in range(units):
                    v.tensor_scalar(normed[:, u], xg[:, u], mv[:, u, 0:1], rstd[:, u:u + 1], ALU.subtract, ALU.mult)
                dve.drain()
                dve.wait_ge(sem["norm_ready"], g + 1)
                for b in range(GB):
                    for u in range(b * NB, (b + 1) * NB):
                        ins = v.tensor_scalar(hn[:, u], normed[:, u], 0.0, norm[:, u:u + 1], ALU.max, ALU.mult)
                    ins.then_inc(sem["hn_ready"], 1)
                for b in range(GB):
                    dve.wait_ge(sem["out_made"], done + (b + 1))
                    for k in range(NB):
                        u = b * NB + k
                        v.scalar_tensor_tensor(z0[:, u], ps_pair[b // 2][:, b % 2, k * P:(k + 1) * P],
                                               norm[:, u:u + 1], bc["L0_gnn_b"][:], ALU.mult, ALU.add)
                dve.drain()
                for b in range(GB):
                    v.tensor_scalar(z0_low[:, of(b)], z0[:, of(b)], 0.0, None, ALU.min).then_inc(sem["z0_low_ready"], 1)
                v.scalar_tensor_tensor(normed[:], z0[:], 0.0, xg, ALU.max, ALU.add)
                dve.drain()
                for b in range(GB):
                    dve.wait_ge(sem["exp_ready"], done + (b + 1))
                    v.scalar_tensor_tensor(xg[:, of(b)], z0_low[:, of(b)], -1.0, normed[:, of(b)], ALU.add, ALU.add)\
                        .then_inc(sem["x_ready"], 1)
                dve.wait_ge(sem["x_ready"], done + GB)
                dve.sem_inc(keep["held"], 1)

                layernorm_sums(xg, sem["var1_ready"])
                dve.wait_ge(sem["rstd1_ready"], g + 1)
                for u in range(units):
                    v.tensor_scalar(normed[:, u], xg[:, u], mv[:, u, 0:1], rstd[:, u:u + 1], ALU.subtract, ALU.mult)
                dve.drain()
                for b in range(GB):
                    v.tensor_scalar(h[:, of(b), 0:D], normed[:, of(b)], 0.0, None, ALU.max).then_inc(sem["h_ready"], 1)
                for u in range(units):
                    v.scalar_tensor_tensor(hn[:, u], normed[:, u], 0.0, normed[:, u], ALU.max, ALU.mult,
                                           accum_out=small["p"][:, u:u + 1])
                dve.drain()
                v.tensor_scalar(sm["pc"], sm["p"], MIN_NORM, None, ALU.max).then_inc(sem["pc_ready"], 1)
                v.tensor_scalar(h[:, :, D], sm["p"], 1.0, None, ALU.add)
                v.tensor_scalar(sm["b1"], sm["p"], -1.0, 1.0, ALU.mult, ALU.add)
                for c in (0, 5, 8):
                    v.tensor_copy(cols[:, :, c], sm["p"])
                dve.drain()
                v.tensor_scalar(sm["lam"], sm["b1"], MIN_NORM, None, ALU.max)
                for b in range(GB):
                    dve.wait_ge(sem["hT_kept"], done + (b + 1))
                    v.tensor_scalar(hT_m2[:, b], hT[:, b], -2.0, None, ALU.mult).then_inc(sem["hT_m2_kept"], 1)
                dve.wait_ge(sem["pn_ready"], g + 1)
                v.tensor_scalar(sm["u"], sm["pn"], MAX_TANH, None, ALU.min).then_inc(sem["u_ready"], 1)
                dve.wait_ge(sem["lns_ready"], g + 1)
                v.tensor_tensor(sm["at"], sm["ln_a"], sm["ln_b"], ALU.subtract)
                dve.drain()
                dve.wait_ge(sem["rpn_ready"], g + 1)
                v.scalar_tensor_tensor(sm["scale"], sm["at"], 0.5, sm["rpn"], ALU.mult, ALU.mult)
                dve.drain()
                dve.wait_ge(sem["lr_made"], g + 1)
                lr = ps_gate[0][:, 0:2 * units].rearrange("p (u c) -> p u c", c=2)
                v.tensor_tensor(cols[:, :, 15], lr[:, :, 0], sm["scale"], ALU.mult)
                v.tensor_tensor(sm["at"], lr[:, :, 1], sm["scale"], ALU.mult)
                dve.drain()
                v.tensor_scalar(cols[:, :, 2], sm["at"], keep["attb"][:, 0:1], None, ALU.add)
                dve.drain().then_inc(sem["cols_ready"], 1)
                for b in range(GB):
                    dve.wait_ge(sem["pair_made"], done + (b + 1))
                    v.tensor_scalar(pair[:, b], ps_pair[b % 2][:], MIN_NORM, None, ALU.max).then_inc(sem["pair_clamped"], 1)
                for b in range(GB):
                    dve.wait_ge(sem["ln_ready"], done + (b + 1))
                    v.tensor_tensor(diff[:, b], pair[:, b, 0], pair[:, b, 1], ALU.subtract).then_inc(sem["diff_ready"], 1)
                for b in range(GB):
                    dve.wait_ge(sem["s_ready"], done + (b + 1))
                    v.tensor_scalar(diff[:, b], diff[:, b], MAX_TANH, None, ALU.min).then_inc(sem["u_clipped"], 1)
                for b in range(GB):
                    dve.wait_ge(sem["artanh_ready"], done + (b + 1))
                    v.tensor_tensor(pair[:, b, 0], pair[:, b, 0], pair[:, b, 1], ALU.subtract)
                dve.drain()
                for b in range(GB):
                    dve.wait_ge(sem["coef_ready"], done + (b + 1))
                    v.scalar_tensor_tensor(total[:, b], pair[:, b, 0], 0.5, total[:, b], ALU.mult, ALU.mult)
                dve.drain()
                for b in range(GB):
                    dve.wait_ge(sem["gated"], done + (b + 1))
                    v.tensor_tensor(pair[:, b, 0], total[:, b], gate[:, b], ALU.mult).then_inc(sem["c_ready"], 1)
                for b in range(GB):
                    dve.wait_ge(sem["s_made"], done + (b + 1))
                    for k in range(NB):
                        u = b * NB + k
                        v.scalar_tensor_tensor(hn[:, u], ps_s[b][:, k * (D + 1):k * (D + 1) + D], 1.0, h[:, u, 0:D],
                                               ALU.mult, ALU.mult, accum_out=small["dot"][:, u:u + 1])
                dve.drain()
                for b in range(GB):
                    v.scalar_tensor_tensor(small["alpha"][:, of(b)], small["dot"][:, of(b)], -2.0,
                                           ps_s[b][:, 0:NB * (D + 1)].rearrange("p (k d) -> p k d", k=NB)[:, :, D],
                                           ALU.mult, ALU.add)
                v.tensor_tensor(sm["kb"], sm["lam"], sm["b1"], ALU.mult)
                v.reciprocal(sm["rlam"], sm["lam"])
                dve.drain()
                v.tensor_tensor(sm["ka"], sm["lam"], sm["alpha"], ALU.mult)
                v.tensor_tensor(sm["hu"], sm["kb"], sm["dot"], ALU.mult)
                dve.drain()
                for u in range(units):
                    v.tensor_scalar(hn[:, u], h[:, u, 0:D], small["ka"][:, u:u + 1], None, ALU.mult)
                v.tensor_tensor(sm["hu2"], sm["ka"], sm["p"], ALU.mult)
                dve.drain()
                for u in range(units):
                    b, k = divmod(u, NB)
                    v.scalar_tensor_tensor(tangent[:, u], ps_s[b][:, k * (D + 1):k * (D + 1) + D], small["kb"][:, u:u + 1],
                                           hn[:, u], ALU.mult, ALU.subtract)
                dve.drain()
                for u in range(units):
                    v.scalar_tensor_tensor(hn[:, u], tangent[:, u], 1.0, tangent[:, u], ALU.mult, ALU.mult,
                                           accum_out=small["norm2"][:, u:u + 1])
                v.tensor_tensor(sm["hu"], sm["hu"], sm["hu2"], ALU.subtract)
                dve.drain()
                v.tensor_scalar(sm["norm2c"], sm["norm2"], MIN_NORM, None, ALU.max).then_inc(sem["norm2_ready"], 1)
                dve.wait_ge(sem["norm1_ready"], g + 1)
                v.tensor_tensor(sm["targ"], sm["norm1"], sm["rlam"], ALU.mult).then_inc(sem["targ_ready"], 1)
                v.reciprocal(sm["rnorm"], sm["norm1"])
                dve.drain()
                dve.wait_ge(sem["th_ready"], g + 1)
                v.tensor_tensor(sm["f"], sm["th"], sm["rnorm"], ALU.mult)
                dve.drain()
                v.tensor_tensor(sm["f2"], sm["f"], sm["f"], ALU.mult)
                v.scalar_tensor_tensor(sm["xy2"], sm["f"], 2.0, sm["hu"], ALU.mult, ALU.mult)
                v.tensor_tensor(sm["cu0"], sm["f"], sm["b1"], ALU.mult)
                dve.drain()
                v.tensor_tensor(sm["y2"], sm["f2"], sm["norm2"], ALU.mult)
                dve.drain()
                v.scalar_tensor_tensor(sm["num"], sm["xy2"], 1.0, sm["y2"], ALU.add, ALU.add)
                v.tensor_tensor(sm["py2"], sm["p"], sm["y2"], ALU.mult)
                dve.drain()
                v.scalar_tensor_tensor(sm["den"], sm["xy2"], 1.0, sm["py2"], ALU.add, ALU.add)
                dve.drain()
                v.tensor_scalar(sm["denc"], sm["den"], MIN_NORM, None, ALU.max)
                dve.drain()
                v.reciprocal(sm["rden"], sm["denc"])
                dve.drain()
                v.tensor_tensor(sm["ch"], sm["num"], sm["rden"], ALU.mult)
                v.tensor_tensor(sm["cu"], sm["cu0"], sm["rden"], ALU.mult)
                dve.drain()
                for u in range(units):
                    v.tensor_scalar(hn[:, u], h[:, u, 0:D], small["ch"][:, u:u + 1], None, ALU.mult)
                dve.drain()
                for u in range(units):
                    v.scalar_tensor_tensor(tangent[:, u], tangent[:, u], small["cu"][:, u:u + 1], hn[:, u], ALU.mult, ALU.add)
                dve.drain()
                v.tensor_tensor(xg, xg, tangent[:], ALU.add).then_inc(sem["group_done"], 1)
                dve.wait_ge(sem["group_done"], g + 1)
                dve.sem_inc(keep["held"], 1)


SLOTS = N + 8
CHUNKS = -(-SLOTS // P)
UNITS = GB * NB
HALF = UNITS // 2
LOWEST = -3.4028235e38


def layer2(nc, w, keep):
    with ExitStack() as stack:
        s = Scope(nc, stack, "l2_")
        x, ident, neg_half, bc = keep["x"], keep["ident"], keep["neg_half"], keep["broadcast"]
        adj = s.sb("adj", [P, UNITS, N])
        signs = s.sb("signs", [P, 2, N], BF16)
        sign_sums = s.sb("sign_sums", [P, 2, UNITS])
        negatives = s.sb("negatives", [P, UNITS])
        needed = s.sb("needed", [P, UNITS])
        needed_p = s.sb("needed_p", [P, 1])
        needed_1 = s.sb("needed_1", [1, 1])
        n_slots = s.sb("n_slots", [1, 1], I32)
        top = s.sb("top", [P, UNITS, 8])
        top_at = s.sb("top_at", [P, UNITS, 8], U32)
        value = s.sb("value", [P, UNITS, SLOTS])
        index = s.sb("index", [P, UNITS, CHUNKS * P])
        indexT = s.sb("indexT", [P, CHUNKS, UNITS * P], BF16)
        ident16 = s.sb("ident16", [P, P], BF16)
        zero16 = s.sb("zero16", [P, 4 * P], BF16)
        node_of = s.sb("node_of", [P, NB])
        W1c = s.sb("W1c", [P, 2, D])
        b1c = s.sb("b1c", [P, D])
        w1_sum = s.sb("w1_sum", [P, 3])
        w1_mean = s.sb("w1_mean", [P, 3])
        stats = s.sb("stats", [P, UNITS, 6])
        mv = s.sb("mv", [P, UNITS, 2])
        var = s.sb("var", [P, UNITS])
        rstd = s.sb("rstd", [P, UNITS])
        normed = s.sb("normed", [P, UNITS, D])
        h = s.sb("h", [P, UNITS, D])
        hT = s.sb("hT", [P, GB, N])
        m = s.sb("m", [P, UNITS, 2, D])
        parts = s.sb("parts", [P, UNITS, 3, 2 * D], BF16)
        spread = s.sb("spread", [P, UNITS * P], BF16)
        onehot = s.sb("onehot", [P, 2, NB, UNITS * P], BF16)
        pstats = s.sb("pstats", [P, UNITS, 6])
        dmean = s.sb("dmean", [P, UNITS])
        dmean2 = s.sb("dmean2", [P, UNITS])
        msum = s.sb("msum", [P, UNITS])
        pvar = s.sb("pvar", [P, UNITS])
        prstd = s.sb("prstd", [P, UNITS])
        z = [s.sb(f"z{i}", [P, UNITS, D]) for i in range(2)]
        msg = [s.sb(f"msg{i}", [P, UNITS, D]) for i in range(2)]
        diag = [s.sb(f"diag{i}", [P, UNITS, D]) for i in range(2)]
        aggT = s.sb("aggT", [P, GB, N])
        upd, scaled = m[:].rearrange("p u t d -> p (u t) d")[:, 0:UNITS], z[0]
        names = ("consts", "w1_ready", "signed", "needed_ready", "needed_turned", "slots_ready", "stats_ready",
                 "var_ready", "rstd_ready", "h_ready", "h_turned", "h_kept", "m_made", "m_ready", "hi_ready",
                 "rest1_ready", "mid_ready", "rest2_ready", "parts_ready", "index_ready", "index_turned", "index_kept",
                 "spread_made", "spread_kept", "onehot_ready", "gathered", "stats_done", "pvar_ready", "prstd_ready",
                 "diag_ready", "z_made", "z_ready", "msg_ready", "summed", "agg_done", "agg_kept", "upd_made",
                 "upd_var_ready", "upd_rstd_ready", "upd_normed", "upd_scaled", "upd_shifted", "x_done", "dve_step",
                 "slots_free")
        sem = {n: s.sem(n) for n in names}
        adj_in = [s.sem(f"adj_in{b}") for b in range(GB)]
        ps_spread = s.psum("ps_spread", [P, UNITS * P])
        ps_m = [s.psum(f"ps_m{i}", [P, UNITS, D]) for i in range(2)]
        ps_agg = s.psum("ps_agg", [P, GB, N])
        block = stack.enter_context(nc.Block())

        def wide(t):
            return t[:].rearrange("p (a d) -> p a d", a=1).broadcast_to((P, UNITS, D))

        @block.sync
        def _(sp):
            with sp.Fori(0, GROUPS) as g:
                done = sp.snap(g * GB)
                for b in range(GB):
                    sp.dma_start(adj[:, b * NB:(b + 1) * NB], w["adj"][bass.ds(done + b, 1)].rearrange(
                        "b (k p) j -> p (b k) j", p=P)).then_inc(adj_in[b], 16)
                sp.wait_ge(sem["index_ready"], g + 1)
                sp.sem_inc(keep["held"], 1)

        @block.gpsimd
        def _(pool):
            nc.gpsimd.memset(ident16[:], 0.0)
            nc.gpsimd.memset(zero16[:], 0.0)
            nc.gpsimd.memset(index[:], 0.0)
            nc.gpsimd.iota(node_of[:], [[P, NB]], base=0, channel_multiplier=1, allow_small_or_imprecise_dtypes=True)
            for i in range(2):
                nc.gpsimd.memset(msg[i][:], 0.0)
            pool.drain()
            nc.gpsimd.affine_select(out=ident16[:], in_=ident16[:], compare_op=ALU.not_equal, fill=1.0, base=0,
                                    pattern=[[-1, P]], channel_multiplier=1).then_inc(sem["consts"], 1)
            count = pool.alloc_register("l2_before_pool")
            pool.reg_mov(count, 0)
            halves = neg_half[:, 0:UNITS]
            with pool.Fori(0, GROUPS) as g:
                done = pool.snap(g * GB)
                pool.wait_ge(sem["var_ready"], g + 1)
                nc.gpsimd.tensor_tensor(rstd[:], var[:], halves, ALU.pow).then_inc(sem["rstd_ready"], 1)
                for b in range(GB):
                    units = slice(b * NB, (b + 1) * NB)
                    pool.wait_ge(sem["hi_ready"], done + (b + 1))
                    nc.gpsimd.tensor_tensor(m[:, units], m[:, units], parts[:, units, 0].rearrange(
                        "p u (t d) -> p u t d", t=2), ALU.subtract).then_inc(sem["rest1_ready"], 1)
                for b in range(GB):
                    units = slice(b * NB, (b + 1) * NB)
                    pool.wait_ge(sem["mid_ready"], done + (b + 1))
                    pool.wait_ge(sem["rest1_ready"], done + (b + 1))
                    nc.gpsimd.tensor_tensor(m[:, units], m[:, units], parts[:, units, 1].rearrange(
                        "p u (t d) -> p u t d", t=2), ALU.subtract).then_inc(sem["rest2_ready"], 1)
                pool.wait_ge(sem["slots_ready"], g + 1)
                pool.sem_inc(keep["held"], 1)
                n = pool.value_load(n_slots[0:1, 0:1], min_val=1, max_val=N)
                pairs = pool.snap((n + 1) // 2)
                before = pool.snap(count)
                with pool.Fori(0, pairs) as t:
                    for par in range(2):
                        step = pool.snap(before + (t * 2 + par))
                        pool.wait_ge(sem["pvar_ready"], step + 1)
                        nc.gpsimd.tensor_tensor(prstd[:], pvar[:], halves, ALU.pow).then_inc(sem["prstd_ready"], 1)
                        for half in range(2):
                            units = slice(half * HALF, (half + 1) * HALF)
                            pool.wait_ge(sem["z_made"], step * 2 + (half + 3))
                            nc.gpsimd.tensor_tensor(z[par][:, units], z[par][:, units], wide(bc["L2_gnn_be1"])[:, units],
                                                    ALU.add).then_inc(sem["z_ready"], 1)
                pool.reg_add(count, count, pairs * 2)
                pool.wait_ge(sem["upd_var_ready"], g + 1)
                nc.gpsimd.tensor_tensor(rstd[:], var[:], halves, ALU.pow).then_inc(sem["upd_rstd_ready"], 1)
                pool.wait_ge(sem["upd_scaled"], g + 1)
                nc.gpsimd.tensor_tensor(scaled[:], scaled[:], wide(bc["L2_gnn_be2"]), ALU.add).then_inc(sem["upd_shifted"], 1)

        @block.scalar
        def _(act):
            act.sem_inc(sem["msg_ready"], 2)
            count = act.alloc_register("l2_before_act")
            act.reg_mov(count, 0)
            with act.Fori(0, GROUPS) as g:
                done = act.snap(g * GB)
                for b in range(GB):
                    act.wait_ge(adj_in[b], g * 16 + 16)
                    for k in range(NB):
                        u = b * NB + k
                        if u >= 1:
                            act.wait_ge(sem["signed"], (g * UNITS + (u - 1)) * 2 + 2)
                        nc.scalar.activation(signs[:, 0], adj[:, u], ACT.Sign,
                                             accum_out=sign_sums[:, 0, u:u + 1]).then_inc(sem["signed"], 1)
                        act.wait_ge(sem["signed"], (g * UNITS + u) * 2 + 1)
                        nc.scalar.activation(signs[:, 1], signs[:, 0], ACT.Square,
                                             accum_out=sign_sums[:, 1, u:u + 1]).then_inc(sem["signed"], 1)
                act.wait_ge(sem["h_turned"], g + 1)
                nc.scalar.activation(hT[:], ps_spread[:].rearrange("p (b n) -> p b n", b=GB), ACT.Copy).then_inc(sem["h_kept"], 1)
                for b in range(GB):
                    units = slice(b * NB, (b + 1) * NB)
                    act.wait_ge(sem["m_ready"], done + (b + 1))
                    nc.scalar.activation(parts[:, units, 0].rearrange("p u (t d) -> p u t d", t=2), m[:, units],
                                         ACT.Copy).then_inc(sem["hi_ready"], 1)
                for i, (wait, then) in enumerate((("rest1_ready", "mid_ready"), ("rest2_ready", "parts_ready"))):
                    for b in range(GB):
                        units = slice(b * NB, (b + 1) * NB)
                        act.wait_ge(sem[wait], done + (b + 1))
                        nc.scalar.activation(parts[:, units, i + 1].rearrange("p u (t d) -> p u t d", t=2), m[:, units],
                                             ACT.Copy).then_inc(sem[then], 1)
                for c in range(CHUNKS):
                    act.wait_ge(sem["index_turned"], g * CHUNKS + (c + 1))
                    nc.scalar.activation(indexT[:, c], ps_spread[:], ACT.Copy).then_inc(sem["index_kept"], 1)
                act.wait_ge(sem["slots_ready"], g + 1)
                act.sem_inc(keep["held"], 1)
                n = act.value_load(n_slots[0:1, 0:1], min_val=1, max_val=N)
                pairs = act.snap((n + 1) // 2)
                before = act.snap(count)

                def keep_spread(ahead):
                    act.wait_ge(sem["spread_made"], ahead + 1)
                    nc.scalar.activation(spread[:], ps_spread[:], ACT.Copy).then_inc(sem["spread_kept"], 1)

                first_ahead = act.snap(before + g * 2)
                keep_spread(first_ahead)
                act.wait_ge(sem["onehot_ready"], first_ahead + 1)
                keep_spread(first_ahead + 1)
                with act.Fori(0, pairs) as t:
                    for par in range(2):
                        step = act.snap(before + (t * 2 + par))
                        ahead = act.snap(step + g * 2 + 2)
                        act.wait_ge(sem["onehot_ready"], ahead)
                        keep_spread(ahead)
                        for half in range(2):
                            units = slice(half * HALF, (half + 1) * HALF)
                            act.wait_ge(sem["z_ready"], step * 2 + (half + 1))
                            nc.scalar.activation(msg[par][:, units], z[par][:, units], ACT.Gelu).then_inc(sem["msg_ready"], 1)
                act.reg_add(count, count, pairs * 2)
                after = act.snap(count)
                act.wait_ge(sem["onehot_ready"], after + (g * 2 + 2))
                act.wait_ge(sem["agg_done"], g + 1)
                nc.scalar.activation(aggT[:], ps_agg[:], ACT.Copy).then_inc(sem["agg_kept"], 1)

        @block.vector
        def _(dve):
            steps = [0]

            nc.vector.tensor_reduce(w1_sum[:, 0:2], keep["W1"][:], AX.X, ALU.add)
            nc.vector.tensor_reduce(w1_sum[:, 2:3], bc["L2_gnn_b1"][:], AX.X, ALU.add)
            nc.vector.memset(value[:], 0.0)
            dve.drain()
            nc.vector.tensor_scalar(w1_mean[:], w1_sum[:], 1.0 / D, None, ALU.mult)
            dve.drain()
            for t in range(2):
                nc.vector.tensor_scalar(W1c[:, t], keep["W1"][:, t], w1_mean[:, t:t + 1], None, ALU.subtract)
            nc.vector.tensor_scalar(b1c[:], bc["L2_gnn_b1"][:], w1_mean[:, 2:3], None, ALU.subtract)
            dve.drain().then_inc(sem["w1_ready"], 1)
            dve.wait_ge(sem["consts"], 1)
            dve.sem_inc(sem["z_made"], 2)
            count = dve.alloc_register("l2_before_dve")
            dve.reg_mov(count, 0)

            with dve.Fori(0, GROUPS) as g:
                done = dve.snap(g * GB)
                xg = x[:, bass.ds(done, GB)].rearrange("p b k d -> p (b k) d")
                for u in range(UNITS):
                    nc.vector.bn_stats(stats[:, u], xg[:, u])
                dve.drain()
                for u in range(UNITS):
                    nc.vector.bn_aggr(mv[:, u], stats[:, u])
                dve.drain()
                nc.vector.tensor_scalar(var[:], mv[:, :, 1], LN_EPS, None, ALU.add).then_inc(sem["var_ready"], 1)
                dve.wait_ge(sem["signed"], g * (2 * UNITS) + 2 * UNITS)
                nc.vector.tensor_tensor(negatives[:], sign_sums[:, 1], sign_sums[:, 0], ALU.subtract)
                dve.drain()
                nc.vector.scalar_tensor_tensor(needed[:], negatives[:], float(N), sign_sums[:, 0], ALU.mult, ALU.add)
                dve.drain()
                nc.vector.tensor_reduce(needed_p[:], needed[:], AX.X, ALU.max).then_inc(sem["needed_ready"], 1)
                dve.wait_ge(sem["rstd_ready"], g + 1)
                for u in range(UNITS):
                    nc.vector.tensor_scalar(normed[:, u], xg[:, u], mv[:, u, 0:1], rstd[:, u:u + 1], ALU.subtract, ALU.mult)
                dve.drain()
                nc.vector.tensor_scalar(h[:], normed[:], 0.0, None, ALU.max).then_inc(sem["h_ready"], 1)
                dve.wait_ge(sem["needed_turned"], g + 1)
                nc.vector.tensor_reduce(needed_1[:], ps_m[0][0:1, 0, :], AX.X, ALU.max)
                dve.drain()
                nc.vector.tensor_scalar(n_slots[:], needed_1[:], 1.0, float(N), ALU.max, ALU.min)
                dve.drain().then_inc(sem["slots_ready"], 1)
                for b in range(GB):
                    dve.wait_ge(sem["m_made"], done + (b + 1))
                    pm = ps_m[b // 2][:, (b % 2) * 4:(b % 2) * 4 + 4].rearrange("p (k t) d -> p k t d", t=2)
                    nc.vector.tensor_copy(m[:, b * NB:(b + 1) * NB, 0], pm[:, :, 0])
                    nc.vector.tensor_tensor(m[:, b * NB:(b + 1) * NB, 1], pm[:, :, 1], b1c[:].rearrange(
                        "p (a d) -> p a d", a=1).broadcast_to((P, NB, D)), ALU.add).then_inc(sem["m_ready"], 1)
                dve.wait_ge(sem["slots_ready"], g + 1)
                dve.sem_inc(keep["held"], 1)
                n = dve.value_load(n_slots[0:1, 0:1], min_val=1, max_val=N)
                pairs = dve.snap((n + 1) // 2)
                before = dve.snap(count)
                with dve.Fori(0, (pairs * 2 + 9) // 8) as r:
                    for u in range(UNITS):
                        nc.vector.max(top[:, u], adj[:, u])
                    dve.drain()
                    for u in range(UNITS):
                        nc.vector.max_index(top_at[:, u], top[:, u], adj[:, u])
                    nc.vector.tensor_copy(value[:, :, bass.ds(r * 8, 8)], top[:])
                    dve.drain()
                    for u in range(UNITS):
                        nc.vector.match_replace(adj[:, u], top[:, u], adj[:, u], LOWEST)
                    nc.vector.tensor_copy(index[:, :, bass.ds(r * 8, 8)], top_at[:])
                    dve.drain()
                dve.drain().then_inc(sem["index_ready"], 1)

                def pick(ahead, par):
                    dve.wait_ge(sem["spread_kept"], ahead + 1)
                    for k in range(NB):
                        ins = nc.vector.tensor_scalar(onehot[:, par, k], spread[:], node_of[:, k:k + 1], None, ALU.is_equal)
                    ins.then_inc(sem["onehot_ready"], 1)

                first_ahead = dve.snap(before + g * 2)
                dve.wait_ge(sem["summed"], before + (g + 1))
                nc.vector.memset(diag[1][:], 0.0).then_inc(sem["diag_ready"], 1)
                pick(first_ahead, 0)
                pick(first_ahead + 1, 1)
                with dve.Fori(0, pairs) as t:
                    for par in range(2):
                        step = dve.snap(before + (t * 2 + par))
                        ahead = dve.snap(step + g * 2 + 2)
                        for half in range(2):
                            dve.wait_ge(sem["gathered"], (step + g) * 2 + (half + 1))
                            for u in range(half * HALF, (half + 1) * HALF):
                                ins = nc.vector.bn_stats(pstats[:, u], ps_m[par][:, u])
                        ins.then_inc(sem["stats_done"], 1)
                        dve.wait_ge(sem["stats_done"], step + 1)
                        nc.vector.tensor_tensor(dmean[:], pstats[:, :, 1], pstats[:, :, 4], ALU.subtract)
                        nc.vector.scalar_tensor_tensor(msum[:], pstats[:, :, 2], D * LN_EPS, pstats[:, :, 5],
                                                       ALU.add, ALU.add).then_inc(sem["dve_step"], 1)
                        dve.wait_ge(sem["dve_step"], step * 2 + 1)
                        nc.vector.scalar_tensor_tensor(dmean2[:], dmean[:], 0.25, dmean[:], ALU.mult,
                                                       ALU.mult).then_inc(sem["dve_step"], 1)
                        dve.wait_ge(sem["dve_step"], step * 2 + 2)
                        nc.vector.scalar_tensor_tensor(pvar[:], msum[:], 1.0 / D, dmean2[:], ALU.mult,
                                                       ALU.add).then_inc(sem["pvar_ready"], 1)
                        pick(ahead, par)
                        dve.wait_ge(sem["summed"], step + (g + 1))
                        slot = dve.snap(t * 2 + par)
                        for u in range(UNITS):
                            ins = nc.vector.tensor_scalar(diag[par][:, u], ident[:], value[:, u, bass.ds(slot, 1)], None, ALU.mult)
                        ins.then_inc(sem["diag_ready"], 1)
                        dve.wait_ge(sem["prstd_ready"], step + 1)
                        for half in range(2):
                            for u in range(half * HALF, (half + 1) * HALF):
                                ins = nc.vector.scalar_tensor_tensor(z[par][:, u], ps_m[par][:, u], prstd[:, u:u + 1],
                                                                     bc["L2_gnn_g1"][:], ALU.mult, ALU.mult)
                            ins.then_inc(sem["z_made"], 1)
                dve.reg_add(count, count, pairs * 2)
                dve.wait_ge(sem["upd_made"], g + 1)
                nc.vector.tensor_tensor(upd, ps_spread[:].rearrange("p (u d) -> p u d", u=UNITS), wide(bc["L2_gnn_b2"]), ALU.add)
                dve.drain()
                for u in range(UNITS):
                    nc.vector.bn_stats(stats[:, u], upd[:, u])
                dve.drain()
                for u in range(UNITS):
                    nc.vector.bn_aggr(mv[:, u], stats[:, u])
                dve.drain()
                nc.vector.tensor_scalar(var[:], mv[:, :, 1], LN_EPS, None, ALU.add).then_inc(sem["upd_var_ready"], 1)
                dve.wait_ge(sem["upd_rstd_ready"], g + 1)
                for u in range(UNITS):
                    nc.vector.tensor_scalar(normed[:, u], upd[:, u], mv[:, u, 0:1], rstd[:, u:u + 1], ALU.subtract, ALU.mult)
                dve.drain()
                nc.vector.tensor_tensor(scaled[:], normed[:], wide(bc["L2_gnn_g2"]), ALU.mult).then_inc(sem["upd_scaled"], 1)
                dve.wait_ge(sem["upd_shifted"], g + 1)
                nc.vector.tensor_tensor(xg, xg, scaled[:], ALU.add).then_inc(sem["x_done"], 1)
                dve.wait_ge(sem["x_done"], g + 1)
                dve.sem_inc(keep["held"], 1)

        @block.tensor
        def _(pe):
            pe.sem_inc(sem["summed"], 1)
            pe.wait_ge(sem["consts"], 1)
            pe.wait_ge(sem["w1_ready"], 1)
            count = pe.alloc_register("l2_before_pe")
            pe.reg_mov(count, 0)
            with pe.Fori(0, GROUPS) as g:
                pe.wait_ge(sem["needed_ready"], g + 1)
                nc.tensor.transpose(ps_m[0][0:1, 0, :], needed_p[:], ident[:]).then_inc(sem["needed_turned"], 1)
                pe.wait_ge(sem["h_ready"], g + 1)
                for u in range(UNITS):
                    ins = nc.tensor.transpose(ps_spread[:, u * P:(u + 1) * P], h[:, u], ident[:])
                ins.then_inc(sem["h_turned"], 1)
                pe.wait_ge(sem["slots_ready"], g + 1)
                pe.wait_ge(sem["h_kept"], g + 1)
                for b in range(GB):
                    for k in range(NB):
                        lane = (b % 2) * 4 + 2 * k
                        ins = nc.tensor.matmul(ps_m[b // 2][:, lane:lane + 2], hT[:, b, k * P:(k + 1) * P], W1c[:],
                                               start=True, stop=True)
                    ins.then_inc(sem["m_made"], 1)
                for b in range(2):
                    nc.tensor.matmul(ps_agg[:].rearrange("p (c b) n -> p c (b n)", c=2)[:, b], zero16[:, 0:P], zero16[:],
                                     start=True, stop=False, skip_group_check=True)
                pe.wait_ge(sem["index_ready"], g + 1)
                for c in range(CHUNKS):
                    if c:
                        pe.wait_ge(sem["index_kept"], g * CHUNKS + c)
                    for u in range(UNITS):
                        ins = nc.tensor.transpose(ps_spread[:, u * P:(u + 1) * P], index[:, u, c * P:(c + 1) * P], ident[:])
                    ins.then_inc(sem["index_turned"], 1)
                pe.wait_ge(sem["index_kept"], g * CHUNKS + CHUNKS)
                pe.sem_inc(keep["held"], 1)
                n = pe.value_load(n_slots[0:1, 0:1], min_val=1, max_val=N)
                pairs = pe.snap((n + 1) // 2)
                before = pe.snap(count)

                def spread_out(slot):
                    for c in range(2):
                        ins = nc.tensor.matmul(ps_spread[:, c * 512:(c + 1) * 512],
                                               ident16[:, bass.ds(slot % P, 1)].broadcast_to((P, P)),
                                               indexT[:, bass.ds(slot // P, 1), c * 512:(c + 1) * 512].rearrange("p a n -> p (a n)"),
                                               start=True, stop=True)
                    ins.then_inc(sem["spread_made"], 1)

                def gather(par):
                    for half in range(2):
                        for u in range(half * HALF, (half + 1) * HALF):
                            b = u // NB
                            for k in range(NB):
                                for t in range(3):
                                    nc.tensor.matmul(ps_m[par][:, u], onehot[:, par, k, u * P:(u + 1) * P],
                                                     parts[:, b * NB + k, t, 0:D], start=k + t == 0, stop=False)
                            for t in range(3):
                                ins = nc.tensor.matmul(ps_m[par][:, u], ident16[:], parts[:, u, t, D:2 * D],
                                                       start=False, stop=t == 2)
                        ins.then_inc(sem["gathered"], 1)

                def aggregate(par):
                    for u in range(UNITS):
                        ins = nc.tensor.matmul(ps_agg[:, u // NB, (u % NB) * P:(u % NB + 1) * P], msg[par][:, u], diag[par][:, u],
                                               start=False, stop=False, skip_group_check=True)
                    ins.then_inc(sem["summed"], 1)

                first_ahead = pe.snap(before + g * 2)
                spread_out(0)
                pe.wait_ge(sem["spread_kept"], first_ahead + 1)
                spread_out(1)
                pe.wait_ge(sem["parts_ready"], g * GB + GB)
                pe.wait_ge(sem["onehot_ready"], first_ahead + 1)
                gather(0)
                with pe.Fori(0, pairs) as t:
                    for par in range(2):
                        step = pe.snap(before + (t * 2 + par))
                        ahead = pe.snap(step + g * 2 + 2)
                        pe.wait_ge(sem["spread_kept"], ahead)
                        spread_out(pe.snap(t * 2 + (par + 2)))
                        pe.wait_ge(sem["onehot_ready"], ahead)
                        pe.wait_ge(sem["z_made"], step * 2 + 2)
                        gather(1 - par)
                        pe.wait_ge(sem["msg_ready"], step * 2 + 2)
                        pe.wait_ge(sem["diag_ready"], step + (g + 1))
                        aggregate(1 - par)
                pe.reg_add(count, count, pairs * 2)
                after = pe.snap(count)
                pe.wait_ge(sem["msg_ready"], after * 2 + 2)
                pe.wait_ge(sem["diag_ready"], after + (g + 1))
                aggregate(1)
                for b in range(2):
                    ins = nc.tensor.matmul(ps_agg[:].rearrange("p (c b) n -> p c (b n)", c=2)[:, b], zero16[:, 0:P], zero16[:],
                                           start=False, stop=True, skip_group_check=True)
                ins.then_inc(sem["agg_done"], 1)
                pe.wait_ge(sem["agg_kept"], g + 1)
                pe.wait_ge(sem["spread_kept"], after + (g * 2 + 2))
                for u in range(UNITS):
                    b, k = divmod(u, NB)
                    nc.tensor.matmul(ps_spread[:, u * P:(u + 1) * P], hT[:, b, k * P:(k + 1) * P], keep["W2"][:, 0],
                                     start=True, stop=False)
                    ins = nc.tensor.matmul(ps_spread[:, u * P:(u + 1) * P], aggT[:, b, k * P:(k + 1) * P], keep["W2"][:, 1],
                                           start=False, stop=True)
                ins.then_inc(sem["upd_made"], 1)
                pe.wait_ge(sem["x_done"], g + 1)
                pe.sem_inc(keep["held"], 1)


def layer3(nc, w, keep, out):
    with ExitStack() as stack:
        s = Scope(nc, stack, "l3_")
        x, ident, neg_half = keep["x"], keep["ident"], keep["neg_half"]
        adj = s.sb("adj", [P, GB, NB, N])
        adj_row = s.sb("adj_row", [P, GB, NB, N])
        adjT_col = s.sb("adjT_col", [P, GB, NB, N])
        rowT = s.sb("rowT", [P, GB, NB, N])
        colA = s.sb("colA", [P, GB, NB, N])
        junk = s.sb("junk", [P, GB, 2, N])
        sums = s.sb("sums", [P, GB, 2, NB])
        clamped = s.sb("clamped", [P, GB, 2, NB])
        inv = s.sb("inv", [P, GB, 2, NB])
        stats = s.sb("stats", [P, GB, NB, 6])
        mv = s.sb("mv", [P, GB, NB, 2])
        var = s.sb("var", [P, GB, NB])
        rstd = s.sb("rstd", [P, GB, NB])
        normed = s.sb("normed", [P, GB, NB, D])
        h = s.sb("h", [P, GB, NB, D])
        fT = s.sb("fT", [P, GB, 5, N])
        sd = s.sb("sd", [P, GB, NB, 2 * D])
        xout = s.sb("xout", [P, GB, NB, D])
        names = ("summed", "clamped", "inv_ready", "stats_ready", "mv_ready", "var_ready", "rstd_ready",
                 "normed_ready", "h_ready", "adj_turned", "row_scaled", "col_scaled", "row_turned", "row_kept",
                 "col_turned", "col_kept", "h_turned", "h_kept", "sd_made", "sd_kept", "f_made", "f_kept",
                 "f_turned", "x_ready", "col_squared", "row_squared")
        sem = {n: s.sem(n) for n in names}
        adj_in = [s.sem(f"adj_in{b}") for b in range(GB)]
        x_stored = [s.sem(f"x_stored{b}") for b in range(GB)]
        ps_adj = [s.psum(f"ps_adj{i}", [P, NB, N]) for i in range(4)]
        ps_sd = ps_adj[2:]
        ps_turn = [s.psum(f"ps_turn{i}", [P, NB, N]) for i in range(2)]
        ps_f = [s.psum(f"ps_f{i}", [P, 512]) for i in range(2)]
        block = stack.enter_context(nc.Block())

        @block.sync
        def _(sp):
            with sp.Fori(0, GROUPS) as g:
                done = sp.snap(g * GB)
                for b in range(GB):
                    sp.dma_start(adj[:, b], w["adj"][bass.ds(done + b, 1)].rearrange(
                        "b (k p) j -> p (b k) j", p=P)).then_inc(adj_in[b], 16)
                for b in range(GB):
                    sp.wait_ge(sem["x_ready"], done + (b + 1))
                    sp.dma_start(out[bass.ds(done + b, 1)].rearrange("b (k p) d -> p (b k) d", p=P),
                                 xout[:, b]).then_inc(x_stored[b], 16)
                for b in range(GB):
                    sp.wait_ge(x_stored[b], g * 16 + 16)
                sp.sem_inc(keep["held"], 1)

        @block.gpsimd
        def _(pool):
            with pool.Fori(0, GROUPS) as g:
                done = pool.snap(g * GB)
                pool.wait_ge(sem["mv_ready"], (done + GB))
                pool.sem_inc(keep["held"], 1)
                nc.gpsimd.tensor_scalar(var[:], mv[:, :, :, 1], LN_EPS, 1.0, ALU.add, ALU.mult).then_inc(sem["var_ready"], 1)
                pool.wait_ge(sem["var_ready"], g + 1)
                nc.gpsimd.tensor_tensor(rstd[:], var[:], neg_half[:, 0:GB * NB].rearrange("p (b k) -> p b k", b=GB),
                                        ALU.pow).then_inc(sem["rstd_ready"], 1)
                for b in range(GB):
                    pool.wait_ge(sem["clamped"], done + (b + 1))
                    nc.gpsimd.tensor_tensor(inv[:, b], clamped[:, b], neg_half[:, 0:2 * NB].rearrange(
                        "p (a k) -> p a k", a=2), ALU.pow).then_inc(sem["inv_ready"], 1)

        @block.vector
        def _(dve):
            with dve.Fori(0, GROUPS) as g:
                done = dve.snap(g * GB)
                for b in range(GB):
                    for k in range(NB):
                        ins = nc.vector.bn_stats(stats[:, b, k], x[:, bass.ds(done + b, 1), k].rearrange("p a d -> p (a d)"))
                    ins.then_inc(sem["stats_ready"], 1)
                for b in range(GB):
                    dve.wait_ge(sem["stats_ready"], done + (b + 1))
                    dve.sem_inc(keep["held"], 1)
                    for k in range(NB):
                        ins = nc.vector.bn_aggr(mv[:, b, k], stats[:, b, k])
                    ins.then_inc(sem["mv_ready"], 1)
                for b in range(GB):
                    dve.wait_ge(sem["summed"], done + (b + 1))
                    nc.vector.tensor_scalar(clamped[:, b], sums[:, b], 1e-24, None, ALU.max).then_inc(sem["clamped"], 1)
                dve.wait_ge(sem["rstd_ready"], g + 1)
                dve.wait_ge(sem["mv_ready"], done + GB)
                for b in range(GB):
                    for k in range(NB):
                        ins = nc.vector.tensor_scalar(normed[:, b, k], x[:, bass.ds(done + b, 1), k].rearrange("p a d -> p (a d)"), mv[:, b, k, 0:1],
                                                      rstd[:, b, k:k + 1], ALU.subtract, ALU.mult)
                    ins.then_inc(sem["normed_ready"], 1)
                for b in range(GB):
                    dve.wait_ge(sem["normed_ready"], done + (b + 1))
                    nc.vector.tensor_scalar(h[:, b], normed[:, b], 0.0, None, ALU.max).then_inc(sem["h_ready"], 1)
                for b in range(GB):
                    dve.wait_ge(sem["inv_ready"], done + (b + 1))
                    dve.wait_ge(adj_in[b], g * 16 + 16)
                    for k in range(NB):
                        ins = nc.vector.tensor_scalar(adj_row[:, b, k], adj[:, b, k], inv[:, b, 0, k:k + 1], None, ALU.mult)
                    ins.then_inc(sem["row_scaled"], 1)
                    for k in range(NB):
                        ins = nc.vector.tensor_scalar(adjT_col[:, b, k], ps_adj[b][:, k], inv[:, b, 1, k:k + 1],
                                                      None, ALU.mult)
                    ins.then_inc(sem["col_scaled"], 1)
                for l in range(4):
                    for b in range(GB):
                        n = (4 * g + l) * GB + (b + 1)
                        dve.wait_ge(sem["sd_made"], n)
                        nc.vector.tensor_tensor(sd[:, b], ps_sd[b % 2][:],
                                                keep["l3_bsd"][:, l:l + 1, :].broadcast_to((P, NB, 2 * D)),
                                                ALU.add).then_inc(sem["sd_kept"], 1)
                for b in range(GB):
                    dve.wait_ge(sem["f_turned"], done + (b + 1))
                    nc.vector.tensor_tensor(xout[:, b], x[:, bass.ds(done + b, 1)].rearrange("p a k d -> p (a k) d"),
                                            ps_turn[b % 2][:, 0, :].rearrange("p (k d) -> p k d", k=NB),
                                            ALU.add).then_inc(sem["x_ready"], 1)
                for b in range(GB):
                    dve.wait_ge(x_stored[b], g * 16 + 16)

        @block.scalar
        def _(act):
            with act.Fori(0, GROUPS) as g:
                done = act.snap(g * GB)
                for b in range(GB):
                    act.wait_ge(adj_in[b], g * 16 + 16)
                    for k in range(NB):
                        ins = nc.scalar.activation(junk[:, b, 0], adj[:, b, k], ACT.Square, accum_out=sums[:, b, 0, k:k + 1])
                        ins.then_inc(sem["row_squared"], 1)
                        act.wait_ge(sem["row_squared"], (done + b) * NB + (k + 1))
                    act.wait_ge(sem["adj_turned"], done + (b + 1))
                    for k in range(NB):
                        ins = nc.scalar.activation(junk[:, b, 1], ps_adj[b][:, k], ACT.Square,
                                                   accum_out=sums[:, b, 1, k:k + 1])
                        if k < NB - 1:
                            ins.then_inc(sem["col_squared"], 1)
                            act.wait_ge(sem["col_squared"], (done + (b + 1)))
                    ins.then_inc(sem["summed"], 1)
                for b in range(GB):
                    act.wait_ge(sem["h_turned"], done + (b + 1))
                    nc.scalar.activation(fT[:, b, 0], ps_f[b % 2][:, 0:N], ACT.Copy).then_inc(sem["h_kept"], 1)
                for b in range(GB):
                    act.wait_ge(sem["row_turned"], done + (b + 1))
                    nc.scalar.activation(rowT[:, b], ps_turn[b % 2][:], ACT.Copy).then_inc(sem["row_kept"], 1)
                for b in range(GB):
                    act.wait_ge(sem["col_turned"], done + (b + 1))
                    nc.scalar.activation(colA[:, b], ps_turn[b % 2][:], ACT.Copy).then_inc(sem["col_kept"], 1)
                for l in range(4):
                    for b in range(GB):
                        n = (4 * g + l) * GB + (b + 1)
                        act.wait_ge(sem["f_made"], n)
                        nc.scalar.activation(fT[:, b, l + 1], ps_f[b % 2][:, 0:N], ACT.Tanh,
                                             bias=keep["l3_c"][:, l:l + 1]).then_inc(sem["f_kept"], 1)

        @block.tensor
        def _(pe):
            def turn(dst, src, last_sem):
                for kr in range(NB):
                    for kc in range(NB):
                        ins = nc.tensor.transpose(dst[:, kc, kr * P:(kr + 1) * P], src[:, kr, kc * P:(kc + 1) * P], ident[:])
                ins.then_inc(last_sem, 1)

            with pe.Fori(0, GROUPS) as g:
                done = pe.snap(g * GB)
                for b in range(GB):
                    pe.wait_ge(adj_in[b], g * 16 + 16)
                    turn(ps_adj[b], adj[:, b], sem["adj_turned"])
                for b in range(GB):
                    pe.wait_ge(sem["h_ready"], done + (b + 1))
                    if b >= 2:
                        pe.wait_ge(sem["h_kept"], done + (b - 1))
                    for k in range(NB):
                        ins = nc.tensor.transpose(ps_f[b % 2][:, k * P:(k + 1) * P], h[:, b, k], ident[:])
                    ins.then_inc(sem["h_turned"], 1)
                for b in range(GB):
                    pe.wait_ge(sem["row_scaled"], done + (b + 1))
                    if b >= 2:
                        pe.wait_ge(sem["row_kept"], done + (b - 1))
                    turn(ps_turn[b % 2], adj_row[:, b], sem["row_turned"])
                for b in range(GB):
                    pe.wait_ge(sem["col_scaled"], done + (b + 1))
                    pe.wait_ge(sem["row_kept"], done + (b + 3 if b < 2 else GB))
                    if b >= 2:
                        pe.wait_ge(sem["col_kept"], done + (b - 1))
                    turn(ps_turn[b % 2], adjT_col[:, b], sem["col_turned"])
                pe.wait_ge(sem["col_kept"], done + GB)
                for l in range(4):
                    for b in range(GB):
                        if l == 0:
                            pe.wait_ge(sem["h_kept"], done + (b + 1))
                        else:
                            pe.wait_ge(sem["f_kept"], (4 * g + (l - 1)) * GB + (b + 1))
                        if l or b >= 2:
                            pe.wait_ge(sem["sd_kept"], (4 * g + l) * GB + (b - 1))
                        for k in range(NB):
                            for t, f in enumerate(L3_ORDER[l]):
                                ins = nc.tensor.matmul(ps_sd[b % 2][:, k], fT[:, b, f, k * P:(k + 1) * P],
                                                       keep["l3_wsd"][:, sum(L3_IN[:l]) + t, :],
                                                       start=t == 0, stop=t == L3_IN[l] - 1)
                        ins.then_inc(sem["sd_made"], 1)
                    for b in range(GB):
                        n = (4 * g + l) * GB + (b + 1)
                        pe.wait_ge(sem["sd_kept"], n)
                        if l == 0:
                            pe.wait_ge(sem["h_kept"], done + GB)
                        if l or b >= 2:
                            pe.wait_ge(sem["f_kept"], (4 * g + l) * GB + (b - 1))
                        acc = ps_f[b % 2][:, 0:N]
                        for t, f in enumerate(L3_ORDER[l]):
                            nc.tensor.matmul(acc, keep["l3_wn"][:, sum(L3_IN[:l]) + t, :], fT[:, b, f],
                                             start=t == 0, stop=False)
                        for k in range(NB):
                            nc.tensor.matmul(acc, sd[:, b, k, 0:D], rowT[:, b, k], start=False, stop=False)
                            ins = nc.tensor.matmul(acc, sd[:, b, k, D:2 * D], colA[:, b, k], start=False, stop=k == NB - 1)
                        ins.then_inc(sem["f_made"], 1)
                for b in range(GB):
                    pe.wait_ge(sem["f_kept"], (4 * g + 3) * GB + (b + 1))
                    if b >= 2:
                        pe.wait_ge(sem["x_ready"], done + (b - 1))
                    for k in range(NB):
                        ins = nc.tensor.transpose(ps_turn[b % 2][:, 0, k * P:(k + 1) * P], fT[:, b, 4, k * P:(k + 1) * P], ident[:])
                    ins.then_inc(sem["f_turned"], 1)
                pe.wait_ge(sem["x_ready"], done + GB)


def build(nc, w, out, layers=(0, 2, 3)):
    with ExitStack() as stack:
        s = Scope(nc, stack, "all_")
        bc = {n: s.sb("bc_" + n, [P, D]) for n in ("L0_gnn_b", "L2_gnn_b1", "L2_gnn_g1", "L2_gnn_be1", "L2_gnn_b2",
                                                    "L2_gnn_g2", "L2_gnn_be2")}
        keep = {
            "x": s.sb("x", [P, B, NB, D]),
            "ident": s.sb("ident", [P, P]), "ones": s.sb("ones", [P, P]), "neg_half": s.sb("neg_half", [P, 16]),
            "broadcast": bc,
            "ready": s.sem("ready"),
            "held": s.sem("held"),
            "W0": s.sb("W0", [P, D]), "att2": s.sb("att2", [P, 2]), "attb": s.sb("attb", [P, 1]),
            "W1": s.sb("W1", [P, 2, D]), "W2": s.sb("W2", [P, 2, D]),
            "l3_wsd": s.sb("l3_wsd", [P, sum(L3_IN), 2 * D]), "l3_wn": s.sb("l3_wn", [P, sum(L3_IN), D]),
            "l3_bsd": s.sb("l3_bsd", [P, 4, 2 * D]), "l3_c": s.sb("l3_c", [P, 4]),
        }
        prepare(nc, w, keep)
        if 0 in layers:
            layers01(nc, w, keep)
        if 2 in layers:
            layer2(nc, w, keep)
        if 3 in layers:
            layer3(nc, w, keep, out)
        else:
            with ExitStack() as st:
                o = st.enter_context(nc.semaphore("o"))
                block = st.enter_context(nc.Block())

                @block.sync
                def _(sp):
                    for g in range(GROUPS):
                        sp.dma_start(out[g * GB:(g + 1) * GB].rearrange("b (k p) d -> p b k d", p=P), keep["x"][:, g * GB:(g + 1) * GB]).then_inc(o, 16)
                    sp.wait_ge(o, 16 * GROUPS)


INPUTS = (["x", "adj", "L0_gnn_W", "L0_gnn_b", "L1_gnn_att_w", "L1_gnn_att_b"]
          + [f"L2_gnn_{n}" for n in ("W1", "b1", "g1", "be1", "W2", "b2", "g2", "be2")]
          + [f"L3_gnn_{n}{l}" for l in range(4) for n in ("ws", "bs", "wd", "bd", "wn", "bn", "wu", "bu")])


def kernel(**inputs):
    import numpy as np
    import concourse.bacc as bacc
    from concourse.bass_utils import run_bass_kernel_spmd

    nc = bacc.Bacc("TRN2", target_bir_lowering=False, num_devices=1)
    arrays, w = {}, {}
    for name in INPUTS:
        a = np.ascontiguousarray(inputs[name])
        if a.ndim == 0:
            a = a.reshape(1)
        arrays["in_" + name] = a
        w[name] = nc.dram_tensor("in_" + name, a.shape, mybir.dt.from_np(a.dtype), kind="ExternalInput").ap()
    out = nc.dram_tensor("out_x", (B, N, D), F32, kind="ExternalOutput").ap()
    build(nc, w, out)
    return run_bass_kernel_spmd(nc, [arrays], core_ids=[0]).results[0]["out_x"]
```

```python
from contextlib import ExitStack

import concourse.bass as bass
from concourse import mybir

P = 128
ALU = mybir.AluOpType
ACT = mybir.ActivationFunctionType
AX = mybir.AxisListType
F32 = mybir.dt.float32
BF16 = mybir.dt.bfloat16
I32 = mybir.dt.int32
U32 = mybir.dt.uint32

B, N, D = 64, 256, 128
NB = N // P
GB = 4
GROUPS = B // GB
LN_EPS = 1e-5
L3_IN = (1, 1, 2, 3)
L3_ORDER = ((0,), (1,), (2, 1), (3, 1, 0))


class Scope:

    def __init__(self, nc, stack, prefix):
        self.nc, self.stack, self.prefix = nc, stack, prefix

    def sb(self, name, shape, dtype=F32):
        return self.stack.enter_context(self.nc.sbuf_tensor(self.prefix + name, shape, dtype))

    def psum(self, name, shape, dtype=F32):
        return self.stack.enter_context(self.nc.psum_tensor(self.prefix + name, shape, dtype))

    def sem(self, name):
        return self.stack.enter_context(self.nc.semaphore(self.prefix + name))


def prepare(nc, w, keep):
    with ExitStack() as stack:
        s = Scope(nc, stack, "w_")
        kinds = ("s", "d", "n")
        tiles = [(l, k, t) for l in range(4) for k in range(3) for t in range(L3_IN[l])]
        raw = s.sb("raw", [P, len(tiles), D])
        wu = s.sb("wu", [P, 4, 3, D])
        bcol = s.sb("bcol", [P, 4, 4])
        bwide = s.sb("bwide", [P, 8, P])
        rawT = s.sb("rawT", [P, 2, P])
        loaded, consts, turned, copied, folded, kept, widened, biased, stored = (
            s.sem(n) for n in ("loaded", "consts", "turned", "copied", "folded", "kept", "widened", "biased", "stored"))
        ps_turn = [s.psum(f"ps_turn{i}", [P, 512]) for i in range(2)]
        ps_fold = [s.psum(f"ps_fold{i}", [P, 512]) for i in range(2)]
        ps_bias = [s.psum(f"ps_bias{i}", [P, 512]) for i in range(2)]
        n_loads = 0
        third = {"s": 0, "n": 1, "d": 2}
        block = stack.enter_context(nc.Block())

        def wide(l, kt):
            return sum(L3_IN[:l]) + kt

        @block.sync
        def _(sp):
            n = 0

            def load(dst, src):
                sp.dma_start(dst, src).then_inc(loaded, 16)

            for i, (l, k, t) in enumerate(tiles):
                if t == 0:
                    src = w[f"L3_gnn_w{kinds[k]}{l}"].rearrange("(t p) d -> p t d", p=P)
                    load(raw[:, i:i + L3_IN[l], :], src)
                    n += 1
            for l in range(4):
                load(wu[:, l], w[f"L3_gnn_wu{l}"].rearrange("(t p) d -> p t d", p=P))
                for c, name in enumerate(("bs", "bd", "bn", "bu")):
                    load(bcol[:, l, c:c + 1], w[f"L3_gnn_{name}{l}"].rearrange("(p a) -> p a", a=1))
                n += 5

            for name, dst in keep["broadcast"].items():
                load(dst[:], w[name].partition_broadcast(P))
                n += 1
            load(keep["W0"][:], w["L0_gnn_W"])
            for c in range(2):
                load(keep["att2"][:, c:c + 1], w["L1_gnn_att_w"][c * D:(c + 1) * D].rearrange("(p a) -> p a", a=1))
            load(keep["attb"][:], w["L1_gnn_att_b"].partition_broadcast(P))
            load(keep["W1"][:], w["L2_gnn_W1"].rearrange("(t p) d -> p t d", p=P))
            load(keep["W2"][:], w["L2_gnn_W2"].rearrange("(t p) d -> p t d", p=P))
            n += 6
            for g in range(GROUPS):
                load(keep["x"][:, g * GB:(g + 1) * GB],
                     w["x"][g * GB:(g + 1) * GB].rearrange("b (k p) d -> p b k d", p=P))
                n += 1
            sp.wait_ge(loaded, 16 * n)
            sp.sem_inc(stored, 1)
            sp.sem_inc(keep["ready"], 1)

        ident, ones, neg_half = keep["ident"], keep["ones"], keep["neg_half"]

        @block.gpsimd
        def _(pool):
            nc.gpsimd.memset(ident[:], 0.0).then_inc(consts, 1)
            pool.wait_ge(consts, 1)
            nc.gpsimd.affine_select(out=ident[:], in_=ident[:], compare_op=ALU.not_equal, fill=1.0, base=0,
                                    pattern=[[-1, P]], channel_multiplier=1).then_inc(consts, 1)
            nc.gpsimd.memset(ones[:], 1.0).then_inc(consts, 1)
            nc.gpsimd.memset(neg_half[:], -0.5).then_inc(consts, 1)

        @block.tensor
        def _(pe):
            pe.wait_ge(stored, 1)
            pe.wait_ge(consts, 4)
            for i, (l, k, t) in enumerate(tiles):
                if i >= 2:
                    pe.wait_ge(copied, i - 1)
                nc.tensor.transpose(ps_turn[i % 2][:, 0:P], raw[:, i, :], ident[:]).then_inc(turned, 1)
                pe.wait_ge(copied, i + 1)
                if i >= 2:
                    pe.wait_ge(kept, i - 1)
                nc.tensor.matmul(ps_fold[i % 2][:, 0:P], rawT[:, i % 2, :], wu[:, l, third[kinds[k]], :],
                                 start=True, stop=True).then_inc(folded, 1)
            pe.wait_ge(widened, 8)
            for l in range(4):
                if l >= 2:
                    pe.wait_ge(biased, l - 1)
                bank = ps_bias[l % 2]
                nc.tensor.matmul(bank[:, 0:D], bwide[:, 2 * l, :], wu[:, l, 0, :], start=True, stop=True)
                nc.tensor.matmul(bank[:, D:2 * D], bwide[:, 2 * l + 1, :], wu[:, l, 2, :], start=True, stop=True)
                nc.tensor.matmul(bank[:, 2 * D:2 * D + 1], wu[:, l, 1, :], bcol[:, l, 2:3],
                                 start=True, stop=True).then_inc(folded, 1)

        @block.scalar
        def _(act):
            for i in range(len(tiles)):
                act.wait_ge(turned, i + 1)
                if i >= 2:
                    act.wait_ge(folded, i - 1)
                nc.scalar.activation(rawT[:, i % 2, :], ps_turn[i % 2][:, 0:P], ACT.Copy).then_inc(copied, 1)

        @block.vector
        def _(dve):
            dve.wait_ge(stored, 1)
            dve.wait_ge(consts, 4)
            for l in range(4):
                for c in range(2):
                    nc.vector.tensor_scalar(bwide[:, 2 * l + c, :], ones[:], bcol[:, l, c:c + 1], None,
                                            ALU.mult).then_inc(widened, 1)
            for i, (l, k, t) in enumerate(tiles):
                dve.wait_ge(folded, i + 1)
                kt = wide(l, t)
                dst = keep["l3_wn"][:, kt, :] if kinds[k] == "n" else keep["l3_wsd"][:, kt, (k == 1) * D:(k == 1) * D + D]
                nc.vector.tensor_copy(dst, ps_fold[i % 2][:, 0:P]).then_inc(kept, 1)
            for l in range(4):
                dve.wait_ge(folded, len(tiles) + l + 1)
                nc.vector.tensor_copy(keep["l3_bsd"][:, l, :], ps_bias[l % 2][:, 0:2 * D])
                nc.vector.tensor_tensor(keep["l3_c"][:, l:l + 1], ps_bias[l % 2][:, 2 * D:2 * D + 1], bcol[:, l, 3:4],
                                        ALU.add).then_inc(biased, 1)





MIN_NORM = 1e-15
MAX_TANH = 1.0 - 1e-7
L0_EPS = 1e-6


def layers01(nc, w, keep):
    with ExitStack() as stack:
        s = Scope(nc, stack, "l01_")
        x, ident, bc = keep["x"], keep["ident"], keep["broadcast"]
        units = GB * NB
        adj = s.sb("adj", [P, units, N])
        adjT = s.sb("adjT", [P, GB, NB, N])
        junk = s.sb("junk", [P, 2, N], BF16)
        signs = s.sb("signs", [P, 2, N], BF16)
        degree = s.sb("degree", [P, units])
        degree_eps = s.sb("degree_eps", [P, units])
        norm = s.sb("norm", [P, units])
        stats = s.sb("stats", [P, units, 6])
        mv = s.sb("mv", [P, units, 2])
        var = s.sb("var", [P, units])
        rstd = s.sb("rstd", [P, units])
        normed = s.sb("normed", [P, units, D])
        hn = s.sb("hn", [P, units, D])
        sumT = s.sb("sumT", [P, GB, N])
        z0 = s.sb("z0", [P, units, D])
        z0_low = s.sb("z0_low", [P, units, D])
        h = s.sb("h", [P, units, D + 1])
        hT = s.sb("hT", [P, GB, N])
        hT_m2 = s.sb("hT_m2", [P, GB, N])
        cols = s.sb("cols", [P, units, 16])
        rows = s.sb("rows", [4, GB, 4, N])
        pair = s.sb("pair", [P, GB, 2, NB * N])
        diff = s.sb("diff", [P, GB, NB * N])
        total = s.sb("total", [P, GB, NB * N])
        gate = s.sb("gate", [P, GB, NB * N])
        tangent = s.sb("tangent", [P, units, D])
        half = s.sb("half", [P, units])
        small = {n: s.sb("s_" + n, [P, units]) for n in (
            "p", "pc", "pn", "rpn", "u", "ln_a", "ln_b", "at", "scale", "one_p", "lam", "dot", "alpha", "kb", "ka",
            "norm2", "norm2c", "norm1", "rlam", "targ", "th", "rnorm", "f", "f2", "y2", "hu", "hu2", "xy2", "num",
            "py2", "den", "denc", "rden", "ch", "cu0", "cu", "b1")}
        names = ("consts", "degree_ready", "eps_ready", "norm_ready", "var_ready", "rstd_ready", "hn_ready", "adj_turned", "adjT_kept",
                 "sum_made", "sum_kept", "out_made", "z0_low_ready", "exp_ready", "x_ready", "var1_ready", "rstd1_ready",
                 "h_ready", "h_turned", "hT_kept", "hT_m2_kept", "lr_made", "pc_ready", "pn_ready", "rpn_ready", "u_ready",
                 "lns_ready", "cols_ready", "cols_turned", "rows_kept", "pair_made", "gate_made", "pair_clamped", "ln_ready",
                 "diff_ready", "total_ready", "s_ready", "coef_ready", "u_clipped", "artanh_ready", "sigmoid_ready",
                 "gated", "c_ready", "s_made", "norm2_ready", "norm1_ready", "targ_ready", "th_ready", "group_done",
                 "abs_step", "signed")
        sem = {n: s.sem(n) for n in names}
        adj_in = [s.sem(f"adj_in{b}") for b in range(GB)]
        ps_pair = [s.psum(f"ps_pair{i}", [P, 2, NB * N]) for i in range(2)]
        ps_gate = [s.psum(f"ps_gate{i}", [P, NB * N]) for i in range(2)]
        ps_work = [s.psum(f"ps_work{i}", [P, NB * N]) for i in range(2)]
        ps_s = ps_work + ps_gate
        block = stack.enter_context(nc.Block())

        def of(b):
            return slice(b * NB, (b + 1) * NB)

        @block.sync
        def _(sp):
            with sp.Fori(0, GROUPS) as g:
                done = sp.snap(g * GB)
                for b in range(GB):
                    sp.dma_start(adj[:, of(b)], w["adj"][bass.ds(done + b, 1)].rearrange(
                        "b (k p) j -> p (b k) j", p=P)).then_inc(adj_in[b], 16)
                sp.wait_ge(sem["degree_ready"], g + 1)
                sp.sem_inc(keep["held"], 1)
                sp.wait_ge(sem["signed"], g * (2 * units) + 2 * units)
                sp.sem_inc(keep["held"], 1)
                sp.wait_ge(sem["adj_turned"], done + GB)
                sp.sem_inc(keep["held"], 1)

        @block.gpsimd
        def _(pool):
            nc.gpsimd.memset(half[:], 0.5)
            nc.gpsimd.memset(cols[:], 0.0)
            pool.drain()
            for c in (1, 3, 4, 9, 14):
                nc.gpsimd.memset(cols[:, :, c:c + 1], 1.0)
            pool.drain().then_inc(sem["consts"], 1)
            minus_half = keep["neg_half"][:, 0:units]
            with pool.Fori(0, GROUPS) as g:
                done = pool.snap(g * GB)
                pool.wait_ge(sem["var_ready"], g + 1)
                nc.gpsimd.tensor_tensor(rstd[:], var[:], minus_half, ALU.pow).then_inc(sem["rstd_ready"], 1)
                pool.wait_ge(sem["eps_ready"], g + 1)
                nc.gpsimd.tensor_tensor(norm[:], degree_eps[:], minus_half, ALU.pow).then_inc(sem["norm_ready"], 1)
                pool.wait_ge(sem["var1_ready"], g + 1)
                nc.gpsimd.tensor_tensor(rstd[:], var[:], minus_half, ALU.pow).then_inc(sem["rstd1_ready"], 1)
                pool.wait_ge(sem["pc_ready"], g + 1)
                nc.gpsimd.tensor_tensor(small["pn"][:], small["pc"][:], half[:], ALU.pow).then_inc(sem["pn_ready"], 1)
                nc.gpsimd.tensor_tensor(small["rpn"][:], small["pc"][:], minus_half, ALU.pow).then_inc(sem["rpn_ready"], 1)
                for b in range(GB):
                    pool.wait_ge(sem["ln_ready"], done + (b + 1))
                    nc.gpsimd.tensor_tensor(total[:, b], pair[:, b, 0], pair[:, b, 1], ALU.add).then_inc(sem["total_ready"], 1)
                for b in range(GB):
                    pool.wait_ge(sem["sigmoid_ready"], done + (b + 1))
                    nc.gpsimd.tensor_tensor(gate[:, b], gate[:, b], adjT[:, b].rearrange("p k n -> p (k n)"),
                                            ALU.mult).then_inc(sem["gated"], 1)
                pool.wait_ge(sem["norm2_ready"], g + 1)
                nc.gpsimd.tensor_tensor(small["norm1"][:], small["norm2c"][:], half[:], ALU.pow).then_inc(sem["norm1_ready"], 1)

        @block.scalar
        def _(act):
            def count_signs(g, part):
                for u in range(part * units // 2, (part + 1) * units // 2):
                    if u >= 1:
                        act.wait_ge(sem["signed"], (g * units + (u - 1)) * 2 + 2)
                    at = bass.ds(g * units + u, 1)
                    nc.scalar.activation(signs[:, 0], adj[:, u], ACT.Sign,
                                         accum_out=keep["sign_sums"][:, 0, at]).then_inc(sem["signed"], 1)
                    act.wait_ge(sem["signed"], (g * units + u) * 2 + 1)
                    nc.scalar.activation(signs[:, 1], signs[:, 0], ACT.Square,
                                         accum_out=keep["sign_sums"][:, 1, at]).then_inc(sem["signed"], 1)

            with act.Fori(0, GROUPS) as g:
                done = act.snap(g * GB)
                for b in range(GB):
                    act.wait_ge(adj_in[b], g * 16 + 16)
                    for k in range(NB):
                        u = b * NB + k
                        if u >= 2:
                            act.wait_ge(sem["abs_step"], g * units + (u - 1))
                        nc.scalar.activation(junk[:, u % 2], adj[:, u], ACT.Abs,
                                             accum_out=degree[:, u:u + 1]).then_inc(sem["abs_step"], 1)
                act.wait_ge(sem["abs_step"], g * units + units)
                act.sem_inc(sem["degree_ready"], 1)
                for b in range(GB):
                    act.wait_ge(sem["adj_turned"], done + (b + 1))
                    nc.scalar.activation(adjT[:, b].rearrange("p k n -> p (k n)"), ps_pair[b // 2][:, b % 2], ACT.Copy)\
                        .then_inc(sem["adjT_kept"], 1)
                count_signs(g, 0)
                for b in range(GB):
                    act.wait_ge(sem["sum_made"], done + (b + 1))
                    nc.scalar.activation(sumT[:, b], ps_work[b % 2][:, 0:N], ACT.Copy).then_inc(sem["sum_kept"], 1)
                for b in range(GB):
                    act.wait_ge(sem["z0_low_ready"], done + (b + 1))
                    nc.scalar.activation(z0_low[:, of(b)], z0_low[:, of(b)], ACT.Exp).then_inc(sem["exp_ready"], 1)
                for b in range(GB):
                    act.wait_ge(sem["h_turned"], done + (b + 1))
                    nc.scalar.activation(hT[:, b], ps_work[b % 2][:, 0:N], ACT.Copy).then_inc(sem["hT_kept"], 1)
                count_signs(g, 1)
                act.wait_ge(sem["u_ready"], g + 1)
                nc.scalar.activation(small["ln_a"][:], small["u"][:], ACT.Ln, bias=1.0)
                nc.scalar.activation(small["ln_b"][:], small["u"][:], ACT.Ln, bias=1.0, scale=-1.0).then_inc(sem["lns_ready"], 1)
                for b in range(GB):
                    act.wait_ge(sem["cols_turned"], done + (b + 1))
                    nc.scalar.activation(rows[:, b], ps_pair[b % 2][0:4].rearrange("p a (c n) -> p (a c) n", c=2),
                                         ACT.Copy).then_inc(sem["rows_kept"], 1)
                for b in range(GB):
                    act.wait_ge(sem["pair_clamped"], done + (b + 1))
                    nc.scalar.activation(pair[:, b], pair[:, b], ACT.Ln).then_inc(sem["ln_ready"], 1)
                for b in range(GB):
                    act.wait_ge(sem["diff_ready"], done + (b + 1))
                    nc.scalar.activation(diff[:, b], diff[:, b], ACT.Exp, scale=0.5).then_inc(sem["s_ready"], 1)
                    act.wait_ge(sem["total_ready"], done + (b + 1))
                    nc.scalar.activation(total[:, b], total[:, b], ACT.Exp, scale=-0.5).then_inc(sem["coef_ready"], 1)
                for b in range(GB):
                    act.wait_ge(sem["u_clipped"], done + (b + 1))
                    act.wait_ge(sem["total_ready"], done + (b + 1))
                    nc.scalar.activation(pair[:, b, 0], diff[:, b], ACT.Ln, bias=1.0)
                    nc.scalar.activation(pair[:, b, 1], diff[:, b], ACT.Ln, bias=1.0, scale=-1.0)\
                        .then_inc(sem["artanh_ready"], 1)
                for b in range(GB):
                    act.wait_ge(sem["gate_made"], done + (b + 1))
                    nc.scalar.activation(gate[:, b], ps_s[b][:], ACT.Sigmoid).then_inc(sem["sigmoid_ready"], 1)
                act.wait_ge(sem["targ_ready"], g + 1)
                nc.scalar.activation(small["th"][:], small["targ"][:], ACT.Tanh).then_inc(sem["th_ready"], 1)

        @block.tensor
        def _(pe):
            pe.wait_ge(sem["consts"], 1)
            with pe.Fori(0, GROUPS) as g:
                done = pe.snap(g * GB)
                for b in range(GB):
                    pe.wait_ge(adj_in[b], g * 16 + 16)
                    for ki in range(NB):
                        for kj in range(NB):
                            ins = nc.tensor.transpose(ps_pair[b // 2][:, b % 2, kj * N + ki * P:kj * N + (ki + 1) * P],
                                                      adj[:, b * NB + ki, kj * P:(kj + 1) * P], ident[:])
                    ins.then_inc(sem["adj_turned"], 1)
                for b in range(GB):
                    pe.wait_ge(sem["adjT_kept"], done + (b + 1))
                    pe.wait_ge(sem["hn_ready"], done + (b + 1))
                    if b >= 2:
                        pe.wait_ge(sem["sum_kept"], done + (b - 1))
                    for k in range(NB):
                        ins = nc.tensor.matmul(ps_work[b % 2][:, 0:N], hn[:, b * NB + k], adjT[:, b, k],
                                               start=k == 0, stop=k == NB - 1)
                    ins.then_inc(sem["sum_made"], 1)
                for b in range(GB):
                    pe.wait_ge(sem["sum_kept"], done + (b + 1))
                    for k in range(NB):
                        ins = nc.tensor.matmul(ps_pair[b // 2][:, b % 2, k * P:(k + 1) * P],
                                               sumT[:, b, k * P:(k + 1) * P], keep["W0"][:], start=True, stop=True)
                    ins.then_inc(sem["out_made"], 1)
                pe.wait_ge(sem["sum_kept"], done + GB)
                for b in range(GB):
                    pe.wait_ge(sem["h_ready"], done + (b + 1))
                    if b >= 2:
                        pe.wait_ge(sem["hT_kept"], done + (b - 1))
                    for k in range(NB):
                        ins = nc.tensor.transpose(ps_work[b % 2][:, k * P:(k + 1) * P], h[:, b * NB + k, 0:D], ident[:])
                    ins.then_inc(sem["h_turned"], 1)
                for b in range(GB):
                    pe.wait_ge(sem["hT_kept"], done + (b + 1))
                    for k in range(NB):
                        u = b * NB + k
                        ins = nc.tensor.matmul(ps_gate[0][:, 2 * u:2 * u + 2], hT[:, b, k * P:(k + 1) * P],
                                               keep["att2"][:], start=True, stop=True)
                ins.then_inc(sem["lr_made"], 1)
                pe.wait_ge(sem["cols_ready"], g + 1)
                pe.wait_ge(sem["hT_m2_kept"], done + GB)

                def turn_cols(b):
                    for q in range(4):
                        for k in range(NB):
                            ins = nc.tensor.transpose(ps_pair[b % 2][0:4, q // 2, (q % 2) * N + k * P:(q % 2) * N + (k + 1) * P],
                                                      cols[:, b * NB + k, 4 * q:4 * q + 4], ident[:])
                    ins.then_inc(sem["cols_turned"], 1)

                turn_cols(0)
                turn_cols(1)
                for b in range(GB):
                    pe.wait_ge(sem["rows_kept"], done + (b + 1))
                    for kj in range(NB):
                        left = rows[:, b, 0, kj * P:(kj + 1) * P]
                        for q in range(2):
                            out = ps_pair[b % 2][:, q, kj * N:(kj + 1) * N]
                            nc.tensor.matmul(out, hT_m2[:, b, kj * P:(kj + 1) * P], hT[:, b], start=True, stop=False)
                            ins = nc.tensor.matmul(out, left, rows[:, b, 1 + q], start=False, stop=True)
                    ins.then_inc(sem["pair_made"], 1)
                    for kj in range(NB):
                        ins = nc.tensor.matmul(ps_s[b][:, kj * N:(kj + 1) * N], rows[:, b, 0, kj * P:(kj + 1) * P],
                                               rows[:, b, 3], start=True, stop=True)
                    ins.then_inc(sem["gate_made"], 1)
                    if b + 2 < GB:
                        pe.wait_ge(sem["pair_clamped"], done + (b + 1))
                        turn_cols(b + 2)
                pe.wait_ge(sem["sigmoid_ready"], done + GB)
                for b in range(GB):
                    pe.wait_ge(sem["c_ready"], done + (b + 1))
                    for ki in range(NB):
                        for kj in range(NB):
                            ins = nc.tensor.matmul(ps_s[b][:, ki * (D + 1):(ki + 1) * (D + 1)],
                                                   pair[:, b, 0, kj * N + ki * P:kj * N + (ki + 1) * P],
                                                   h[:, b * NB + kj], start=kj == 0, stop=kj == NB - 1)
                    ins.then_inc(sem["s_made"], 1)
                pe.wait_ge(sem["group_done"], g + 1)
                pe.sem_inc(keep["held"], 1)

        @block.vector
        def _(dve):
            v = nc.vector
            dve.wait_ge(sem["consts"], 1)
            sm = {n: t[:] for n, t in small.items()}

            def layernorm_sums(xg, then):
                for u in range(units):
                    v.bn_stats(stats[:, u], xg[:, u])
                dve.drain()
                for u in range(units):
                    v.bn_aggr(mv[:, u], stats[:, u])
                dve.drain()
                v.tensor_scalar(var[:], mv[:, :, 1], LN_EPS, None, ALU.add).then_inc(then, 1)

            with dve.Fori(0, GROUPS) as g:
                done = dve.snap(g * GB)
                xg = x[:, bass.ds(done, GB)].rearrange("p b k d -> p (b k) d")
                layernorm_sums(xg, sem["var_ready"])
                dve.wait_ge(sem["degree_ready"], g + 1)
                v.tensor_scalar(degree_eps[:], degree[:], L0_EPS, None, ALU.add).then_inc(sem["eps_ready"], 1)
                dve.wait_ge(sem["rstd_ready"], g + 1)
                for u in range(units):
                    v.tensor_scalar(normed[:, u], xg[:, u], mv[:, u, 0:1], rstd[:, u:u + 1], ALU.subtract, ALU.mult)
                dve.drain()
                dve.wait_ge(sem["norm_ready"], g + 1)
                for b in range(GB):
                    for u in range(b * NB, (b + 1) * NB):
                        ins = v.tensor_scalar(hn[:, u], normed[:, u], 0.0, norm[:, u:u + 1], ALU.max, ALU.mult)
                    ins.then_inc(sem["hn_ready"], 1)
                for b in range(GB):
                    dve.wait_ge(sem["out_made"], done + (b + 1))
                    for k in range(NB):
                        u = b * NB + k
                        v.scalar_tensor_tensor(z0[:, u], ps_pair[b // 2][:, b % 2, k * P:(k + 1) * P],
                                               norm[:, u:u + 1], bc["L0_gnn_b"][:], ALU.mult, ALU.add)
                dve.drain()
                for b in range(GB):
                    v.tensor_scalar(z0_low[:, of(b)], z0[:, of(b)], 0.0, None, ALU.min).then_inc(sem["z0_low_ready"], 1)
                v.scalar_tensor_tensor(normed[:], z0[:], 0.0, xg, ALU.max, ALU.add)
                dve.drain()
                for b in range(GB):
                    dve.wait_ge(sem["exp_ready"], done + (b + 1))
                    v.scalar_tensor_tensor(xg[:, of(b)], z0_low[:, of(b)], -1.0, normed[:, of(b)], ALU.add, ALU.add)\
                        .then_inc(sem["x_ready"], 1)
                dve.wait_ge(sem["x_ready"], done + GB)
                dve.sem_inc(keep["held"], 1)

                layernorm_sums(xg, sem["var1_ready"])
                dve.wait_ge(sem["rstd1_ready"], g + 1)
                for u in range(units):
                    v.tensor_scalar(normed[:, u], xg[:, u], mv[:, u, 0:1], rstd[:, u:u + 1], ALU.subtract, ALU.mult)
                dve.drain()
                for b in range(GB):
                    v.tensor_scalar(h[:, of(b), 0:D], normed[:, of(b)], 0.0, None, ALU.max).then_inc(sem["h_ready"], 1)
                for u in range(units):
                    v.scalar_tensor_tensor(hn[:, u], normed[:, u], 0.0, normed[:, u], ALU.max, ALU.mult,
                                           accum_out=small["p"][:, u:u + 1])
                dve.drain()
                v.tensor_scalar(sm["pc"], sm["p"], MIN_NORM, None, ALU.max).then_inc(sem["pc_ready"], 1)
                v.tensor_scalar(h[:, :, D], sm["p"], 1.0, None, ALU.add)
                v.tensor_scalar(sm["b1"], sm["p"], -1.0, 1.0, ALU.mult, ALU.add)
                for c in (0, 5, 8):
                    v.tensor_copy(cols[:, :, c], sm["p"])
                dve.drain()
                v.tensor_scalar(sm["lam"], sm["b1"], MIN_NORM, None, ALU.max)
                for b in range(GB):
                    dve.wait_ge(sem["hT_kept"], done + (b + 1))
                    v.tensor_scalar(hT_m2[:, b], hT[:, b], -2.0, None, ALU.mult).then_inc(sem["hT_m2_kept"], 1)
                dve.wait_ge(sem["pn_ready"], g + 1)
                v.tensor_scalar(sm["u"], sm["pn"], MAX_TANH, None, ALU.min).then_inc(sem["u_ready"], 1)
                dve.wait_ge(sem["lns_ready"], g + 1)
                v.tensor_tensor(sm["at"], sm["ln_a"], sm["ln_b"], ALU.subtract)
                dve.drain()
                dve.wait_ge(sem["rpn_ready"], g + 1)
                v.scalar_tensor_tensor(sm["scale"], sm["at"], 0.5, sm["rpn"], ALU.mult, ALU.mult)
                dve.drain()
                dve.wait_ge(sem["lr_made"], g + 1)
                lr = ps_gate[0][:, 0:2 * units].rearrange("p (u c) -> p u c", c=2)
                v.tensor_tensor(cols[:, :, 15], lr[:, :, 0], sm["scale"], ALU.mult)
                v.tensor_tensor(sm["at"], lr[:, :, 1], sm["scale"], ALU.mult)
                dve.drain()
                v.tensor_scalar(cols[:, :, 2], sm["at"], keep["attb"][:, 0:1], None, ALU.add)
                dve.drain().then_inc(sem["cols_ready"], 1)
                for b in range(GB):
                    dve.wait_ge(sem["pair_made"], done + (b + 1))
                    v.tensor_scalar(pair[:, b], ps_pair[b % 2][:], MIN_NORM, None, ALU.max).then_inc(sem["pair_clamped"], 1)
                for b in range(GB):
                    dve.wait_ge(sem["ln_ready"], done + (b + 1))
                    v.tensor_tensor(diff[:, b], pair[:, b, 0], pair[:, b, 1], ALU.subtract).then_inc(sem["diff_ready"], 1)
                for b in range(GB):
                    dve.wait_ge(sem["s_ready"], done + (b + 1))
                    v.tensor_scalar(diff[:, b], diff[:, b], MAX_TANH, None, ALU.min).then_inc(sem["u_clipped"], 1)
                for b in range(GB):
                    dve.wait_ge(sem["artanh_ready"], done + (b + 1))
                    v.tensor_tensor(pair[:, b, 0], pair[:, b, 0], pair[:, b, 1], ALU.subtract)
                dve.drain()
                for b in range(GB):
                    dve.wait_ge(sem["coef_ready"], done + (b + 1))
                    v.scalar_tensor_tensor(total[:, b], pair[:, b, 0], 0.5, total[:, b], ALU.mult, ALU.mult)
                dve.drain()
                for b in range(GB):
                    dve.wait_ge(sem["gated"], done + (b + 1))
                    v.tensor_tensor(pair[:, b, 0], total[:, b], gate[:, b], ALU.mult).then_inc(sem["c_ready"], 1)
                for b in range(GB):
                    dve.wait_ge(sem["s_made"], done + (b + 1))
                    for k in range(NB):
                        u = b * NB + k
                        v.scalar_tensor_tensor(hn[:, u], ps_s[b][:, k * (D + 1):k * (D + 1) + D], 1.0, h[:, u, 0:D],
                                               ALU.mult, ALU.mult, accum_out=small["dot"][:, u:u + 1])
                dve.drain()
                for b in range(GB):
                    v.scalar_tensor_tensor(small["alpha"][:, of(b)], small["dot"][:, of(b)], -2.0,
                                           ps_s[b][:, 0:NB * (D + 1)].rearrange("p (k d) -> p k d", k=NB)[:, :, D],
                                           ALU.mult, ALU.add)
                v.tensor_tensor(sm["kb"], sm["lam"], sm["b1"], ALU.mult)
                v.reciprocal(sm["rlam"], sm["lam"])
                dve.drain()
                v.tensor_tensor(sm["ka"], sm["lam"], sm["alpha"], ALU.mult)
                v.tensor_tensor(sm["hu"], sm["kb"], sm["dot"], ALU.mult)
                dve.drain()
                for u in range(units):
                    v.tensor_scalar(hn[:, u], h[:, u, 0:D], small["ka"][:, u:u + 1], None, ALU.mult)
                v.tensor_tensor(sm["hu2"], sm["ka"], sm["p"], ALU.mult)
                dve.drain()
                for u in range(units):
                    b, k = divmod(u, NB)
                    v.scalar_tensor_tensor(tangent[:, u], ps_s[b][:, k * (D + 1):k * (D + 1) + D], small["kb"][:, u:u + 1],
                                           hn[:, u], ALU.mult, ALU.subtract)
                dve.drain()
                for u in range(units):
                    v.scalar_tensor_tensor(hn[:, u], tangent[:, u], 1.0, tangent[:, u], ALU.mult, ALU.mult,
                                           accum_out=small["norm2"][:, u:u + 1])
                v.tensor_tensor(sm["hu"], sm["hu"], sm["hu2"], ALU.subtract)
                dve.drain()
                v.tensor_scalar(sm["norm2c"], sm["norm2"], MIN_NORM, None, ALU.max).then_inc(sem["norm2_ready"], 1)
                dve.wait_ge(sem["norm1_ready"], g + 1)
                v.tensor_tensor(sm["targ"], sm["norm1"], sm["rlam"], ALU.mult).then_inc(sem["targ_ready"], 1)
                v.reciprocal(sm["rnorm"], sm["norm1"])
                dve.drain()
                dve.wait_ge(sem["th_ready"], g + 1)
                v.tensor_tensor(sm["f"], sm["th"], sm["rnorm"], ALU.mult)
                dve.drain()
                v.tensor_tensor(sm["f2"], sm["f"], sm["f"], ALU.mult)
                v.scalar_tensor_tensor(sm["xy2"], sm["f"], 2.0, sm["hu"], ALU.mult, ALU.mult)
                v.tensor_tensor(sm["cu0"], sm["f"], sm["b1"], ALU.mult)
                dve.drain()
                v.tensor_tensor(sm["y2"], sm["f2"], sm["norm2"], ALU.mult)
                dve.drain()
                v.scalar_tensor_tensor(sm["num"], sm["xy2"], 1.0, sm["y2"], ALU.add, ALU.add)
                v.tensor_tensor(sm["py2"], sm["p"], sm["y2"], ALU.mult)
                dve.drain()
                v.scalar_tensor_tensor(sm["den"], sm["xy2"], 1.0, sm["py2"], ALU.add, ALU.add)
                dve.drain()
                v.tensor_scalar(sm["denc"], sm["den"], MIN_NORM, None, ALU.max)
                dve.drain()
                v.reciprocal(sm["rden"], sm["denc"])
                dve.drain()
                v.tensor_tensor(sm["ch"], sm["num"], sm["rden"], ALU.mult)
                v.tensor_tensor(sm["cu"], sm["cu0"], sm["rden"], ALU.mult)
                dve.drain()
                for u in range(units):
                    v.tensor_scalar(hn[:, u], h[:, u, 0:D], small["ch"][:, u:u + 1], None, ALU.mult)
                dve.drain()
                for u in range(units):
                    v.scalar_tensor_tensor(tangent[:, u], tangent[:, u], small["cu"][:, u:u + 1], hn[:, u], ALU.mult, ALU.add)
                dve.drain()
                v.tensor_tensor(xg, xg, tangent[:], ALU.add).then_inc(sem["group_done"], 1)
                dve.wait_ge(sem["group_done"], g + 1)
                dve.sem_inc(keep["held"], 1)


SLOTS = N + 8
CHUNKS = -(-SLOTS // P)
UNITS = GB * NB
HALF = UNITS // 2
LOWEST = -3.4028235e38


def layer2(nc, w, keep):
    with ExitStack() as stack:
        s = Scope(nc, stack, "l2_")
        x, ident, neg_half, bc = keep["x"], keep["ident"], keep["neg_half"], keep["broadcast"]
        adj = s.sb("adj", [P, UNITS, N])
        negatives = s.sb("negatives", [P, GROUPS * UNITS])
        needed = s.sb("needed", [P, GROUPS * UNITS])
        needed_p = s.sb("needed_p", [P, GROUPS])
        needed_g = s.sb("needed_g", [GROUPS, 1])
        n_slots = s.sb("n_slots", [1, GROUPS], I32)
        top = s.sb("top", [P, UNITS, 8])
        top_at = s.sb("top_at", [P, UNITS, 8], U32)
        value = s.sb("value", [P, UNITS, SLOTS])
        index = s.sb("index", [P, UNITS, CHUNKS * P])
        indexT = s.sb("indexT", [P, CHUNKS, UNITS * P], BF16)
        ident16 = s.sb("ident16", [P, P], BF16)
        zero16 = s.sb("zero16", [P, 4 * P], BF16)
        node_of = s.sb("node_of", [P, NB])
        W1c = s.sb("W1c", [P, 2, D])
        b1c = s.sb("b1c", [P, D])
        w1_sum = s.sb("w1_sum", [P, 3])
        w1_mean = s.sb("w1_mean", [P, 3])
        stats = s.sb("stats", [P, UNITS, 6])
        mv = s.sb("mv", [P, UNITS, 2])
        var = s.sb("var", [P, UNITS])
        rstd = s.sb("rstd", [P, UNITS])
        normed = s.sb("normed", [P, UNITS, D])
        h = s.sb("h", [P, UNITS, D])
        hT = s.sb("hT", [P, GB, N])
        m = s.sb("m", [P, UNITS, D])
        own = s.sb("own", [P, UNITS, D])
        parts = s.sb("parts", [P, UNITS, 3, D], BF16)
        spread = s.sb("spread", [P, UNITS * P], BF16)
        onehot = s.sb("onehot", [P, 2, NB, UNITS * P], BF16)
        pstats = s.sb("pstats", [P, UNITS, 6])
        dmean = s.sb("dmean", [P, UNITS])
        dmean2 = s.sb("dmean2", [P, UNITS])
        msum = s.sb("msum", [P, UNITS])
        pvar = s.sb("pvar", [P, UNITS])
        prstd = s.sb("prstd", [P, UNITS])
        z = [s.sb(f"z{i}", [P, UNITS, D]) for i in range(2)]
        msg = [s.sb(f"msg{i}", [P, UNITS, D]) for i in range(2)]
        diag = [s.sb(f"diag{i}", [P, UNITS, D]) for i in range(2)]
        aggT = s.sb("aggT", [P, GB, N])
        upd, scaled = m[:], z[0]
        names = ("consts", "w1_ready", "needed_ready", "needed_turned", "slots_ready", "stats_ready",
                 "var_ready", "rstd_ready", "h_ready", "h_turned", "h_kept", "m_made", "m_ready", "hi_ready",
                 "rest1_ready", "mid_ready", "rest2_ready", "parts_ready", "index_ready", "index_turned", "index_kept",
                 "spread_made", "spread_kept", "onehot_ready", "gathered", "stats_done", "pvar_ready", "prstd_ready",
                 "diag_ready", "summed", "z_made", "z_ready", "msg_ready", "seeded", "bits_set", "agg_done", "agg_kept", "upd_made",
                 "upd_var_ready", "upd_rstd_ready", "upd_normed", "upd_scaled", "upd_shifted", "x_done", "dve_step",
                 "upd_read")
        sem = {n: s.sem(n) for n in names}
        adj_in = [s.sem(f"adj_in{b}") for b in range(GB)]
        ps_spread = s.psum("ps_spread", [P, UNITS * P])
        ps_m = [s.psum(f"ps_m{i}", [P, UNITS, D]) for i in range(2)]
        ps_agg = s.psum("ps_agg", [P, GB, N])
        block = stack.enter_context(nc.Block())

        def wide(t):
            return t[:].rearrange("p (a d) -> p a d", a=1).broadcast_to((P, UNITS, D))

        @block.sync
        def _(sp):
            with sp.Fori(0, GROUPS) as g:
                done = sp.snap(g * GB)
                for b in range(GB):
                    sp.dma_start(adj[:, b * NB:(b + 1) * NB], w["adj"][bass.ds(done + b, 1)].rearrange(
                        "b (k p) j -> p (b k) j", p=P)).then_inc(adj_in[b], 16)
                sp.wait_ge(sem["index_ready"], g + 1)
                sp.sem_inc(keep["held"], 1)

        @block.gpsimd
        def _(pool):
            nc.gpsimd.memset(ident16[:], 0.0)
            nc.gpsimd.memset(zero16[:], 0.0)
            nc.gpsimd.memset(index[:], 0.0)
            nc.gpsimd.iota(node_of[:], [[P, NB]], base=0, channel_multiplier=1, allow_small_or_imprecise_dtypes=True)
            for i in range(2):
                nc.gpsimd.memset(msg[i][:], 0.0)
            pool.drain()
            nc.gpsimd.affine_select(out=ident16[:], in_=ident16[:], compare_op=ALU.not_equal, fill=1.0, base=0,
                                    pattern=[[-1, P]], channel_multiplier=1).then_inc(sem["consts"], 1)
            count = pool.alloc_register("l2_before_pool")
            pool.sem_inc(sem["z_ready"], 2)
            pool.reg_mov(count, 0)
            halves = neg_half[:, 0:UNITS]
            pool.wait_ge(sem["slots_ready"], 1)
            with pool.Fori(0, GROUPS) as g:
                done = pool.snap(g * GB)
                pool.wait_ge(sem["var_ready"], g + 1)
                nc.gpsimd.tensor_tensor(rstd[:], var[:], halves, ALU.pow).then_inc(sem["rstd_ready"], 1)
                for b in range(GB):
                    units = slice(b * NB, (b + 1) * NB)
                    pool.wait_ge(sem["hi_ready"], done + (b + 1))
                    nc.gpsimd.tensor_tensor(m[:, units], m[:, units], parts[:, units, 0], ALU.subtract).then_inc(sem["rest1_ready"], 1)
                for b in range(GB):
                    units = slice(b * NB, (b + 1) * NB)
                    pool.wait_ge(sem["mid_ready"], done + (b + 1))
                    pool.wait_ge(sem["rest1_ready"], done + (b + 1))
                    nc.gpsimd.tensor_tensor(m[:, units], m[:, units], parts[:, units, 1], ALU.subtract).then_inc(sem["rest2_ready"], 1)
                n = pool.value_load(n_slots[0:1, bass.ds(g, 1)], min_val=3, max_val=N)
                pairs = pool.snap((n + 1) // 2)
                before = pool.snap(count)

                def shift(par, steps, half):
                    units = slice(half * HALF, (half + 1) * HALF)
                    pool.wait_ge(sem["z_made"], steps * 2 + (half + 1))
                    nc.gpsimd.tensor_tensor(z[par][:, units], z[par][:, units], wide(bc["L2_gnn_be1"])[:, units],
                                            ALU.add).then_inc(sem["z_ready"], 1)

                def pool_step(par, step, first=False):
                    if not first:
                        shift(1 - par, step, 0)
                    pool.wait_ge(sem["pvar_ready"], step + 1)
                    nc.gpsimd.tensor_tensor(prstd[:], pvar[:], halves, ALU.pow).then_inc(sem["prstd_ready"], 1)
                    if not first:
                        shift(1 - par, step, 1)

                pool_step(0, before, first=True)
                pool_step(1, pool.snap(before + 1))
                with pool.Fori(1, pairs) as t:
                    for par in range(2):
                        pool_step(par, pool.snap(before + (t * 2 + par)))
                pool.reg_add(count, count, pairs * 2)
                after = pool.snap(count)
                shift(1, after, 0)
                shift(1, after, 1)
                pool.wait_ge(sem["upd_var_ready"], g + 1)
                nc.gpsimd.tensor_tensor(rstd[:], var[:], halves, ALU.pow).then_inc(sem["upd_rstd_ready"], 1)
                pool.wait_ge(sem["upd_scaled"], g + 1)
                nc.gpsimd.tensor_tensor(scaled[:], scaled[:], wide(bc["L2_gnn_be2"]), ALU.add).then_inc(sem["upd_shifted"], 1)

        @block.scalar
        def _(act):
            count = act.alloc_register("l2_before_act")
            act.sem_inc(sem["msg_ready"], 6)
            act.sem_inc(sem["diag_ready"], 1)
            act.reg_mov(count, 0)

            def seed(par, half):
                units = slice(half * HALF, (half + 1) * HALF)
                nc.scalar.activation(ps_m[par][:, units], own[:, units], ACT.Copy).then_inc(sem["seeded"], 1)

            def keep_index(g):
                for c in range(CHUNKS):
                    act.wait_ge(sem["index_turned"], g * CHUNKS + (c + 1))
                    nc.scalar.activation(indexT[:, c], ps_spread[:], ACT.Copy).then_inc(sem["index_kept"], 1)

            act.wait_ge(sem["slots_ready"], 1)
            keep_index(0)

            def act_group(g, last=False):
                done = act.snap(g * GB)
                act.wait_ge(sem["h_turned"], g + 1)
                nc.scalar.activation(hT[:], ps_m[0][:].rearrange("p (b k) d -> p b (k d)", b=GB), ACT.Copy).then_inc(sem["h_kept"], 1)
                for b in range(GB):
                    units = slice(b * NB, (b + 1) * NB)
                    act.wait_ge(sem["m_ready"], done + (b + 1))
                    nc.scalar.activation(parts[:, units, 0], m[:, units],
                                         ACT.Copy).then_inc(sem["hi_ready"], 1)
                act.wait_ge(sem["bits_set"], g + 1)
                for par in range(2):
                    seed(par, 0)
                    seed(par, 1)
                for i, (wait, then) in enumerate((("rest1_ready", "mid_ready"), ("rest2_ready", "parts_ready"))):
                    for b in range(GB):
                        units = slice(b * NB, (b + 1) * NB)
                        act.wait_ge(sem[wait], done + (b + 1))
                        nc.scalar.activation(parts[:, units, i + 1], m[:, units],
                                             ACT.Copy).then_inc(sem[then], 1)
                n = act.value_load(n_slots[0:1, bass.ds(g, 1)], min_val=3, max_val=N)
                pairs = act.snap((n + 1) // 2)
                before = act.snap(count)

                def keep_spread(ahead):
                    act.wait_ge(sem["spread_made"], ahead + (g + 1))
                    nc.scalar.activation(spread[:], ps_spread[:], ACT.Copy).then_inc(sem["spread_kept"], 1)

                first_ahead = act.snap(before + g * 2)
                keep_spread(first_ahead)
                act.wait_ge(sem["onehot_ready"], first_ahead + 1)
                keep_spread(first_ahead + 1)

                def gelu(par, steps, half):
                    units = slice(half * HALF, (half + 1) * HALF)
                    act.wait_ge(sem["z_ready"], steps * 2 + (half + 1))
                    act.wait_ge(sem["summed"], steps * 2 + (half + 1))
                    nc.scalar.activation(msg[par][:, units], z[par][:, units], ACT.Gelu).then_inc(sem["msg_ready"], 1)

                def diagonals(par, steps, slot):
                    act.wait_ge(sem["summed"], steps * 2 + 2)
                    for u in range(UNITS):
                        ins = nc.scalar.activation(diag[par][:, u], ident[:], ACT.Copy,
                                                   scale=value[:, u, bass.ds(slot, 1)])
                    ins.then_inc(sem["diag_ready"], 1)

                def act_step(par, step, slot, first=False, second=False):
                    ahead = act.snap(step + g * 2 + 2)
                    act.wait_ge(sem["onehot_ready"], ahead)
                    keep_spread(ahead)
                    if not (first or second):
                        gelu(par, act.snap(step - 1), 1)
                    if not first:
                        for half in range(2):
                            act.wait_ge(sem["z_made"], step * 2 + (half + 1))
                            seed(1 - par, half)
                        gelu(1 - par, step, 0)
                        diagonals(1 - par, step, slot - 1)

                act_step(0, before, 0, first=True)
                act_step(1, act.snap(before + 1), 1, second=True)
                with act.Fori(1, pairs) as t:
                    for par in range(2):
                        slot = act.snap(t * 2 + par)
                        act_step(par, act.snap(before + slot), slot)
                act.reg_add(count, count, pairs * 2)
                after = act.snap(count)
                gelu(0, act.snap(after - 1), 1)
                gelu(1, after, 0)
                diagonals(1, after, act.snap(pairs * 2 - 1))
                gelu(1, after, 1)
                act.wait_ge(sem["onehot_ready"], after + (g * 2 + 2))
                act.wait_ge(sem["agg_done"], g + 1)
                nc.scalar.activation(aggT[:], ps_agg[:], ACT.Copy).then_inc(sem["agg_kept"], 1)
                if not last:
                    keep_index(g + 1)

            with act.Fori(0, GROUPS - 1) as g:
                act_group(g)
            act_group(GROUPS - 1, last=True)

        @block.vector
        def _(dve):
            nc.vector.tensor_reduce(w1_sum[:, 0:2], keep["W1"][:], AX.X, ALU.add)
            nc.vector.tensor_reduce(w1_sum[:, 2:3], bc["L2_gnn_b1"][:], AX.X, ALU.add)
            nc.vector.memset(value[:], 0.0)
            dve.drain()
            nc.vector.tensor_scalar(w1_mean[:], w1_sum[:], 1.0 / D, None, ALU.mult)
            dve.drain()
            for t in range(2):
                nc.vector.tensor_scalar(W1c[:, t], keep["W1"][:, t], w1_mean[:, t:t + 1], None, ALU.subtract)
            nc.vector.tensor_scalar(b1c[:], bc["L2_gnn_b1"][:], w1_mean[:, 2:3], None, ALU.subtract)
            dve.drain().then_inc(sem["w1_ready"], 1)
            dve.wait_ge(sem["consts"], 1)
            sign_sums = keep["sign_sums"]
            nc.vector.tensor_tensor(negatives[:], sign_sums[:, 1], sign_sums[:, 0], ALU.subtract)
            dve.drain()
            nc.vector.scalar_tensor_tensor(needed[:], negatives[:], float(N), sign_sums[:, 0], ALU.mult, ALU.add)
            dve.drain()
            nc.vector.tensor_reduce(needed_p[:], needed[:].rearrange("p (g u) -> p g u", g=GROUPS), AX.X,
                                    ALU.max).then_inc(sem["needed_ready"], 1)
            dve.wait_ge(sem["needed_turned"], 1)
            nc.vector.tensor_reduce(needed_g[:], ps_m[0][0:GROUPS, 0, :], AX.X, ALU.max).then_inc(sem["needed_ready"], 1)
            dve.wait_ge(sem["needed_turned"], 2)
            nc.vector.tensor_scalar(n_slots[:], ps_m[1][0:1, 0, 0:GROUPS], 3.0, float(N), ALU.max, ALU.min)
            dve.drain().then_inc(sem["slots_ready"], 1)
            dve.wait_ge(sem["slots_ready"], 1)
            count = dve.alloc_register("l2_before_dve")
            dve.sem_inc(sem["z_made"], 2)
            dve.reg_mov(count, 0)

            def take_slots(g):
                for b in range(GB):
                    dve.wait_ge(adj_in[b], g * 16 + 16)
                dve.sem_inc(keep["held"], 1)
                n = dve.value_load(n_slots[0:1, bass.ds(g, 1)], min_val=3, max_val=N)
                with dve.Fori(0, ((n + 1) // 2 * 2 + 10) // 8) as r:
                    for u in range(UNITS):
                        nc.vector.max(top[:, u], adj[:, u])
                    dve.drain()
                    for u in range(UNITS):
                        nc.vector.max_index(top_at[:, u], top[:, u], adj[:, u])
                    nc.vector.tensor_copy(value[:, :, bass.ds(r * 8, 8)], top[:])
                    dve.drain()
                    for u in range(UNITS):
                        nc.vector.match_replace(adj[:, u], top[:, u], adj[:, u], LOWEST)
                    nc.vector.tensor_copy(index[:, :, bass.ds(r * 8, 8)], top_at[:])
                    dve.drain()
                dve.drain().then_inc(sem["index_ready"], 1)

            take_slots(0)

            def dve_group(g, last=False):
                done = dve.snap(g * GB)
                xg = x[:, bass.ds(done, GB)].rearrange("p b k d -> p (b k) d")
                for u in range(UNITS):
                    nc.vector.bn_stats(stats[:, u], xg[:, u])
                dve.drain()
                for u in range(UNITS):
                    nc.vector.bn_aggr(mv[:, u], stats[:, u])
                dve.drain()
                nc.vector.tensor_scalar(var[:], mv[:, :, 1], LN_EPS, None, ALU.add).then_inc(sem["var_ready"], 1)
                dve.wait_ge(sem["rstd_ready"], g + 1)
                for u in range(UNITS):
                    nc.vector.tensor_scalar(normed[:, u], xg[:, u], mv[:, u, 0:1], rstd[:, u:u + 1], ALU.subtract, ALU.mult)
                dve.drain()
                nc.vector.tensor_scalar(h[:], normed[:], 0.0, None, ALU.max).then_inc(sem["h_ready"], 1)
                for b in range(GB):
                    dve.wait_ge(sem["m_made"], done + (b + 1))
                    pm = ps_m[b // 2][:, (b % 2) * 4:(b % 2) * 4 + 4].rearrange("p (k t) d -> p k t d", t=2)
                    nc.vector.tensor_copy(m[:, b * NB:(b + 1) * NB], pm[:, :, 0])
                    nc.vector.tensor_tensor(own[:, b * NB:(b + 1) * NB], pm[:, :, 1], b1c[:].rearrange(
                        "p (a d) -> p a d", a=1).broadcast_to((P, NB, D)), ALU.add).then_inc(sem["m_ready"], 1)
                n = dve.value_load(n_slots[0:1, bass.ds(g, 1)], min_val=3, max_val=N)
                pairs = dve.snap((n + 1) // 2)
                before = dve.snap(count)

                def pick(ahead, par):
                    dve.wait_ge(sem["spread_kept"], ahead + 1)
                    for k in range(NB):
                        ins = nc.vector.tensor_scalar(onehot[:, par, k], spread[:], node_of[:, k:k + 1], None, ALU.is_equal)
                    ins.then_inc(sem["onehot_ready"], 1)

                first_ahead = dve.snap(before + g * 2)
                pick(first_ahead, 0)
                pick(first_ahead + 1, 1)

                def normalise(par, half):
                    for u in range(half * HALF, (half + 1) * HALF):
                        ins = nc.vector.scalar_tensor_tensor(z[par][:, u], ps_m[par][:, u], prstd[:, u:u + 1],
                                                             bc["L2_gnn_g1"][:], ALU.mult, ALU.mult)
                    ins.then_inc(sem["z_made"], 1)

                def dve_step(par, step, first=False):
                    for half in range(2):
                        dve.wait_ge(sem["gathered"], (step + g) * 2 + (half + 1))
                        for u in range(half * HALF, (half + 1) * HALF):
                            ins = nc.vector.bn_stats(pstats[:, u], ps_m[par][:, u])
                        if half == 1:
                            ins.then_inc(sem["stats_done"], 1)
                        if not first:
                            dve.wait_ge(sem["prstd_ready"], step)
                            dve.wait_ge(sem["msg_ready"], step * 2 + (half + 1))
                            normalise(1 - par, half)
                    dve.wait_ge(sem["stats_done"], step + 1)
                    nc.vector.tensor_tensor(dmean[:], pstats[:, :, 1], pstats[:, :, 4], ALU.subtract)
                    nc.vector.scalar_tensor_tensor(msum[:], pstats[:, :, 2], D * LN_EPS, pstats[:, :, 5],
                                                   ALU.add, ALU.add).then_inc(sem["dve_step"], 1)
                    dve.wait_ge(sem["dve_step"], step * 2 + 1)
                    nc.vector.scalar_tensor_tensor(dmean2[:], dmean[:], 0.25, dmean[:], ALU.mult,
                                                   ALU.mult).then_inc(sem["dve_step"], 1)
                    dve.wait_ge(sem["dve_step"], step * 2 + 2)
                    nc.vector.scalar_tensor_tensor(pvar[:], msum[:], 1.0 / D, dmean2[:], ALU.mult,
                                                   ALU.add).then_inc(sem["pvar_ready"], 1)
                    pick(dve.snap(step + g * 2 + 2), par)

                dve_step(0, before, first=True)
                dve_step(1, dve.snap(before + 1))
                with dve.Fori(1, pairs) as t:
                    for par in range(2):
                        dve_step(par, dve.snap(before + (t * 2 + par)))
                dve.reg_add(count, count, pairs * 2)
                after = dve.snap(count)
                dve.wait_ge(sem["gathered"], (after + g) * 2 + 2)
                dve.wait_ge(sem["prstd_ready"], after)
                for half in range(2):
                    dve.wait_ge(sem["msg_ready"], after * 2 + (half + 1))
                    normalise(1, half)
                if not last:
                    dve.wait_ge(sem["diag_ready"], after + 1)
                    take_slots(g + 1)
                dve.wait_ge(sem["upd_made"], g + 1)
                nc.vector.tensor_tensor(upd, ps_spread[:].rearrange("p (u d) -> p u d", u=UNITS), wide(bc["L2_gnn_b2"]),
                                        ALU.add).then_inc(sem["upd_read"], 1)
                dve.drain()
                for u in range(UNITS):
                    nc.vector.bn_stats(stats[:, u], upd[:, u])
                dve.drain()
                for u in range(UNITS):
                    nc.vector.bn_aggr(mv[:, u], stats[:, u])
                dve.drain()
                nc.vector.tensor_scalar(var[:], mv[:, :, 1], LN_EPS, None, ALU.add).then_inc(sem["upd_var_ready"], 1)
                dve.wait_ge(sem["upd_rstd_ready"], g + 1)
                for u in range(UNITS):
                    nc.vector.tensor_scalar(normed[:, u], upd[:, u], mv[:, u, 0:1], rstd[:, u:u + 1], ALU.subtract, ALU.mult)
                dve.drain()
                nc.vector.tensor_tensor(scaled[:], normed[:], wide(bc["L2_gnn_g2"]), ALU.mult).then_inc(sem["upd_scaled"], 1)
                dve.wait_ge(sem["upd_shifted"], g + 1)
                nc.vector.tensor_tensor(xg, xg, scaled[:], ALU.add).then_inc(sem["x_done"], 1)
                dve.wait_ge(sem["x_done"], g + 1)
                dve.sem_inc(keep["held"], 1)

            with dve.Fori(0, GROUPS - 1) as g:
                dve_group(g)
            dve_group(GROUPS - 1, last=True)

        @block.tensor
        def _(pe):
            pe.wait_ge(sem["consts"], 1)
            pe.wait_ge(sem["w1_ready"], 1)
            count = pe.alloc_register("l2_before_pe")
            pe.sem_inc(sem["summed"], 6)
            pe.reg_mov(count, 0)

            def turn_index(g):
                pe.wait_ge(sem["index_ready"], g + 1)
                for c in range(CHUNKS):
                    if c:
                        pe.wait_ge(sem["index_kept"], g * CHUNKS + c)
                    for u in range(UNITS):
                        ins = nc.tensor.transpose(ps_spread[:, u * P:(u + 1) * P], index[:, u, c * P:(c + 1) * P], ident[:])
                    ins.then_inc(sem["index_turned"], 1)

            pe.wait_ge(sem["needed_ready"], 1)
            nc.tensor.transpose(ps_m[0][0:GROUPS, 0, :], needed_p[:], ident[:]).then_inc(sem["needed_turned"], 1)
            pe.wait_ge(sem["needed_ready"], 2)
            nc.tensor.transpose(ps_m[1][0:1, 0, 0:GROUPS], needed_g[:], ident[0:GROUPS, 0:GROUPS]).then_inc(sem["needed_turned"], 1)
            pe.wait_ge(sem["slots_ready"], 1)
            turn_index(0)

            def pe_group(g, last=False):
                pe.wait_ge(sem["h_ready"], g + 1)
                for u in range(UNITS):
                    ins = nc.tensor.transpose(ps_m[0][:, u], h[:, u], ident[:])
                ins.then_inc(sem["h_turned"], 1)
                pe.wait_ge(sem["h_kept"], g + 1)
                for b in range(GB):
                    for k in range(NB):
                        lane = (b % 2) * 4 + 2 * k
                        ins = nc.tensor.matmul(ps_m[b // 2][:, lane:lane + 2], hT[:, b, k * P:(k + 1) * P], W1c[:],
                                               start=True, stop=True)
                    ins.then_inc(sem["m_made"], 1)
                pe.wait_ge(sem["m_ready"], g * GB + GB)
                for i in range(2):
                    for c in range(2):
                        ins = nc.tensor.matmul(ps_m[i][:, c * HALF:(c + 1) * HALF], zero16[:, 0:P], zero16[:],
                                               start=True, stop=False, skip_group_check=True)
                ins.then_inc(sem["bits_set"], 1)
                for b in range(2):
                    nc.tensor.matmul(ps_agg[:].rearrange("p (c b) n -> p c (b n)", c=2)[:, b], zero16[:, 0:P], zero16[:],
                                     start=True, stop=False, skip_group_check=True)
                pe.wait_ge(sem["index_kept"], g * CHUNKS + CHUNKS)
                pe.sem_inc(keep["held"], 1)
                n = pe.value_load(n_slots[0:1, bass.ds(g, 1)], min_val=3, max_val=N)
                pairs = pe.snap((n + 1) // 2)
                before = pe.snap(count)

                def spread_out(slot):
                    for c in range(2):
                        ins = nc.tensor.matmul(ps_spread[:, c * 512:(c + 1) * 512],
                                               ident16[:, bass.ds(slot % P, 1)].broadcast_to((P, P)),
                                               indexT[:, bass.ds(slot // P, 1), c * 512:(c + 1) * 512].rearrange("p a n -> p (a n)"),
                                               start=True, stop=True)
                    ins.then_inc(sem["spread_made"], 1)

                def gather(par, number, half):
                    pe.wait_ge(sem["seeded"], number * 2 + (half + 1))
                    for u in range(half * HALF, (half + 1) * HALF):
                        b = u // NB
                        for k in range(NB):
                            for t in range(3):
                                ins = nc.tensor.matmul(ps_m[par][:, u], onehot[:, par, k, u * P:(u + 1) * P],
                                                       parts[:, b * NB + k, t], start=False, stop=False,
                                                       skip_group_check=True)
                    ins.then_inc(sem["gathered"], 1)

                def aggregate(par, steps, half):
                    pe.wait_ge(sem["msg_ready"], steps * 2 + (half + 5))
                    pe.wait_ge(sem["diag_ready"], steps + 1)
                    for u in range(half * HALF, (half + 1) * HALF):
                        ins = nc.tensor.matmul(ps_agg[:, u // NB, (u % NB) * P:(u % NB + 1) * P], msg[par][:, u], diag[par][:, u],
                                               start=False, stop=False, skip_group_check=True)
                    ins.then_inc(sem["summed"], 1)

                first_ahead = pe.snap(before + g * 2)
                spread_out(0)
                pe.wait_ge(sem["spread_kept"], first_ahead + 1)
                spread_out(1)
                pe.wait_ge(sem["parts_ready"], g * GB + GB)
                pe.wait_ge(sem["onehot_ready"], first_ahead + 1)
                for half in range(2):
                    gather(0, pe.snap(before + g), half)
                pe.wait_ge(sem["spread_kept"], first_ahead + 2)
                spread_out(2)

                def pe_step(par, step, slot, first=False, second=False):
                    ahead = pe.snap(step + g * 2 + 2)
                    pe.wait_ge(sem["onehot_ready"], ahead)
                    gather(1 - par, pe.snap(step + g + 1), 0)
                    pe.wait_ge(sem["spread_kept"], ahead + 1)
                    spread_out(slot + 3)
                    gather(1 - par, pe.snap(step + g + 1), 1)
                    if not (first or second):
                        for half in range(2):
                            aggregate(par, pe.snap(step - 1), half)

                pe_step(0, before, 0, first=True)
                pe_step(1, pe.snap(before + 1), 1, second=True)
                with pe.Fori(1, pairs) as t:
                    for par in range(2):
                        slot = pe.snap(t * 2 + par)
                        pe_step(par, pe.snap(before + slot), slot)
                pe.reg_add(count, count, pairs * 2)
                after = pe.snap(count)
                for par in range(2):
                    for half in range(2):
                        aggregate(par, pe.snap(after + par - 1), half)
                for b in range(2):
                    ins = nc.tensor.matmul(ps_agg[:].rearrange("p (c b) n -> p c (b n)", c=2)[:, b], zero16[:, 0:P], zero16[:],
                                           start=False, stop=True, skip_group_check=True)
                ins.then_inc(sem["agg_done"], 1)
                pe.wait_ge(sem["agg_kept"], g + 1)
                pe.wait_ge(sem["spread_kept"], after + (g * 2 + 2))
                pe.wait_ge(sem["spread_made"], after + (g * 3 + 3))
                for u in range(UNITS):
                    b, k = divmod(u, NB)
                    nc.tensor.matmul(ps_spread[:, u * P:(u + 1) * P], hT[:, b, k * P:(k + 1) * P], keep["W2"][:, 0],
                                     start=True, stop=False)
                    ins = nc.tensor.matmul(ps_spread[:, u * P:(u + 1) * P], aggT[:, b, k * P:(k + 1) * P], keep["W2"][:, 1],
                                           start=False, stop=True)
                ins.then_inc(sem["upd_made"], 1)
                if not last:
                    pe.wait_ge(sem["upd_read"], g + 1)
                    turn_index(g + 1)

            with pe.Fori(0, GROUPS - 1) as g:
                pe_group(g)
            pe_group(GROUPS - 1, last=True)



def layer3(nc, w, keep, out):
    with ExitStack() as stack:
        s = Scope(nc, stack, "l3_")
        x, ident, neg_half = keep["x"], keep["ident"], keep["neg_half"]
        adj = s.sb("adj", [P, GB, NB, N])
        adj_row = s.sb("adj_row", [P, GB, NB, N])
        adjT_col = s.sb("adjT_col", [P, GB, NB, N])
        rowT = s.sb("rowT", [P, GB, NB, N])
        colA = s.sb("colA", [P, GB, NB, N])
        junk = s.sb("junk", [P, GB, 2, N])
        sums = s.sb("sums", [P, GB, 2, NB])
        clamped = s.sb("clamped", [P, GB, 2, NB])
        inv = s.sb("inv", [P, GB, 2, NB])
        stats = s.sb("stats", [P, GB, NB, 6])
        mv = s.sb("mv", [P, GB, NB, 2])
        var = s.sb("var", [P, GB, NB])
        rstd = s.sb("rstd", [P, GB, NB])
        normed = s.sb("normed", [P, GB, NB, D])
        h = s.sb("h", [P, GB, NB, D])
        fT = s.sb("fT", [P, GB, 5, N])
        sd = s.sb("sd", [P, GB, NB, 2 * D])
        xout = s.sb("xout", [P, GB, NB, D])
        names = ("summed", "clamped", "inv_ready", "stats_ready", "mv_ready", "var_ready", "rstd_ready",
                 "normed_ready", "h_ready", "adj_turned", "row_scaled", "col_scaled", "row_turned", "row_kept",
                 "col_turned", "col_kept", "h_turned", "h_kept", "sd_made", "sd_kept", "f_made", "f_kept",
                 "f_turned", "x_ready", "col_squared", "row_squared")
        sem = {n: s.sem(n) for n in names}
        adj_in = [s.sem(f"adj_in{b}") for b in range(GB)]
        x_stored = [s.sem(f"x_stored{b}") for b in range(GB)]
        ps_adj = [s.psum(f"ps_adj{i}", [P, NB, N]) for i in range(4)]
        ps_sd = ps_adj[2:]
        ps_turn = [s.psum(f"ps_turn{i}", [P, NB, N]) for i in range(2)]
        ps_f = [s.psum(f"ps_f{i}", [P, 512]) for i in range(2)]
        block = stack.enter_context(nc.Block())

        @block.sync
        def _(sp):
            with sp.Fori(0, GROUPS) as g:
                done = sp.snap(g * GB)
                for b in range(GB):
                    sp.dma_start(adj[:, b], w["adj"][bass.ds(done + b, 1)].rearrange(
                        "b (k p) j -> p (b k) j", p=P)).then_inc(adj_in[b], 16)
                for b in range(GB):
                    sp.wait_ge(sem["x_ready"], done + (b + 1))
                    sp.dma_start(out[bass.ds(done + b, 1)].rearrange("b (k p) d -> p (b k) d", p=P),
                                 xout[:, b]).then_inc(x_stored[b], 16)
                for b in range(GB):
                    sp.wait_ge(x_stored[b], g * 16 + 16)
                sp.sem_inc(keep["held"], 1)

        @block.gpsimd
        def _(pool):
            with pool.Fori(0, GROUPS) as g:
                done = pool.snap(g * GB)
                pool.wait_ge(sem["mv_ready"], (done + GB))
                pool.sem_inc(keep["held"], 1)
                nc.gpsimd.tensor_scalar(var[:], mv[:, :, :, 1], LN_EPS, 1.0, ALU.add, ALU.mult).then_inc(sem["var_ready"], 1)
                pool.wait_ge(sem["var_ready"], g + 1)
                nc.gpsimd.tensor_tensor(rstd[:], var[:], neg_half[:, 0:GB * NB].rearrange("p (b k) -> p b k", b=GB),
                                        ALU.pow).then_inc(sem["rstd_ready"], 1)
                for b in range(GB):
                    pool.wait_ge(sem["clamped"], done + (b + 1))
                    nc.gpsimd.tensor_tensor(inv[:, b], clamped[:, b], neg_half[:, 0:2 * NB].rearrange(
                        "p (a k) -> p a k", a=2), ALU.pow).then_inc(sem["inv_ready"], 1)

        @block.vector
        def _(dve):
            with dve.Fori(0, GROUPS) as g:
                done = dve.snap(g * GB)
                for b in range(GB):
                    for k in range(NB):
                        ins = nc.vector.bn_stats(stats[:, b, k], x[:, bass.ds(done + b, 1), k].rearrange("p a d -> p (a d)"))
                    ins.then_inc(sem["stats_ready"], 1)
                for b in range(GB):
                    dve.wait_ge(sem["stats_ready"], done + (b + 1))
                    dve.sem_inc(keep["held"], 1)
                    for k in range(NB):
                        ins = nc.vector.bn_aggr(mv[:, b, k], stats[:, b, k])
                    ins.then_inc(sem["mv_ready"], 1)
                for b in range(GB):
                    dve.wait_ge(sem["summed"], done + (b + 1))
                    nc.vector.tensor_scalar(clamped[:, b], sums[:, b], 1e-24, None, ALU.max).then_inc(sem["clamped"], 1)
                dve.wait_ge(sem["rstd_ready"], g + 1)
                dve.wait_ge(sem["mv_ready"], done + GB)
                for b in range(GB):
                    for k in range(NB):
                        ins = nc.vector.tensor_scalar(normed[:, b, k], x[:, bass.ds(done + b, 1), k].rearrange("p a d -> p (a d)"), mv[:, b, k, 0:1],
                                                      rstd[:, b, k:k + 1], ALU.subtract, ALU.mult)
                    ins.then_inc(sem["normed_ready"], 1)
                for b in range(GB):
                    dve.wait_ge(sem["normed_ready"], done + (b + 1))
                    nc.vector.tensor_scalar(h[:, b], normed[:, b], 0.0, None, ALU.max).then_inc(sem["h_ready"], 1)
                for b in range(GB):
                    dve.wait_ge(sem["inv_ready"], done + (b + 1))
                    dve.wait_ge(adj_in[b], g * 16 + 16)
                    for k in range(NB):
                        ins = nc.vector.tensor_scalar(adj_row[:, b, k], adj[:, b, k], inv[:, b, 0, k:k + 1], None, ALU.mult)
                    ins.then_inc(sem["row_scaled"], 1)
                    for k in range(NB):
                        ins = nc.vector.tensor_scalar(adjT_col[:, b, k], ps_adj[b][:, k], inv[:, b, 1, k:k + 1],
                                                      None, ALU.mult)
                    ins.then_inc(sem["col_scaled"], 1)
                for l in range(4):
                    for b in range(GB):
                        n = (4 * g + l) * GB + (b + 1)
                        dve.wait_ge(sem["sd_made"], n)
                        nc.vector.tensor_tensor(sd[:, b], ps_sd[b % 2][:],
                                                keep["l3_bsd"][:, l:l + 1, :].broadcast_to((P, NB, 2 * D)),
                                                ALU.add).then_inc(sem["sd_kept"], 1)
                for b in range(GB):
                    dve.wait_ge(sem["f_turned"], done + (b + 1))
                    nc.vector.tensor_tensor(xout[:, b], x[:, bass.ds(done + b, 1)].rearrange("p a k d -> p (a k) d"),
                                            ps_turn[b % 2][:, 0, :].rearrange("p (k d) -> p k d", k=NB),
                                            ALU.add).then_inc(sem["x_ready"], 1)
                for b in range(GB):
                    dve.wait_ge(x_stored[b], g * 16 + 16)

        @block.scalar
        def _(act):
            with act.Fori(0, GROUPS) as g:
                done = act.snap(g * GB)
                for b in range(GB):
                    act.wait_ge(adj_in[b], g * 16 + 16)
                    for k in range(NB):
                        ins = nc.scalar.activation(junk[:, b, 0], adj[:, b, k], ACT.Square, accum_out=sums[:, b, 0, k:k + 1])
                        ins.then_inc(sem["row_squared"], 1)
                        act.wait_ge(sem["row_squared"], (done + b) * NB + (k + 1))
                    act.wait_ge(sem["adj_turned"], done + (b + 1))
                    for k in range(NB):
                        ins = nc.scalar.activation(junk[:, b, 1], ps_adj[b][:, k], ACT.Square,
                                                   accum_out=sums[:, b, 1, k:k + 1])
                        if k < NB - 1:
                            ins.then_inc(sem["col_squared"], 1)
                            act.wait_ge(sem["col_squared"], (done + (b + 1)))
                    ins.then_inc(sem["summed"], 1)
                for b in range(GB):
                    act.wait_ge(sem["h_turned"], done + (b + 1))
                    nc.scalar.activation(fT[:, b, 0], ps_f[b % 2][:, 0:N], ACT.Copy).then_inc(sem["h_kept"], 1)
                for b in range(GB):
                    act.wait_ge(sem["row_turned"], done + (b + 1))
                    nc.scalar.activation(rowT[:, b], ps_turn[b % 2][:], ACT.Copy).then_inc(sem["row_kept"], 1)
                for b in range(GB):
                    act.wait_ge(sem["col_turned"], done + (b + 1))
                    nc.scalar.activation(colA[:, b], ps_turn[b % 2][:], ACT.Copy).then_inc(sem["col_kept"], 1)
                for l in range(4):
                    for b in range(GB):
                        n = (4 * g + l) * GB + (b + 1)
                        act.wait_ge(sem["f_made"], n)
                        nc.scalar.activation(fT[:, b, l + 1], ps_f[b % 2][:, 0:N], ACT.Tanh,
                                             bias=keep["l3_c"][:, l:l + 1]).then_inc(sem["f_kept"], 1)

        @block.tensor
        def _(pe):
            def turn(dst, src, last_sem):
                for kr in range(NB):
                    for kc in range(NB):
                        ins = nc.tensor.transpose(dst[:, kc, kr * P:(kr + 1) * P], src[:, kr, kc * P:(kc + 1) * P], ident[:])
                ins.then_inc(last_sem, 1)

            with pe.Fori(0, GROUPS) as g:
                done = pe.snap(g * GB)
                for b in range(GB):
                    pe.wait_ge(adj_in[b], g * 16 + 16)
                    turn(ps_adj[b], adj[:, b], sem["adj_turned"])
                for b in range(GB):
                    pe.wait_ge(sem["h_ready"], done + (b + 1))
                    if b >= 2:
                        pe.wait_ge(sem["h_kept"], done + (b - 1))
                    for k in range(NB):
                        ins = nc.tensor.transpose(ps_f[b % 2][:, k * P:(k + 1) * P], h[:, b, k], ident[:])
                    ins.then_inc(sem["h_turned"], 1)
                for b in range(GB):
                    pe.wait_ge(sem["row_scaled"], done + (b + 1))
                    if b >= 2:
                        pe.wait_ge(sem["row_kept"], done + (b - 1))
                    turn(ps_turn[b % 2], adj_row[:, b], sem["row_turned"])
                for b in range(GB):
                    pe.wait_ge(sem["col_scaled"], done + (b + 1))
                    pe.wait_ge(sem["row_kept"], done + (b + 3 if b < 2 else GB))
                    if b >= 2:
                        pe.wait_ge(sem["col_kept"], done + (b - 1))
                    turn(ps_turn[b % 2], adjT_col[:, b], sem["col_turned"])
                pe.wait_ge(sem["col_kept"], done + GB)
                for l in range(4):
                    for b in range(GB):
                        if l == 0:
                            pe.wait_ge(sem["h_kept"], done + (b + 1))
                        else:
                            pe.wait_ge(sem["f_kept"], (4 * g + (l - 1)) * GB + (b + 1))
                        if l or b >= 2:
                            pe.wait_ge(sem["sd_kept"], (4 * g + l) * GB + (b - 1))
                        for k in range(NB):
                            for t, f in enumerate(L3_ORDER[l]):
                                ins = nc.tensor.matmul(ps_sd[b % 2][:, k], fT[:, b, f, k * P:(k + 1) * P],
                                                       keep["l3_wsd"][:, sum(L3_IN[:l]) + t, :],
                                                       start=t == 0, stop=t == L3_IN[l] - 1)
                        ins.then_inc(sem["sd_made"], 1)
                    for b in range(GB):
                        n = (4 * g + l) * GB + (b + 1)
                        pe.wait_ge(sem["sd_kept"], n)
                        if l == 0:
                            pe.wait_ge(sem["h_kept"], done + GB)
                        if l or b >= 2:
                            pe.wait_ge(sem["f_kept"], (4 * g + l) * GB + (b - 1))
                        acc = ps_f[b % 2][:, 0:N]
                        for t, f in enumerate(L3_ORDER[l]):
                            nc.tensor.matmul(acc, keep["l3_wn"][:, sum(L3_IN[:l]) + t, :], fT[:, b, f],
                                             start=t == 0, stop=False)
                        for k in range(NB):
                            nc.tensor.matmul(acc, sd[:, b, k, 0:D], rowT[:, b, k], start=False, stop=False)
                            ins = nc.tensor.matmul(acc, sd[:, b, k, D:2 * D], colA[:, b, k], start=False, stop=k == NB - 1)
                        ins.then_inc(sem["f_made"], 1)
                for b in range(GB):
                    pe.wait_ge(sem["f_kept"], (4 * g + 3) * GB + (b + 1))
                    if b >= 2:
                        pe.wait_ge(sem["x_ready"], done + (b - 1))
                    for k in range(NB):
                        ins = nc.tensor.transpose(ps_turn[b % 2][:, 0, k * P:(k + 1) * P], fT[:, b, 4, k * P:(k + 1) * P], ident[:])
                    ins.then_inc(sem["f_turned"], 1)
                pe.wait_ge(sem["x_ready"], done + GB)


def build(nc, w, out, layers=(0, 2, 3)):
    with ExitStack() as stack:
        s = Scope(nc, stack, "all_")
        bc = {n: s.sb("bc_" + n, [P, D]) for n in ("L0_gnn_b", "L2_gnn_b1", "L2_gnn_g1", "L2_gnn_be1", "L2_gnn_b2",
                                                    "L2_gnn_g2", "L2_gnn_be2")}
        keep = {
            "x": s.sb("x", [P, B, NB, D]),
            "ident": s.sb("ident", [P, P]), "ones": s.sb("ones", [P, P]), "neg_half": s.sb("neg_half", [P, 16]),
            "broadcast": bc, "sign_sums": s.sb("sign_sums", [P, 2, B * NB]),
            "ready": s.sem("ready"),
            "held": s.sem("held"),
            "W0": s.sb("W0", [P, D]), "att2": s.sb("att2", [P, 2]), "attb": s.sb("attb", [P, 1]),
            "W1": s.sb("W1", [P, 2, D]), "W2": s.sb("W2", [P, 2, D]),
            "l3_wsd": s.sb("l3_wsd", [P, sum(L3_IN), 2 * D]), "l3_wn": s.sb("l3_wn", [P, sum(L3_IN), D]),
            "l3_bsd": s.sb("l3_bsd", [P, 4, 2 * D]), "l3_c": s.sb("l3_c", [P, 4]),
        }
        prepare(nc, w, keep)
        if 0 in layers:
            layers01(nc, w, keep)
        if 2 in layers:
            layer2(nc, w, keep)
        if 3 in layers:
            layer3(nc, w, keep, out)
        else:
            with ExitStack() as st:
                o = st.enter_context(nc.semaphore("o"))
                block = st.enter_context(nc.Block())

                @block.sync
                def _(sp):
                    for g in range(GROUPS):
                        sp.dma_start(out[g * GB:(g + 1) * GB].rearrange("b (k p) d -> p b k d", p=P), keep["x"][:, g * GB:(g + 1) * GB]).then_inc(o, 16)
                    sp.wait_ge(o, 16 * GROUPS)


INPUTS = (["x", "adj", "L0_gnn_W", "L0_gnn_b", "L1_gnn_att_w", "L1_gnn_att_b"]
          + [f"L2_gnn_{n}" for n in ("W1", "b1", "g1", "be1", "W2", "b2", "g2", "be2")]
          + [f"L3_gnn_{n}{l}" for l in range(4) for n in ("ws", "bs", "wd", "bd", "wn", "bn", "wu", "bu")])


def kernel(**inputs):
    import numpy as np
    import concourse.bacc as bacc
    from concourse.bass_utils import run_bass_kernel_spmd

    nc = bacc.Bacc("TRN2", target_bir_lowering=False, num_devices=1)
    arrays, w = {}, {}
    for name in INPUTS:
        a = np.ascontiguousarray(inputs[name])
        if a.ndim == 0:
            a = a.reshape(1)
        arrays["in_" + name] = a
        w[name] = nc.dram_tensor("in_" + name, a.shape, mybir.dt.from_np(a.dtype), kind="ExternalInput").ap()
    out = nc.dram_tensor("out_x", (B, N, D), F32, kind="ExternalOutput").ap()
    build(nc, w, out)
    return run_bass_kernel_spmd(nc, [arrays], core_ids=[0]).results[0]["out_x"]
```

```python
from contextlib import ExitStack

import concourse.bass as bass
from concourse import mybir

P = 128
ALU = mybir.AluOpType
ACT = mybir.ActivationFunctionType
AX = mybir.AxisListType
F32 = mybir.dt.float32
BF16 = mybir.dt.bfloat16
I32 = mybir.dt.int32
U32 = mybir.dt.uint32

B, N, D = 64, 256, 128
NB = N // P
GB = 4
GROUPS = B // GB
LN_EPS = 1e-5
L3_IN = (1, 1, 2, 3)
L3_ORDER = ((0,), (1,), (2, 1), (3, 1, 0))


class Scope:

    def __init__(self, nc, stack, prefix):
        self.nc, self.stack, self.prefix = nc, stack, prefix

    def sb(self, name, shape, dtype=F32):
        return self.stack.enter_context(self.nc.sbuf_tensor(self.prefix + name, shape, dtype))

    def psum(self, name, shape, dtype=F32):
        return self.stack.enter_context(self.nc.psum_tensor(self.prefix + name, shape, dtype))

    def sem(self, name):
        return self.stack.enter_context(self.nc.semaphore(self.prefix + name))


def prepare(nc, w, keep):
    with ExitStack() as stack:
        s = Scope(nc, stack, "w_")
        kinds = ("s", "d", "n")
        tiles = [(l, k, t) for l in range(4) for k in range(3) for t in range(L3_IN[l])]
        raw = s.sb("raw", [P, len(tiles), D])
        wu = s.sb("wu", [P, 4, 3, D])
        bcol = s.sb("bcol", [P, 4, 4])
        bwide = s.sb("bwide", [P, 8, P])
        rawT = s.sb("rawT", [P, 2, P])
        loaded, consts, turned, copied, folded, kept, widened, biased, stored = (
            s.sem(n) for n in ("loaded", "consts", "turned", "copied", "folded", "kept", "widened", "biased", "stored"))
        ps_turn = [s.psum(f"ps_turn{i}", [P, 512]) for i in range(2)]
        ps_fold = [s.psum(f"ps_fold{i}", [P, 512]) for i in range(2)]
        ps_bias = [s.psum(f"ps_bias{i}", [P, 512]) for i in range(2)]
        n_loads = 0
        third = {"s": 0, "n": 1, "d": 2}
        block = stack.enter_context(nc.Block())

        def wide(l, kt):
            return sum(L3_IN[:l]) + kt

        @block.sync
        def _(sp):
            n = 0

            def load(dst, src):
                sp.dma_start(dst, src).then_inc(loaded, 16)

            for i, (l, k, t) in enumerate(tiles):
                if t == 0:
                    src = w[f"L3_gnn_w{kinds[k]}{l}"].rearrange("(t p) d -> p t d", p=P)
                    load(raw[:, i:i + L3_IN[l], :], src)
                    n += 1
            for l in range(4):
                load(wu[:, l], w[f"L3_gnn_wu{l}"].rearrange("(t p) d -> p t d", p=P))
                for c, name in enumerate(("bs", "bd", "bn", "bu")):
                    load(bcol[:, l, c:c + 1], w[f"L3_gnn_{name}{l}"].rearrange("(p a) -> p a", a=1))
                n += 5

            for name, dst in keep["broadcast"].items():
                load(dst[:], w[name].partition_broadcast(P))
                n += 1
            load(keep["W0"][:], w["L0_gnn_W"])
            for c in range(2):
                load(keep["att2"][:, c:c + 1], w["L1_gnn_att_w"][c * D:(c + 1) * D].rearrange("(p a) -> p a", a=1))
            load(keep["attb"][:], w["L1_gnn_att_b"].partition_broadcast(P))
            load(keep["W1"][:], w["L2_gnn_W1"].rearrange("(t p) d -> p t d", p=P))
            load(keep["W2"][:], w["L2_gnn_W2"].rearrange("(t p) d -> p t d", p=P))
            n += 6
            sp.wait_ge(loaded, 16 * n)
            sp.sem_inc(stored, 1)

        ident, ones, neg_half = keep["ident"], keep["ones"], keep["neg_half"]

        @block.gpsimd
        def _(pool):
            nc.gpsimd.memset(ident[:], 0.0).then_inc(consts, 1)
            pool.wait_ge(consts, 1)
            nc.gpsimd.affine_select(out=ident[:], in_=ident[:], compare_op=ALU.not_equal, fill=1.0, base=0,
                                    pattern=[[-1, P]], channel_multiplier=1).then_inc(consts, 1)
            nc.gpsimd.memset(ones[:], 1.0).then_inc(consts, 1)
            nc.gpsimd.memset(neg_half[:], -0.5).then_inc(consts, 1)

        @block.tensor
        def _(pe):
            pe.wait_ge(stored, 1)
            pe.wait_ge(consts, 4)

            def turn(i):
                if i >= 2:
                    pe.wait_ge(copied, i - 1)
                nc.tensor.transpose(ps_turn[i % 2][:, 0:P], raw[:, i, :], ident[:]).then_inc(turned, 1)

            turn(0)
            for i, (l, k, t) in enumerate(tiles):
                if i + 1 < len(tiles):
                    turn(i + 1)
                pe.wait_ge(copied, i + 1)
                if i >= 2:
                    pe.wait_ge(kept, i - 1)
                nc.tensor.matmul(ps_fold[i % 2][:, 0:P], rawT[:, i % 2, :], wu[:, l, third[kinds[k]], :],
                                 start=True, stop=True).then_inc(folded, 1)
            pe.wait_ge(widened, 8)
            for l in range(4):
                if l >= 2:
                    pe.wait_ge(biased, l - 1)
                bank = ps_bias[l % 2]
                nc.tensor.matmul(bank[:, 0:D], bwide[:, 2 * l, :], wu[:, l, 0, :], start=True, stop=True)
                nc.tensor.matmul(bank[:, D:2 * D], bwide[:, 2 * l + 1, :], wu[:, l, 2, :], start=True, stop=True)
                nc.tensor.matmul(bank[:, 2 * D:2 * D + 1], wu[:, l, 1, :], bcol[:, l, 2:3],
                                 start=True, stop=True).then_inc(folded, 1)

        @block.scalar
        def _(act):
            for i in range(len(tiles)):
                act.wait_ge(turned, i + 1)
                if i >= 2:
                    act.wait_ge(folded, i - 1)
                nc.scalar.activation(rawT[:, i % 2, :], ps_turn[i % 2][:, 0:P], ACT.Copy).then_inc(copied, 1)

        @block.vector
        def _(dve):
            dve.wait_ge(stored, 1)
            dve.wait_ge(consts, 4)
            for l in range(4):
                for c in range(2):
                    nc.vector.tensor_scalar(bwide[:, 2 * l + c, :], ones[:], bcol[:, l, c:c + 1], None,
                                            ALU.mult).then_inc(widened, 1)
            for i, (l, k, t) in enumerate(tiles):
                dve.wait_ge(folded, i + 1)
                kt = wide(l, t)
                dst = keep["l3_wn"][:, kt, :] if kinds[k] == "n" else keep["l3_wsd"][:, kt, (k == 1) * D:(k == 1) * D + D]
                nc.vector.tensor_copy(dst, ps_fold[i % 2][:, 0:P]).then_inc(kept, 1)
            for l in range(4):
                dve.wait_ge(folded, len(tiles) + l + 1)
                nc.vector.tensor_copy(keep["l3_bsd"][:, l, :], ps_bias[l % 2][:, 0:2 * D])
                nc.vector.tensor_tensor(keep["l3_c"][:, l:l + 1], ps_bias[l % 2][:, 2 * D:2 * D + 1], bcol[:, l, 3:4],
                                        ALU.add).then_inc(biased, 1)





MIN_NORM = 1e-15
MAX_TANH = 1.0 - 1e-7
L0_EPS = 1e-6
LN_EXP_TABLES = "natural_log_exp_and_others"
RANKS = 21


def layers01(nc, w, keep):
    with ExitStack() as stack:
        s = Scope(nc, stack, "l01_")
        x, ident, bc = keep["x"], keep["ident"], keep["broadcast"]
        units = GB * NB
        adj = s.sb("adj", [P, units, N])
        adjT = s.sb("adjT", [P, GB, NB, N])
        junk = s.sb("junk", [P, 2, N], BF16)
        signs = s.sb("signs", [P, 2, N], BF16)
        degree = s.sb("degree", [P, units])
        degree_eps = s.sb("degree_eps", [P, units])
        norm = s.sb("norm", [P, units])
        stats = s.sb("stats", [P, units, 6])
        mv = s.sb("mv", [P, units, 2])
        var = s.sb("var", [P, units])
        rstd = s.sb("rstd", [P, units])
        normed = s.sb("normed", [P, units, D])
        hn = s.sb("hn", [P, units, D])
        sumT = s.sb("sumT", [P, GB, N])
        z0 = s.sb("z0", [P, units, D])
        z0_low = s.sb("z0_low", [P, units, D])
        h = s.sb("h", [P, units, D + 1])
        hT = s.sb("hT", [P, GB, N])
        hT_m2 = s.sb("hT_m2", [P, GB, N])
        cols = s.sb("cols", [P, units, 4, 32])
        rows = s.sb("rows", [32, GB, 4, N], BF16)
        whole = s.sb("whole", [P, 4, units])
        part = s.sb("part", [P, 3, 4, units], BF16)
        pair = s.sb("pair", [P, GB, 2, NB * N])
        diff = s.sb("diff", [P, GB, NB * N])
        total = s.sb("total", [P, GB, NB * N])
        gate = s.sb("gate", [P, GB, NB * N])
        tangent = s.sb("tangent", [P, units, D])
        half = s.sb("half", [P, units])
        small = {n: s.sb("s_" + n, [P, units]) for n in (
            "p", "pc", "pn", "rpn", "u", "ln_a", "ln_b", "at", "scale", "lam", "dot", "alpha", "kb", "ka",
            "norm2", "norm2c", "norm1", "rlam", "targ", "th", "rnorm", "f", "f2", "y2", "hu", "hu2", "xy2", "num",
            "py2", "den", "denc", "rden", "ch", "cu0", "cu", "b1")}
        names = ("consts", "degree_ready", "eps_ready", "norm_ready", "var_ready", "rstd_ready", "hn_ready",
                 "adj_turned", "adjT_kept",
                 "sum_made", "sum_kept", "out_made", "z0_low_ready", "exp_ready", "x_ready", "var1_ready", "rstd1_ready",
                 "h_ready", "h_turned", "hT_kept", "hT_m2_kept", "lr_made", "pc_ready", "pn_ready", "rpn_ready", "u_ready",
                 "lns_ready", "cols_ready", "cols_turned", "rows_kept", "pair_made", "gate_made", "pair_clamped",
                 "pair_read", "square_ready", "ln_ready",
                 "diff_ready", "total_ready", "s_ready", "coef_ready", "u_clipped", "artanh_ready", "sigmoid_ready",
                 "gated", "c_ready", "s_made", "norm2_ready", "norm1_ready", "targ_ready", "th_ready", "group_done",
                 "abs_step", "signed")
        sem = {n: s.sem(n) for n in names}
        x_in = s.sem("x_in")
        adj_in = [s.sem(f"adj_in{b}") for b in range(GB)]
        ps_pair = [s.psum(f"ps_pair{i}", [P, 2, NB * N]) for i in range(2)]
        ps_gate = [s.psum(f"ps_gate{i}", [P, NB * N]) for i in range(2)]
        ps_work = [s.psum(f"ps_work{i}", [P, NB * N]) for i in range(2)]
        ps_s = ps_work + ps_gate
        scratch = diff[:].rearrange("p b (k e) -> p (b k) e", k=NB)[:, :, 0:D]
        block = stack.enter_context(nc.Block())


        def of(b):
            return slice(b * NB, (b + 1) * NB)

        @block.sync
        def _(sp):
            with sp.Fori(0, GROUPS) as g:
                done = sp.snap(g * GB)
                for b in range(GB):
                    sp.dma_start(adj[:, of(b)], w["adj"][bass.ds(done + b, 1)].rearrange(
                        "b (k p) j -> p (b k) j", p=P)).then_inc(adj_in[b], 16)
                sp.dma_start(x[:, bass.ds(done, GB)], w["x"][bass.ds(done, GB)].rearrange(
                    "b (k p) d -> p b k d", p=P)).then_inc(x_in, 16)
                sp.wait_ge(sem["degree_ready"], g + 1)
                sp.sem_inc(keep["held"], 1)
                sp.wait_ge(sem["signed"], g * (2 * units) + 2 * units)
                sp.sem_inc(keep["held"], 1)
                sp.wait_ge(sem["adj_turned"], done + GB)
                sp.sem_inc(keep["held"], 1)
                sp.wait_ge(x_in, g * 16 + 16)
                sp.sem_inc(keep["held"], 1)

        @block.gpsimd
        def _(pool):
            nc.gpsimd.memset(half[:], 0.5)
            nc.gpsimd.memset(cols[:], 0.0)
            pool.drain()
            for q, c in ((0, 0), (0, 6), (1, 3), (2, 9)):
                nc.gpsimd.memset(cols[:, :, q, c:c + 3], 1.0)
            pool.drain().then_inc(sem["consts"], 1)
            minus_half = keep["neg_half"][:, 0:units]

            def layer0_powers(g):
                pool.wait_ge(sem["var_ready"], g + 1)
                nc.gpsimd.tensor_tensor(rstd[:], var[:], minus_half, ALU.pow).then_inc(sem["rstd_ready"], 1)
                pool.wait_ge(sem["eps_ready"], g + 1)
                nc.gpsimd.tensor_tensor(norm[:], degree_eps[:], minus_half, ALU.pow).then_inc(sem["norm_ready"], 1)

            def layer1_rstd(g):
                pool.wait_ge(sem["var1_ready"], g + 1)
                nc.gpsimd.tensor_tensor(rstd[:], var[:], minus_half, ALU.pow).then_inc(sem["rstd1_ready"], 1)

            def pool_group(g, last=False):
                done = pool.snap(g * GB)
                pool.wait_ge(sem["pc_ready"], g + 1)
                nc.gpsimd.tensor_tensor(small["pn"][:], small["pc"][:], half[:], ALU.pow).then_inc(sem["pn_ready"], 1)
                nc.gpsimd.tensor_tensor(small["rpn"][:], small["pc"][:], minus_half, ALU.pow).then_inc(sem["rpn_ready"], 1)
                if not last:
                    layer0_powers(g + 1)
                for b in range(GB):
                    pool.wait_ge(sem["sigmoid_ready"], done + (b + 1))
                    nc.gpsimd.tensor_tensor(gate[:, b], gate[:, b], adjT[:, b].rearrange("p k n -> p (k n)"),
                                            ALU.mult).then_inc(sem["gated"], 1)
                for b in range(GB):
                    pool.wait_ge(sem["ln_ready"], done + (b + 1))
                    nc.gpsimd.tensor_tensor(total[:, b], pair[:, b, 0], pair[:, b, 1], ALU.add).then_inc(sem["total_ready"], 1)
                pool.wait_ge(sem["norm2_ready"], g + 1)
                nc.gpsimd.tensor_tensor(small["norm1"][:], small["norm2c"][:], half[:], ALU.pow).then_inc(sem["norm1_ready"], 1)
                if not last:
                    layer1_rstd(g + 1)

            layer0_powers(0)
            layer1_rstd(0)
            with pool.Fori(0, GROUPS - 1) as g:
                pool_group(g)
            pool_group(GROUPS - 1, last=True)

        @block.scalar
        def _(act):
            def count_signs(g):
                for u in range(units):
                    if u >= 1:
                        act.wait_ge(sem["signed"], (g * units + (u - 1)) * 2 + 2)
                    at = bass.ds(g * units + u, 1)
                    nc.scalar.activation(signs[:, 0], adj[:, u], ACT.Sign,
                                         accum_out=keep["sign_sums"][:, 0, at]).then_inc(sem["signed"], 1)
                    act.wait_ge(sem["signed"], (g * units + u) * 2 + 1)
                    nc.scalar.activation(signs[:, 1], signs[:, 0], ACT.Square,
                                         accum_out=keep["sign_sums"][:, 1, at]).then_inc(sem["signed"], 1)

            def layer0_degrees(g):
                for b in range(GB):
                    act.wait_ge(adj_in[b], g * 16 + 16)
                    for k in range(NB):
                        u = b * NB + k
                        if u >= 2:
                            act.wait_ge(sem["abs_step"], g * units + (u - 1))
                        nc.scalar.activation(junk[:, u % 2], adj[:, u], ACT.Abs,
                                             accum_out=degree[:, u:u + 1]).then_inc(sem["abs_step"], 1)
                act.wait_ge(sem["abs_step"], g * units + units)
                act.sem_inc(sem["degree_ready"], 1)

            def layer0_keep_adjT(g):
                for b in range(GB):
                    act.wait_ge(sem["adj_turned"], g * GB + (b + 1))
                    nc.scalar.activation(adjT[:, b].rearrange("p k n -> p (k n)"), ps_pair[b // 2][:, b % 2], ACT.Copy)\
                        .then_inc(sem["adjT_kept"], 1)

            def layer0_keep_sums(g):
                for b in range(GB):
                    act.wait_ge(sem["sum_made"], g * GB + (b + 1))
                    nc.scalar.activation(sumT[:, b], ps_pair[b // 2][:, b % 2, 0:N], ACT.Copy).then_inc(sem["sum_kept"], 1)

            def layer0_exp(g):
                for b in range(GB):
                    act.wait_ge(sem["z0_low_ready"], g * GB + (b + 1))
                    nc.scalar.activation(z0_low[:, of(b)], z0_low[:, of(b)], ACT.Exp).then_inc(sem["exp_ready"], 1)

            def act_group(g, last=False):
                done = act.snap(g * GB)

                def keep_rows(b):
                    act.wait_ge(sem["cols_turned"], done + (b + 1))
                    for q in range(4):
                        ins = nc.scalar.activation(rows[0:RANKS, b, q], ps_pair[b % 2][32 * q:32 * q + RANKS, 0, 0:N], ACT.Copy)
                    ins.then_inc(sem["rows_kept"], 1)

                def sigmoid(b):
                    act.wait_ge(sem["gate_made"], done + (b + 1))
                    nc.scalar.activation(gate[:, b], ps_s[b][:], ACT.Sigmoid).then_inc(sem["sigmoid_ready"], 1)

                if not last:
                    layer0_degrees(g + 1)
                for b in range(GB):
                    act.wait_ge(sem["h_turned"], done + (b + 1))
                    nc.scalar.activation(hT[:, b], ps_pair[b // 2][:, b % 2, 0:N], ACT.Copy).then_inc(sem["hT_kept"], 1)
                act.preload_act_table_set(LN_EXP_TABLES)
                act.wait_ge(sem["u_ready"], g + 1)
                nc.scalar.activation(small["ln_a"][:], small["u"][:], ACT.Ln, bias=1.0)
                nc.scalar.activation(small["ln_b"][:], small["u"][:], ACT.Ln, bias=1.0, scale=-1.0).then_inc(sem["lns_ready"], 1)
                keep_rows(0)
                keep_rows(1)
                sigmoid(0)
                keep_rows(2)
                sigmoid(1)
                keep_rows(3)
                sigmoid(2)
                sigmoid(3)
                act.preload_act_table_set(LN_EXP_TABLES)
                for b in range(GB):
                    act.wait_ge(sem["pair_clamped"], done + (b + 1))
                    nc.scalar.activation(pair[:, b], pair[:, b], ACT.Ln).then_inc(sem["ln_ready"], 1)
                if not last:
                    act.wait_ge(sem["gated"], done + GB)
                    layer0_keep_adjT(g + 1)
                for b in range(GB):
                    act.wait_ge(sem["diff_ready"], done + (b + 1))
                    nc.scalar.activation(diff[:, b], diff[:, b], ACT.Exp, scale=0.5).then_inc(sem["s_ready"], 1)
                    act.wait_ge(sem["total_ready"], done + (b + 1))
                    nc.scalar.activation(total[:, b], total[:, b], ACT.Exp, scale=-0.5).then_inc(sem["coef_ready"], 1)
                for b in range(GB):
                    act.wait_ge(sem["u_clipped"], done + (b + 1))
                    act.wait_ge(sem["total_ready"], done + (b + 1))
                    nc.scalar.activation(pair[:, b, 0], diff[:, b], ACT.Ln, bias=1.0)
                    nc.scalar.activation(pair[:, b, 1], diff[:, b], ACT.Ln, bias=1.0, scale=-1.0)\
                        .then_inc(sem["artanh_ready"], 1)
                if not last:
                    layer0_keep_sums(g + 1)
                    layer0_exp(g + 1)
                    count_signs(g + 1)
                act.wait_ge(sem["targ_ready"], g + 1)
                nc.scalar.activation(small["th"][:], small["targ"][:], ACT.Tanh).then_inc(sem["th_ready"], 1)

            layer0_degrees(0)
            count_signs(0)
            layer0_keep_adjT(0)
            layer0_keep_sums(0)
            layer0_exp(0)
            with act.Fori(0, GROUPS - 1) as g:
                act_group(g)
            act_group(GROUPS - 1, last=True)

        @block.tensor
        def _(pe):
            pe.wait_ge(sem["consts"], 1)

            def layer0_turn(g):
                for b in range(GB):
                    pe.wait_ge(adj_in[b], g * 16 + 16)
                    for ki in range(NB):
                        for kj in range(NB):
                            ins = nc.tensor.transpose(ps_pair[b // 2][:, b % 2, kj * N + ki * P:kj * N + (ki + 1) * P],
                                                      adj[:, b * NB + ki, kj * P:(kj + 1) * P], ident[:])
                    ins.then_inc(sem["adj_turned"], 1)

            def layer0_products(g):
                done = pe.snap(g * GB)
                for b in range(GB):
                    pe.wait_ge(sem["adjT_kept"], done + (b + 1))
                    pe.wait_ge(sem["hn_ready"], done + (b + 1))
                    for k in range(NB):
                        ins = nc.tensor.matmul(ps_pair[b // 2][:, b % 2, 0:N], hn[:, b * NB + k], adjT[:, b, k],
                                               start=k == 0, stop=k == NB - 1)
                    ins.then_inc(sem["sum_made"], 1)
                for b in range(GB):
                    pe.wait_ge(sem["sum_kept"], done + (b + 1))
                    for k in range(NB):
                        ins = nc.tensor.matmul(ps_pair[b // 2][:, b % 2, N + k * P:N + (k + 1) * P],
                                               sumT[:, b, k * P:(k + 1) * P], keep["W0"][:], start=True, stop=True)
                    ins.then_inc(sem["out_made"], 1)

            def pe_group(g, last=False):
                done = pe.snap(g * GB)
                for b in range(GB):
                    pe.wait_ge(sem["h_ready"], done + (b + 1))
                    for k in range(NB):
                        ins = nc.tensor.transpose(ps_pair[b // 2][:, b % 2, k * P:(k + 1) * P], h[:, b * NB + k, 0:D], ident[:])
                    ins.then_inc(sem["h_turned"], 1)
                for b in range(GB):
                    pe.wait_ge(sem["hT_kept"], done + (b + 1))
                    for k in range(NB):
                        u = b * NB + k
                        ins = nc.tensor.matmul(ps_gate[0][:, 2 * u:2 * u + 2], hT[:, b, k * P:(k + 1) * P],
                                               keep["att2"][:], start=True, stop=True)
                ins.then_inc(sem["lr_made"], 1)
                pe.wait_ge(sem["cols_ready"], g + 1)
                pe.wait_ge(sem["hT_m2_kept"], done + GB)

                def turn_cols(b):
                    for k in range(NB):
                        ins = nc.tensor.transpose(ps_pair[b % 2][:, 0, k * P:(k + 1) * P],
                                                  cols[:, b * NB + k].rearrange("p q c -> p (q c)"), ident[:])
                    ins.then_inc(sem["cols_turned"], 1)

                turn_cols(0)
                turn_cols(1)
                for b in range(GB):
                    pe.wait_ge(sem["rows_kept"], done + (b + 1))
                    right = rows[0:RANKS, b, 0]
                    for kj in range(NB):
                        ins = nc.tensor.matmul(ps_s[b][:, kj * N:(kj + 1) * N], rows[0:RANKS, b, 2, kj * P:(kj + 1) * P],
                                               right, start=True, stop=True)
                    ins.then_inc(sem["gate_made"], 1)
                    for kj in range(NB):
                        out = ps_pair[b % 2][:, 0, kj * N:(kj + 1) * N]
                        nc.tensor.matmul(out, hT_m2[:, b, kj * P:(kj + 1) * P], hT[:, b], start=True, stop=False)
                        nc.tensor.matmul(out, rows[0:RANKS, b, 1, kj * P:(kj + 1) * P], right, start=False, stop=True)
                        ins = nc.tensor.matmul(ps_pair[b % 2][:, 1, kj * N:(kj + 1) * N],
                                               rows[0:RANKS, b, 3, kj * P:(kj + 1) * P], right, start=True, stop=True)
                    ins.then_inc(sem["pair_made"], 1)
                    if b + 2 < GB:
                        pe.wait_ge(sem["pair_read"], done + (b + 1))
                        turn_cols(b + 2)
                if not last:
                    pe.wait_ge(sem["pair_read"], done + GB)
                    layer0_turn(g + 1)
                    layer0_products(g + 1)
                pe.wait_ge(sem["sigmoid_ready"], done + GB)
                for b in range(GB):
                    pe.wait_ge(sem["c_ready"], done + (b + 1))
                    for ki in range(NB):
                        for kj in range(NB):
                            ins = nc.tensor.matmul(ps_s[b][:, ki * (D + 1):(ki + 1) * (D + 1)],
                                                   pair[:, b, 0, kj * N + ki * P:kj * N + (ki + 1) * P],
                                                   h[:, b * NB + kj], start=kj == 0, stop=kj == NB - 1)
                    ins.then_inc(sem["s_made"], 1)

            layer0_turn(0)
            layer0_products(0)
            with pe.Fori(0, GROUPS - 1) as g:
                pe_group(g)
            pe_group(GROUPS - 1, last=True)

        @block.vector
        def _(dve):
            v = nc.vector
            dve.wait_ge(sem["consts"], 1)
            sm = {n: t[:] for n, t in small.items()}

            def split(first):
                two = slice(first, first + 2)
                for t in range(3):
                    v.tensor_copy(part[:, t, two], whole[:, two])
                    dve.drain()
                    if t < 2:
                        v.tensor_tensor(whole[:, two], whole[:, two], part[:, t, two], ALU.subtract)
                        dve.drain()

            def layernorm_sums(xg, then):
                for u in range(units):
                    v.bn_stats(stats[:, u], xg[:, u])
                dve.drain()
                for u in range(units):
                    v.bn_aggr(mv[:, u], stats[:, u])
                dve.drain()
                v.tensor_scalar(var[:], mv[:, :, 1], LN_EPS, None, ALU.add).then_inc(then, 1)

            def nodes(g):
                return x[:, bass.ds(g * GB, GB)].rearrange("p b k d -> p (b k) d")

            def layer0_stats(g):
                dve.wait_ge(x_in, g * 16 + 16)
                layernorm_sums(nodes(g), sem["var_ready"])

            def layer0_normed(g):
                dve.wait_ge(sem["degree_ready"], g + 1)
                v.tensor_scalar(degree_eps[:], degree[:], L0_EPS, None, ALU.add).then_inc(sem["eps_ready"], 1)
                dve.wait_ge(sem["rstd_ready"], g + 1)
                xg = nodes(g)
                for u in range(units):
                    v.tensor_scalar(normed[:, u], xg[:, u], mv[:, u, 0:1], rstd[:, u:u + 1], ALU.subtract, ALU.mult)
                dve.drain()

            def layer0_scaled(g):
                dve.wait_ge(sem["norm_ready"], g + 1)
                for b in range(GB):
                    for u in range(b * NB, (b + 1) * NB):
                        ins = v.tensor_scalar(hn[:, u], normed[:, u], 0.0, norm[:, u:u + 1], ALU.max, ALU.mult)
                    ins.then_inc(sem["hn_ready"], 1)

            def layer0_z(g):
                for b in range(GB):
                    dve.wait_ge(sem["out_made"], g * GB + (b + 1))
                    for k in range(NB):
                        u = b * NB + k
                        v.scalar_tensor_tensor(z0[:, u], ps_pair[b // 2][:, b % 2, N + k * P:N + (k + 1) * P],
                                               norm[:, u:u + 1], bc["L0_gnn_b"][:], ALU.mult, ALU.add)
                dve.drain()
                for b in range(GB):
                    v.tensor_scalar(z0_low[:, of(b)], z0[:, of(b)], 0.0, None, ALU.min).then_inc(sem["z0_low_ready"], 1)
                v.scalar_tensor_tensor(normed[:], z0[:], 0.0, nodes(g), ALU.max, ALU.add)
                dve.drain()

            def layer0_finish(g):
                xg = nodes(g)
                for b in range(GB):
                    dve.wait_ge(sem["exp_ready"], g * GB + (b + 1))
                    v.scalar_tensor_tensor(xg[:, of(b)], z0_low[:, of(b)], -1.0, normed[:, of(b)], ALU.add, ALU.add)\
                        .then_inc(sem["x_ready"], 1)
                dve.wait_ge(sem["x_ready"], g * GB + GB)
                dve.sem_inc(keep["held"], 1)
                layernorm_sums(xg, sem["var1_ready"])

            def dve_group(g, last=False):
                done = dve.snap(g * GB)
                xg = nodes(g)
                dve.wait_ge(sem["rstd1_ready"], g + 1)
                for u in range(units):
                    v.tensor_scalar(normed[:, u], xg[:, u], mv[:, u, 0:1], rstd[:, u:u + 1], ALU.subtract, ALU.mult)
                dve.drain()
                for b in range(GB):
                    v.tensor_scalar(h[:, of(b), 0:D], normed[:, of(b)], 0.0, None, ALU.max).then_inc(sem["h_ready"], 1)
                for u in range(units):
                    v.scalar_tensor_tensor(scratch[:, u], normed[:, u], 0.0, normed[:, u], ALU.max, ALU.mult,
                                           accum_out=small["p"][:, u:u + 1])
                dve.drain()
                v.tensor_scalar(sm["pc"], sm["p"], MIN_NORM, None, ALU.max).then_inc(sem["pc_ready"], 1)
                v.tensor_scalar(h[:, :, D], sm["p"], 1.0, None, ALU.add)
                v.tensor_scalar(sm["b1"], sm["p"], -1.0, 1.0, ALU.mult, ALU.add)
                v.tensor_copy(whole[:, 0], sm["p"])
                dve.drain()
                v.tensor_scalar(sm["lam"], sm["b1"], MIN_NORM, None, ALU.max)
                v.tensor_copy(whole[:, 1], sm["b1"])
                dve.drain()
                split(0)
                p_parts, c_parts = part[:, :, 0].rearrange("p t u -> p u t"), part[:, :, 1]
                v.tensor_copy(cols[:, :, 0, 3:6], p_parts)
                v.tensor_copy(cols[:, :, 1, 0:3], p_parts)
                v.tensor_copy(cols[:, :, 0, 12:21].rearrange("p u (a t) -> p u a t", a=3),
                              c_parts.rearrange("p t (u a) -> p u a t", a=1).broadcast_to((P, units, 3, 3)))
                v.tensor_copy(cols[:, :, 3, 12:21].rearrange("p u (t a) -> p u t a", a=3),
                              c_parts.rearrange("p t (u a) -> p u t a", a=1).broadcast_to((P, units, 3, 3)))
                for b in range(GB):
                    dve.wait_ge(sem["hT_kept"], done + (b + 1))
                    v.tensor_scalar(hT_m2[:, b], hT[:, b], -2.0, None, ALU.mult).then_inc(sem["hT_m2_kept"], 1)
                dve.wait_ge(sem["pn_ready"], g + 1)
                v.tensor_scalar(sm["u"], sm["pn"], MAX_TANH, None, ALU.min).then_inc(sem["u_ready"], 1)
                dve.wait_ge(sem["lns_ready"], g + 1)
                v.tensor_tensor(sm["at"], sm["ln_a"], sm["ln_b"], ALU.subtract)
                dve.drain()
                dve.wait_ge(sem["rpn_ready"], g + 1)
                v.scalar_tensor_tensor(sm["scale"], sm["at"], 0.5, sm["rpn"], ALU.mult, ALU.mult)
                dve.drain()
                dve.wait_ge(sem["lr_made"], g + 1)
                lr = ps_gate[0][:, 0:2 * units].rearrange("p (u c) -> p u c", c=2)
                v.tensor_tensor(whole[:, 2], lr[:, :, 0], sm["scale"], ALU.mult)
                v.tensor_tensor(sm["at"], lr[:, :, 1], sm["scale"], ALU.mult)
                dve.drain()
                v.tensor_scalar(whole[:, 3], sm["at"], keep["attb"][:, 0:1], None, ALU.add)
                dve.drain()
                split(2)
                v.tensor_copy(cols[:, :, 0, 9:12], part[:, :, 2].rearrange("p t u -> p u t"))
                v.tensor_copy(cols[:, :, 2, 6:9], part[:, :, 3].rearrange("p t u -> p u t"))
                dve.drain().then_inc(sem["cols_ready"], 1)
                for b in range(GB):
                    dve.wait_ge(sem["pair_made"], done + (b + 1))
                    v.tensor_scalar(pair[:, b, 0], ps_pair[b % 2][:, 0], MIN_NORM, None, ALU.max).then_inc(sem["square_ready"], 1)
                    dve.wait_ge(sem["square_ready"], done + (b + 1))
                    v.tensor_tensor(pair[:, b, 1], pair[:, b, 0], ps_pair[b % 2][:, 1],
                                    ALU.add).then_inc(sem["pair_read"], 1)
                    if not last and b < 3:
                        (layer0_stats, layer0_normed, layer0_scaled)[b](g + 1)
                    dve.wait_ge(sem["pair_read"], done + (b + 1))
                    v.tensor_scalar(pair[:, b, 1], pair[:, b, 1], MIN_NORM, None, ALU.max).then_inc(sem["pair_clamped"], 1)
                for b in range(GB):
                    dve.wait_ge(sem["ln_ready"], done + (b + 1))
                    v.tensor_tensor(diff[:, b], pair[:, b, 0], pair[:, b, 1], ALU.subtract).then_inc(sem["diff_ready"], 1)
                for b in range(GB):
                    dve.wait_ge(sem["s_ready"], done + (b + 1))
                    v.tensor_scalar(diff[:, b], diff[:, b], MAX_TANH, None, ALU.min).then_inc(sem["u_clipped"], 1)
                for b in range(GB):
                    dve.wait_ge(sem["artanh_ready"], done + (b + 1))
                    v.tensor_tensor(pair[:, b, 0], pair[:, b, 0], pair[:, b, 1], ALU.subtract)
                dve.drain()
                for b in range(GB):
                    dve.wait_ge(sem["coef_ready"], done + (b + 1))
                    v.scalar_tensor_tensor(total[:, b], pair[:, b, 0], 0.5, total[:, b], ALU.mult, ALU.mult)
                dve.drain()
                for b in range(GB):
                    dve.wait_ge(sem["gated"], done + (b + 1))
                    v.tensor_tensor(pair[:, b, 0], total[:, b], gate[:, b], ALU.mult).then_inc(sem["c_ready"], 1)
                if not last:
                    layer0_z(g + 1)
                for b in range(GB):
                    dve.wait_ge(sem["s_made"], done + (b + 1))
                    for k in range(NB):
                        u = b * NB + k
                        v.scalar_tensor_tensor(scratch[:, u], ps_s[b][:, k * (D + 1):k * (D + 1) + D], 1.0, h[:, u, 0:D],
                                               ALU.mult, ALU.mult, accum_out=small["dot"][:, u:u + 1])
                dve.drain()
                for b in range(GB):
                    v.scalar_tensor_tensor(small["alpha"][:, of(b)], small["dot"][:, of(b)], -2.0,
                                           ps_s[b][:, 0:NB * (D + 1)].rearrange("p (k d) -> p k d", k=NB)[:, :, D],
                                           ALU.mult, ALU.add)
                v.tensor_tensor(sm["kb"], sm["lam"], sm["b1"], ALU.mult)
                v.reciprocal(sm["rlam"], sm["lam"])
                dve.drain()
                v.tensor_tensor(sm["ka"], sm["lam"], sm["alpha"], ALU.mult)
                v.tensor_tensor(sm["hu"], sm["kb"], sm["dot"], ALU.mult)
                dve.drain()
                for u in range(units):
                    v.tensor_scalar(scratch[:, u], h[:, u, 0:D], small["ka"][:, u:u + 1], None, ALU.mult)
                v.tensor_tensor(sm["hu2"], sm["ka"], sm["p"], ALU.mult)
                dve.drain()
                for u in range(units):
                    b, k = divmod(u, NB)
                    v.scalar_tensor_tensor(tangent[:, u], ps_s[b][:, k * (D + 1):k * (D + 1) + D], small["kb"][:, u:u + 1],
                                           scratch[:, u], ALU.mult, ALU.subtract)
                dve.drain()
                for u in range(units):
                    v.scalar_tensor_tensor(scratch[:, u], tangent[:, u], 1.0, tangent[:, u], ALU.mult, ALU.mult,
                                           accum_out=small["norm2"][:, u:u + 1])
                v.tensor_tensor(sm["hu"], sm["hu"], sm["hu2"], ALU.subtract)
                dve.drain()
                v.tensor_scalar(sm["norm2c"], sm["norm2"], MIN_NORM, None, ALU.max).then_inc(sem["norm2_ready"], 1)
                if not last:
                    layer0_finish(g + 1)
                dve.wait_ge(sem["norm1_ready"], g + 1)
                v.tensor_tensor(sm["targ"], sm["norm1"], sm["rlam"], ALU.mult).then_inc(sem["targ_ready"], 1)
                v.reciprocal(sm["rnorm"], sm["norm1"])
                dve.drain()
                dve.wait_ge(sem["th_ready"], g + 1)
                v.tensor_tensor(sm["f"], sm["th"], sm["rnorm"], ALU.mult)
                dve.drain()
                v.tensor_tensor(sm["f2"], sm["f"], sm["f"], ALU.mult)
                v.scalar_tensor_tensor(sm["xy2"], sm["f"], 2.0, sm["hu"], ALU.mult, ALU.mult)
                v.tensor_tensor(sm["cu0"], sm["f"], sm["b1"], ALU.mult)
                dve.drain()
                v.tensor_tensor(sm["y2"], sm["f2"], sm["norm2"], ALU.mult)
                dve.drain()
                v.scalar_tensor_tensor(sm["num"], sm["xy2"], 1.0, sm["y2"], ALU.add, ALU.add)
                v.tensor_tensor(sm["py2"], sm["p"], sm["y2"], ALU.mult)
                dve.drain()
                v.scalar_tensor_tensor(sm["den"], sm["xy2"], 1.0, sm["py2"], ALU.add, ALU.add)
                dve.drain()
                v.tensor_scalar(sm["denc"], sm["den"], MIN_NORM, None, ALU.max)
                dve.drain()
                v.reciprocal(sm["rden"], sm["denc"])
                dve.drain()
                v.tensor_tensor(sm["ch"], sm["num"], sm["rden"], ALU.mult)
                v.tensor_tensor(sm["cu"], sm["cu0"], sm["rden"], ALU.mult)
                dve.drain()
                for u in range(units):
                    v.scalar_tensor_tensor(xg[:, u], h[:, u, 0:D], small["ch"][:, u:u + 1], xg[:, u], ALU.mult, ALU.add)
                dve.drain()
                for u in range(units):
                    ins = v.scalar_tensor_tensor(xg[:, u], tangent[:, u], small["cu"][:, u:u + 1], xg[:, u], ALU.mult, ALU.add)
                ins.then_inc(sem["group_done"], 1)
                dve.wait_ge(sem["group_done"], g + 1)
                dve.sem_inc(keep["held"], 1)

            for piece in (layer0_stats, layer0_normed, layer0_scaled, layer0_z, layer0_finish):
                piece(0)
            with dve.Fori(0, GROUPS - 1) as g:
                dve_group(g)
            dve_group(GROUPS - 1, last=True)


SLOTS = N + 8
CHUNKS = -(-SLOTS // P)
UNITS = GB * NB
HALF = UNITS // 2
BY_ACT = 6
LOWEST = -3.4028235e38


def layer2(nc, w, keep):
    with ExitStack() as stack:
        s = Scope(nc, stack, "l2_")
        x, ident, neg_half, bc = keep["x"], keep["ident"], keep["neg_half"], keep["broadcast"]
        adj = s.sb("adj", [P, UNITS, N])
        negatives = s.sb("negatives", [P, GROUPS * UNITS])
        needed = s.sb("needed", [P, GROUPS * UNITS])
        needed_p = s.sb("needed_p", [P, GROUPS])
        needed_g = s.sb("needed_g", [GROUPS, 1])
        n_slots = s.sb("n_slots", [1, GROUPS], I32)
        top = s.sb("top", [P, UNITS, 8])
        top_at = s.sb("top_at", [P, UNITS, 8], U32)
        value = s.sb("value", [P, UNITS, SLOTS])
        index = s.sb("index", [P, UNITS, CHUNKS * P])
        indexT = s.sb("indexT", [P, CHUNKS, UNITS * P], BF16)
        ident16 = s.sb("ident16", [P, P], BF16)
        zero16 = s.sb("zero16", [P, 4 * P], BF16)
        node_of = s.sb("node_of", [P, NB])
        W1c = s.sb("W1c", [P, 2, D])
        b1c = s.sb("b1c", [P, D])
        w1_sum = s.sb("w1_sum", [P, 3])
        w1_mean = s.sb("w1_mean", [P, 3])
        stats = s.sb("stats", [P, UNITS, 6])
        mv = s.sb("mv", [P, UNITS, 2])
        var = s.sb("var", [P, UNITS])
        rstd = s.sb("rstd", [P, UNITS])
        normed = s.sb("normed", [P, UNITS, D])
        upd = s.sb("upd", [P, UNITS, D])
        hT = s.sb("hT", [P, GB, N])
        m = s.sb("m", [P, UNITS, D])
        own = s.sb("own", [P, UNITS, D])
        parts = s.sb("parts", [P, UNITS, 3, D], BF16)
        spread = s.sb("spread", [P, UNITS * P], BF16)
        onehot = s.sb("onehot", [P, 2, NB, UNITS * P], BF16)
        pstats = s.sb("pstats", [P, UNITS, 6])
        dmean = s.sb("dmean", [P, UNITS])
        dmean2 = s.sb("dmean2", [P, UNITS])
        msum = s.sb("msum", [P, UNITS])
        pvar = s.sb("pvar", [P, UNITS])
        prstd = s.sb("prstd", [P, UNITS])
        z = [s.sb(f"z{i}", [P, UNITS, D]) for i in range(2)]
        msg = [s.sb(f"msg{i}", [P, UNITS, D]) for i in range(2)]
        diag = [s.sb(f"diag{i}", [P, UNITS, D]) for i in range(2)]
        aggT = s.sb("aggT", [P, GB, N])
        scaled = z[0]
        names = ("consts", "w1_ready", "needed_ready", "needed_turned", "slots_ready", "stats_ready",
                 "var_ready", "rstd_ready", "normed_ready", "h_turned", "h_kept", "m_made", "own_ready", "hi_ready",
                 "rest1_ready", "mid_ready", "rest2_ready", "parts_ready", "index_ready", "index_turned", "index_kept",
                 "spread_made", "spread_kept", "onehot_ready", "gathered", "stats_done", "pvar_ready", "prstd_ready",
                 "diag_ready", "diag2_ready", "summed", "z_made", "z_ready", "msg_ready",
                 "seeded", "bits_set", "agg_done", "agg_kept", "upd_made",
                 "upd_var_ready", "upd_rstd_ready", "upd_scaled", "upd_shifted", "x_done", "dve_step",
                 "upd_read")
        sem = {n: s.sem(n) for n in names}
        adj_in = [s.sem(f"adj_in{b}") for b in range(GB)]
        ps_spread = s.psum("ps_spread", [P, UNITS * P])
        ps_m = [s.psum(f"ps_m{i}", [P, UNITS, D]) for i in range(2)]
        ps_agg = s.psum("ps_agg", [P, GB, N])
        flat_agg = ps_agg[:].rearrange("p b n -> p (b n)")
        block = stack.enter_context(nc.Block())

        def wide(t):
            return t[:].rearrange("p (a d) -> p a d", a=1).broadcast_to((P, UNITS, D))

        @block.sync
        def _(sp):
            with sp.Fori(0, GROUPS) as g:
                done = sp.snap(g * GB)
                for b in range(GB):
                    sp.dma_start(adj[:, b * NB:(b + 1) * NB], w["adj"][bass.ds(done + b, 1)].rearrange(
                        "b (k p) j -> p (b k) j", p=P)).then_inc(adj_in[b], 16)
                sp.wait_ge(sem["index_ready"], g + 1)
                sp.sem_inc(keep["held"], 1)

        @block.gpsimd
        def _(pool):
            nc.gpsimd.memset(ident16[:], 0.0)
            nc.gpsimd.memset(zero16[:], 0.0)
            nc.gpsimd.memset(index[:], 0.0)
            nc.gpsimd.iota(node_of[:], [[P, NB]], base=0, channel_multiplier=1, allow_small_or_imprecise_dtypes=True)
            for i in range(2):
                nc.gpsimd.memset(msg[i][:], 0.0)
            pool.drain()
            nc.gpsimd.affine_select(out=ident16[:], in_=ident16[:], compare_op=ALU.not_equal, fill=1.0, base=0,
                                    pattern=[[-1, P]], channel_multiplier=1).then_inc(sem["consts"], 1)
            count = pool.alloc_register("l2_before_pool")
            pool.sem_inc(sem["diag2_ready"], 1)
            pool.sem_inc(sem["prstd_ready"], 1)
            pool.sem_inc(sem["z_ready"], 2)
            pool.reg_mov(count, 0)
            halves = neg_half[:, 0:UNITS]
            pool.wait_ge(sem["slots_ready"], 1)
            def split_m(g):
                done = pool.snap(g * GB)
                pool.wait_ge(sem["var_ready"], g + 1)
                nc.gpsimd.tensor_tensor(rstd[:], var[:], halves, ALU.pow).then_inc(sem["rstd_ready"], 1)
                for b in range(GB):
                    units = slice(b * NB, (b + 1) * NB)
                    pool.wait_ge(sem["hi_ready"], done + (b + 1))
                    nc.gpsimd.tensor_tensor(m[:, units], m[:, units], parts[:, units, 0],
                                            ALU.subtract).then_inc(sem["rest1_ready"], 1)
                    nc.gpsimd.tensor_tensor(own[:, units], own[:, units], b1c[:].rearrange(
                        "p (a d) -> p a d", a=1).broadcast_to((P, NB, D)), ALU.add).then_inc(sem["own_ready"], 1)
                for b in range(GB):
                    units = slice(b * NB, (b + 1) * NB)
                    pool.wait_ge(sem["mid_ready"], done + (b + 1))
                    pool.wait_ge(sem["rest1_ready"], done + (b + 1))
                    nc.gpsimd.tensor_tensor(m[:, units], m[:, units], parts[:, units, 1],
                                            ALU.subtract).then_inc(sem["rest2_ready"], 1)

            split_m(0)

            def pool_group(g, last=False):
                n = pool.value_load(n_slots[0:1, bass.ds(g, 1)], min_val=3, max_val=N)
                pairs = pool.snap((n + 1) // 2)
                before = pool.snap(count)

                def shift(par, steps, half):
                    units = slice(half * HALF, (half + 1) * HALF)
                    pool.wait_ge(sem["z_made"], steps * 2 + (half + 1))
                    nc.gpsimd.tensor_tensor(z[par][:, units], z[par][:, units], wide(bc["L2_gnn_be1"])[:, units],
                                            ALU.add).then_inc(sem["z_ready"], 1)

                def diagonals(par, steps, slot):
                    pool.wait_ge(sem["summed"], steps * 2 + 2)
                    for u in range(BY_ACT, UNITS):
                        ins = nc.gpsimd.tensor_tensor(diag[par][:, u], ident[:],
                                                      value[:, u, bass.ds(slot, 1)].broadcast_to((P, P)), ALU.mult)
                    ins.then_inc(sem["diag2_ready"], 1)

                def pool_step(par, step, slot, first=False):
                    if not first:
                        shift(1 - par, step, 0)
                    pool.wait_ge(sem["pvar_ready"], step + 1)
                    for half in range(2):
                        units = slice(half * HALF, (half + 1) * HALF)
                        nc.gpsimd.tensor_tensor(prstd[:, units], pvar[:, units], halves[:, units],
                                                ALU.pow).then_inc(sem["prstd_ready"], 1)
                    if not first:
                        shift(1 - par, step, 1)
                        diagonals(1 - par, step, slot - 1)

                pool_step(0, before, 0, first=True)
                pool_step(1, pool.snap(before + 1), 1)
                with pool.Fori(1, pairs) as t:
                    for par in range(2):
                        slot = pool.snap(t * 2 + par)
                        pool_step(par, pool.snap(before + slot), slot)
                pool.reg_add(count, count, pairs * 2)
                after = pool.snap(count)
                shift(1, after, 0)
                shift(1, after, 1)
                diagonals(1, after, pool.snap(pairs * 2 - 1))
                if not last:
                    split_m(g + 1)
                pool.wait_ge(sem["upd_var_ready"], g + 1)
                nc.gpsimd.tensor_tensor(rstd[:], var[:], halves, ALU.pow).then_inc(sem["upd_rstd_ready"], 1)
                pool.wait_ge(sem["upd_scaled"], g + 1)
                nc.gpsimd.tensor_tensor(scaled[:], scaled[:], wide(bc["L2_gnn_be2"]), ALU.add).then_inc(sem["upd_shifted"], 1)

            with pool.Fori(0, GROUPS - 1) as g:
                pool_group(g)
            pool_group(GROUPS - 1, last=True)

        @block.scalar
        def _(act):
            act.preload_act_table_set("gelu_and_others")
            count = act.alloc_register("l2_before_act")
            act.sem_inc(sem["msg_ready"], 6)
            act.sem_inc(sem["diag_ready"], 1)
            act.reg_mov(count, 0)

            def seed(par, half):
                units = slice(half * HALF, (half + 1) * HALF)
                nc.scalar.activation(ps_m[par][:, units], own[:, units], ACT.Copy).then_inc(sem["seeded"], 1)

            def keep_spread(g, ahead):
                act.wait_ge(sem["spread_made"], ahead + (g + 1))
                nc.scalar.activation(spread[:], ps_spread[:], ACT.Copy).then_inc(sem["spread_kept"], 1)

            def start_slots(g, before):
                first_ahead = act.snap(before + g * 2)
                for c in range(CHUNKS):
                    act.wait_ge(sem["index_turned"], g * CHUNKS + (c + 1))
                    nc.scalar.activation(indexT[:, c], flat_agg if c else ps_spread[:], ACT.Copy)\
                        .then_inc(sem["index_kept"], 1)
                    if c == 1:
                        keep_spread(g, first_ahead)
                act.wait_ge(sem["onehot_ready"], first_ahead + 1)
                keep_spread(g, first_ahead + 1)

            def split_m(g):
                done = act.snap(g * GB)
                act.wait_ge(sem["h_turned"], g + 1)
                nc.scalar.activation(hT[:], ps_m[0][:].rearrange("p (b k) d -> p b (k d)", b=GB), ACT.Relu)\
                    .then_inc(sem["h_kept"], 1)
                for b in range(GB):
                    units = slice(b * NB, (b + 1) * NB)
                    pm = ps_m[b // 2][:, (b % 2) * 4:(b % 2) * 4 + 4].rearrange("p (k t) d -> p k t d", t=2)
                    act.wait_ge(sem["m_made"], done + (b + 1))
                    nc.scalar.activation(m[:, units], pm[:, :, 0], ACT.Copy)
                    nc.scalar.activation(own[:, units], pm[:, :, 1], ACT.Copy)
                    nc.scalar.activation(parts[:, units, 0], pm[:, :, 0], ACT.Copy).then_inc(sem["hi_ready"], 1)
                for i, (wait, then) in enumerate((("rest1_ready", "mid_ready"), ("rest2_ready", "parts_ready"))):
                    for b in range(GB):
                        units = slice(b * NB, (b + 1) * NB)
                        act.wait_ge(sem[wait], done + (b + 1))
                        nc.scalar.activation(parts[:, units, i + 1], m[:, units], ACT.Copy).then_inc(sem[then], 1)
                act.wait_ge(sem["bits_set"], g + 1)
                act.wait_ge(sem["own_ready"], done + GB)
                for par in range(2):
                    seed(par, 0)
                    seed(par, 1)

            split_m(0)
            act.wait_ge(sem["slots_ready"], 1)
            start_slots(0, act.snap(count))

            def act_group(g, last=False):
                done = act.snap(g * GB)
                n = act.value_load(n_slots[0:1, bass.ds(g, 1)], min_val=3, max_val=N)
                pairs = act.snap((n + 1) // 2)
                before = act.snap(count)

                def gelu(par, steps, half):
                    units = slice(half * HALF, (half + 1) * HALF)
                    act.wait_ge(sem["z_ready"], steps * 2 + (half + 1))
                    act.wait_ge(sem["summed"], steps * 2 + (half + 1))
                    nc.scalar.activation(msg[par][:, units], z[par][:, units], ACT.Gelu).then_inc(sem["msg_ready"], 1)

                def diagonals(par, steps, slot):
                    act.wait_ge(sem["summed"], steps * 2 + 2)
                    for u in range(BY_ACT):
                        ins = nc.scalar.activation(diag[par][:, u], ident[:], ACT.Copy,
                                                   scale=value[:, u, bass.ds(slot, 1)])
                    ins.then_inc(sem["diag_ready"], 1)

                def act_step(par, step, slot, first=False, second=False):
                    ahead = act.snap(step + g * 2 + 2)
                    act.wait_ge(sem["onehot_ready"], ahead)
                    keep_spread(g, ahead)
                    if not (first or second):
                        gelu(par, act.snap(step - 1), 1)
                    if not first:
                        for half in range(2):
                            act.wait_ge(sem["z_made"], step * 2 + (half + 1))
                            seed(1 - par, half)
                        gelu(1 - par, step, 0)
                        diagonals(1 - par, step, slot - 1)

                act_step(0, before, 0, first=True)
                act_step(1, act.snap(before + 1), 1, second=True)
                with act.Fori(1, pairs) as t:
                    for par in range(2):
                        slot = act.snap(t * 2 + par)
                        act_step(par, act.snap(before + slot), slot)
                act.reg_add(count, count, pairs * 2)
                after = act.snap(count)
                gelu(0, act.snap(after - 1), 1)
                gelu(1, after, 0)
                diagonals(1, after, act.snap(pairs * 2 - 1))
                gelu(1, after, 1)
                act.wait_ge(sem["onehot_ready"], after + (g * 2 + 2))
                act.wait_ge(sem["agg_done"], g + 1)
                nc.scalar.activation(aggT[:], ps_agg[:], ACT.Copy).then_inc(sem["agg_kept"], 1)
                if not last:
                    split_m(g + 1)
                    start_slots(g + 1, after)

            with act.Fori(0, GROUPS - 1) as g:
                act_group(g)
            act_group(GROUPS - 1, last=True)

        @block.vector
        def _(dve):
            nc.vector.tensor_reduce(w1_sum[:, 0:2], keep["W1"][:], AX.X, ALU.add)
            nc.vector.tensor_reduce(w1_sum[:, 2:3], bc["L2_gnn_b1"][:], AX.X, ALU.add)
            nc.vector.memset(value[:], 0.0)
            dve.drain()
            nc.vector.tensor_scalar(w1_mean[:], w1_sum[:], 1.0 / D, None, ALU.mult)
            dve.drain()
            for t in range(2):
                nc.vector.tensor_scalar(W1c[:, t], keep["W1"][:, t], w1_mean[:, t:t + 1], None, ALU.subtract)
            nc.vector.tensor_scalar(b1c[:], bc["L2_gnn_b1"][:], w1_mean[:, 2:3], None, ALU.subtract)
            dve.drain().then_inc(sem["w1_ready"], 1)
            dve.wait_ge(sem["consts"], 1)
            sign_sums = keep["sign_sums"]
            nc.vector.tensor_tensor(negatives[:], sign_sums[:, 1], sign_sums[:, 0], ALU.subtract)
            dve.drain()
            nc.vector.scalar_tensor_tensor(needed[:], negatives[:], float(N), sign_sums[:, 0], ALU.mult, ALU.add)
            dve.drain()
            nc.vector.tensor_reduce(needed_p[:], needed[:].rearrange("p (g u) -> p g u", g=GROUPS), AX.X,
                                    ALU.max).then_inc(sem["needed_ready"], 1)
            dve.wait_ge(sem["needed_turned"], 1)
            nc.vector.tensor_reduce(needed_g[:], ps_m[0][0:GROUPS, 0, :], AX.X, ALU.max).then_inc(sem["needed_ready"], 1)
            dve.wait_ge(sem["needed_turned"], 2)
            nc.vector.tensor_scalar(n_slots[:], ps_m[1][0:1, 0, 0:GROUPS], 3.0, float(N), ALU.max, ALU.min)
            dve.drain().then_inc(sem["slots_ready"], 1)
            dve.wait_ge(sem["slots_ready"], 1)
            count = dve.alloc_register("l2_before_dve")
            dve.sem_inc(sem["z_made"], 2)
            dve.reg_mov(count, 0)

            def take_slots(g):
                for b in range(GB):
                    dve.wait_ge(adj_in[b], g * 16 + 16)
                dve.sem_inc(keep["held"], 1)
                n = dve.value_load(n_slots[0:1, bass.ds(g, 1)], min_val=3, max_val=N)
                with dve.Fori(0, ((n + 1) // 2 * 2 + 10) // 8) as r:
                    for u in range(UNITS):
                        nc.vector.max(top[:, u], adj[:, u])
                    dve.drain()
                    for u in range(UNITS):
                        nc.vector.max_index(top_at[:, u], top[:, u], adj[:, u])
                    nc.vector.tensor_copy(value[:, :, bass.ds(r * 8, 8)], top[:])
                    dve.drain()
                    for u in range(UNITS):
                        nc.vector.match_replace(adj[:, u], top[:, u], adj[:, u], LOWEST)
                    nc.vector.tensor_copy(index[:, :, bass.ds(r * 8, 8)], top_at[:])
                    dve.drain()
                dve.drain().then_inc(sem["index_ready"], 1)

            def nodes(g):
                return x[:, bass.ds(g * GB, GB)].rearrange("p b k d -> p (b k) d")

            def normalise_nodes(g):
                xg = nodes(g)
                for u in range(UNITS):
                    nc.vector.bn_stats(stats[:, u], xg[:, u])
                dve.drain()
                for u in range(UNITS):
                    nc.vector.bn_aggr(mv[:, u], stats[:, u])
                dve.drain()
                nc.vector.tensor_scalar(var[:], mv[:, :, 1], LN_EPS, None, ALU.add).then_inc(sem["var_ready"], 1)
                dve.wait_ge(sem["rstd_ready"], g + 1)
                for u in range(UNITS):
                    nc.vector.tensor_scalar(normed[:, u], xg[:, u], mv[:, u, 0:1], rstd[:, u:u + 1], ALU.subtract, ALU.mult)
                dve.drain().then_inc(sem["normed_ready"], 1)

            def pick(ahead, par):
                dve.wait_ge(sem["spread_kept"], ahead + 1)
                for k in range(NB):
                    ins = nc.vector.tensor_scalar(onehot[:, par, k], spread[:], node_of[:, k:k + 1], None, ALU.is_equal)
                ins.then_inc(sem["onehot_ready"], 1)

            normalise_nodes(0)
            take_slots(0)
            pick(dve.snap(count), 0)
            pick(dve.snap(count) + 1, 1)

            def dve_group(g, last=False):
                done = dve.snap(g * GB)
                n = dve.value_load(n_slots[0:1, bass.ds(g, 1)], min_val=3, max_val=N)
                pairs = dve.snap((n + 1) // 2)
                before = dve.snap(count)

                def normalise(par, half):
                    for u in range(half * HALF, (half + 1) * HALF):
                        ins = nc.vector.scalar_tensor_tensor(z[par][:, u], ps_m[par][:, u], prstd[:, u:u + 1],
                                                             bc["L2_gnn_g1"][:], ALU.mult, ALU.mult)
                    ins.then_inc(sem["z_made"], 1)

                def dve_step(par, step, first=False):
                    for half in range(2):
                        dve.wait_ge(sem["gathered"], (step + g) * 2 + (half + 1))
                        for u in range(half * HALF, (half + 1) * HALF):
                            ins = nc.vector.bn_stats(pstats[:, u], ps_m[par][:, u])
                        if half == 1:
                            ins.then_inc(sem["stats_done"], 1)
                        if not first:
                            dve.wait_ge(sem["prstd_ready"], step * 2 + half)
                            dve.wait_ge(sem["msg_ready"], step * 2 + (half + 1))
                            normalise(1 - par, half)
                    dve.wait_ge(sem["stats_done"], step + 1)
                    nc.vector.tensor_tensor(dmean[:], pstats[:, :, 1], pstats[:, :, 4], ALU.subtract)
                    nc.vector.scalar_tensor_tensor(msum[:], pstats[:, :, 2], D * LN_EPS, pstats[:, :, 5],
                                                   ALU.add, ALU.add).then_inc(sem["dve_step"], 1)
                    dve.wait_ge(sem["dve_step"], step * 2 + 1)
                    nc.vector.scalar_tensor_tensor(dmean2[:], dmean[:], 0.25, dmean[:], ALU.mult,
                                                   ALU.mult).then_inc(sem["dve_step"], 1)
                    dve.wait_ge(sem["dve_step"], step * 2 + 2)
                    nc.vector.scalar_tensor_tensor(pvar[:], msum[:], 1.0 / D, dmean2[:], ALU.mult,
                                                   ALU.add).then_inc(sem["pvar_ready"], 1)
                    pick(dve.snap(step + g * 2 + 2), par)

                dve_step(0, before, first=True)
                dve_step(1, dve.snap(before + 1))
                with dve.Fori(1, pairs) as t:
                    for par in range(2):
                        dve_step(par, dve.snap(before + (t * 2 + par)))
                dve.reg_add(count, count, pairs * 2)
                after = dve.snap(count)
                dve.wait_ge(sem["gathered"], (after + g) * 2 + 2)
                for half in range(2):
                    dve.wait_ge(sem["prstd_ready"], after * 2 + half)
                    dve.wait_ge(sem["msg_ready"], after * 2 + (half + 1))
                    normalise(1, half)
                if not last:
                    normalise_nodes(g + 1)
                    dve.wait_ge(sem["diag_ready"], after + 1)
                    dve.wait_ge(sem["diag2_ready"], after + 1)
                    take_slots(g + 1)
                if not last:
                    dve.wait_ge(sem["h_turned"], g + 2)
                first_ahead = dve.snap(after + (g + 1) * 2)
                xg = nodes(g)
                dve.wait_ge(sem["upd_made"], g + 1)
                nc.vector.tensor_tensor(upd[:], flat_agg.rearrange("p (u d) -> p u d", u=UNITS), wide(bc["L2_gnn_b2"]),
                                        ALU.add).then_inc(sem["upd_read"], 1)
                dve.drain()
                for u in range(UNITS):
                    nc.vector.bn_stats(stats[:, u], upd[:, u])
                dve.drain()
                for u in range(UNITS):
                    nc.vector.bn_aggr(mv[:, u], stats[:, u])
                dve.drain()
                nc.vector.tensor_scalar(var[:], mv[:, :, 1], LN_EPS, None, ALU.add).then_inc(sem["upd_var_ready"], 1)
                if not last:
                    pick(first_ahead, 0)
                dve.wait_ge(sem["upd_rstd_ready"], g + 1)
                for u in range(UNITS):
                    nc.vector.tensor_scalar(normed[:, u], upd[:, u], mv[:, u, 0:1], rstd[:, u:u + 1], ALU.subtract, ALU.mult)
                dve.drain()
                nc.vector.tensor_tensor(scaled[:], normed[:], wide(bc["L2_gnn_g2"]), ALU.mult).then_inc(sem["upd_scaled"], 1)
                if not last:
                    pick(first_ahead + 1, 1)
                dve.wait_ge(sem["upd_shifted"], g + 1)
                nc.vector.tensor_tensor(xg, xg, scaled[:], ALU.add).then_inc(sem["x_done"], 1)
                dve.wait_ge(sem["x_done"], g + 1)
                dve.sem_inc(keep["held"], 1)

            with dve.Fori(0, GROUPS - 1) as g:
                dve_group(g)
            dve_group(GROUPS - 1, last=True)

        @block.tensor
        def _(pe):
            pe.wait_ge(sem["consts"], 1)
            pe.wait_ge(sem["w1_ready"], 1)
            count = pe.alloc_register("l2_before_pe")
            pe.sem_inc(sem["summed"], 6)
            pe.reg_mov(count, 0)

            def spread_out(slot):
                for c in range(2):
                    ins = nc.tensor.matmul(ps_spread[:, c * 512:(c + 1) * 512],
                                           ident16[:, bass.ds(slot % P, 1)].broadcast_to((P, P)),
                                           indexT[:, bass.ds(slot // P, 1), c * 512:(c + 1) * 512].rearrange("p a n -> p (a n)"),
                                           start=True, stop=True)
                ins.then_inc(sem["spread_made"], 1)

            def start_slots(g, before, first=False):
                first_ahead = pe.snap(before + g * 2)
                if not first:
                    pe.wait_ge(sem["spread_kept"], first_ahead)
                    pe.wait_ge(sem["spread_made"], first_ahead + g)
                pe.wait_ge(sem["index_ready"], g + 1)
                for c in range(CHUNKS):
                    if c == 1 and not first:
                        pe.wait_ge(sem["upd_read"], g)
                    if c > 1:
                        pe.wait_ge(sem["index_kept"], g * CHUNKS + c)
                    for u in range(UNITS):
                        ins = nc.tensor.transpose((flat_agg if c else ps_spread)[:, u * P:(u + 1) * P],
                                                  index[:, u, c * P:(c + 1) * P], ident[:])
                    ins.then_inc(sem["index_turned"], 1)
                    if c == 1:
                        pe.wait_ge(sem["index_kept"], g * CHUNKS + 1)
                        spread_out(0)
                pe.wait_ge(sem["spread_kept"], first_ahead + 1)
                spread_out(1)
                pe.wait_ge(sem["index_kept"], g * CHUNKS + CHUNKS)

            pe.wait_ge(sem["needed_ready"], 1)
            nc.tensor.transpose(ps_m[0][0:GROUPS, 0, :], needed_p[:], ident[:]).then_inc(sem["needed_turned"], 1)
            pe.wait_ge(sem["needed_ready"], 2)
            nc.tensor.transpose(ps_m[1][0:1, 0, 0:GROUPS], needed_g[:], ident[0:GROUPS, 0:GROUPS]).then_inc(sem["needed_turned"], 1)
            pe.wait_ge(sem["slots_ready"], 1)

            def make_m(g):
                pe.wait_ge(sem["normed_ready"], g + 1)
                for u in range(UNITS):
                    ins = nc.tensor.transpose(ps_m[0][:, u], normed[:, u], ident[:])
                ins.then_inc(sem["h_turned"], 1)
                pe.wait_ge(sem["h_kept"], g + 1)
                for b in range(GB):
                    for k in range(NB):
                        lane = (b % 2) * 4 + 2 * k
                        ins = nc.tensor.matmul(ps_m[b // 2][:, lane:lane + 2], hT[:, b, k * P:(k + 1) * P], W1c[:],
                                               start=True, stop=True)
                    ins.then_inc(sem["m_made"], 1)
                pe.wait_ge(sem["hi_ready"], g * GB + GB)
                for i in range(2):
                    for c in range(2):
                        ins = nc.tensor.matmul(ps_m[i][:, c * HALF:(c + 1) * HALF], zero16[:, 0:P], zero16[:],
                                               start=True, stop=False, skip_group_check=True)
                ins.then_inc(sem["bits_set"], 1)

            make_m(0)
            start_slots(0, pe.snap(count), first=True)

            def pe_group(g, last=False):
                for b in range(2):
                    nc.tensor.matmul(ps_agg[:].rearrange("p (c b) n -> p c (b n)", c=2)[:, b], zero16[:, 0:P], zero16[:],
                                     start=True, stop=False, skip_group_check=True)
                pe.sem_inc(keep["held"], 1)
                n = pe.value_load(n_slots[0:1, bass.ds(g, 1)], min_val=3, max_val=N)
                pairs = pe.snap((n + 1) // 2)
                before = pe.snap(count)

                def gather(par, number, half):
                    pe.wait_ge(sem["seeded"], number * 2 + (half + 1))
                    for u in range(half * HALF, (half + 1) * HALF):
                        b = u // NB
                        for k in range(NB):
                            for t in range(3):
                                ins = nc.tensor.matmul(ps_m[par][:, u], onehot[:, par, k, u * P:(u + 1) * P],
                                                       parts[:, b * NB + k, t], start=False, stop=False,
                                                       skip_group_check=True)
                    ins.then_inc(sem["gathered"], 1)

                def aggregate(par, steps, half):
                    pe.wait_ge(sem["msg_ready"], steps * 2 + (half + 5))
                    pe.wait_ge(sem["diag_ready"], steps + 1)
                    if half == 1:
                        pe.wait_ge(sem["diag2_ready"], steps + 1)
                    for u in range(half * HALF, (half + 1) * HALF):
                        ins = nc.tensor.matmul(ps_agg[:, u // NB, (u % NB) * P:(u % NB + 1) * P], msg[par][:, u], diag[par][:, u],
                                               start=False, stop=False, skip_group_check=True)
                    ins.then_inc(sem["summed"], 1)

                first_ahead = pe.snap(before + g * 2)
                pe.wait_ge(sem["parts_ready"], g * GB + GB)
                pe.wait_ge(sem["onehot_ready"], first_ahead + 1)
                for half in range(2):
                    gather(0, pe.snap(before + g), half)
                pe.wait_ge(sem["spread_kept"], first_ahead + 2)
                spread_out(2)

                def pe_step(par, step, slot, first=False, second=False):
                    ahead = pe.snap(step + g * 2 + 2)
                    pe.wait_ge(sem["onehot_ready"], ahead)
                    gather(1 - par, pe.snap(step + g + 1), 0)
                    pe.wait_ge(sem["spread_kept"], ahead + 1)
                    spread_out(slot + 3)
                    gather(1 - par, pe.snap(step + g + 1), 1)
                    if not (first or second):
                        for half in range(2):
                            aggregate(par, pe.snap(step - 1), half)

                pe_step(0, before, 0, first=True)
                pe_step(1, pe.snap(before + 1), 1, second=True)
                with pe.Fori(1, pairs) as t:
                    for par in range(2):
                        slot = pe.snap(t * 2 + par)
                        pe_step(par, pe.snap(before + slot), slot)
                pe.reg_add(count, count, pairs * 2)
                after = pe.snap(count)
                for par in range(2):
                    for half in range(2):
                        aggregate(par, pe.snap(after + par - 1), half)
                for b in range(2):
                    ins = nc.tensor.matmul(ps_agg[:].rearrange("p (c b) n -> p c (b n)", c=2)[:, b], zero16[:, 0:P], zero16[:],
                                           start=False, stop=True, skip_group_check=True)
                ins.then_inc(sem["agg_done"], 1)
                pe.wait_ge(sem["agg_kept"], g + 1)
                for u in range(UNITS):
                    b, k = divmod(u, NB)
                    nc.tensor.matmul(flat_agg[:, u * P:(u + 1) * P], hT[:, b, k * P:(k + 1) * P], keep["W2"][:, 0],
                                     start=True, stop=False)
                    ins = nc.tensor.matmul(flat_agg[:, u * P:(u + 1) * P], aggT[:, b, k * P:(k + 1) * P], keep["W2"][:, 1],
                                           start=False, stop=True)
                ins.then_inc(sem["upd_made"], 1)
                if not last:
                    make_m(g + 1)
                    start_slots(g + 1, after)

            with pe.Fori(0, GROUPS - 1) as g:
                pe_group(g)
            pe_group(GROUPS - 1, last=True)



def layer3(nc, w, keep, out):
    with ExitStack() as stack:
        s = Scope(nc, stack, "l3_")
        x, ident, neg_half = keep["x"], keep["ident"], keep["neg_half"]
        adj = s.sb("adj", [P, GB, NB, N])
        adjT = s.sb("adjT", [P, GB, NB, N])
        rowT = s.sb("rowT", [P, 2, GB, NB, N])
        colA = s.sb("colA", [P, 2, GB, NB, N])
        junk = s.sb("junk", [P, GB, 2, N])
        sums = s.sb("sums", [P, GB, 2, NB])
        clamped = s.sb("clamped", [P, GB, 2, NB])
        inv = s.sb("inv", [P, GB, 2, NB])
        stats = s.sb("stats", [P, GB, NB, 6])
        mv = s.sb("mv", [P, GB, NB, 2])
        var = s.sb("var", [P, GB, NB])
        rstd = s.sb("rstd", [P, GB, NB])
        normed = s.sb("normed", [P, GB, NB, D])
        h = s.sb("h", [P, GB, NB, D])
        fT = s.sb("fT", [P, GB, 5, N])
        sd = s.sb("sd", [P, GB, NB, 2 * D])
        xout = s.sb("xout", [P, GB, NB, D])
        names = ("summed", "clamped", "inv_ready", "stats_ready", "mv_ready", "var_ready", "rstd_ready",
                 "normed_ready", "h_ready", "adj_turned", "adjT_kept", "norms_spread", "scaled", "h_turned",
                 "h_kept", "sd_made", "sd_kept", "f_made", "f_kept", "f_turned", "x_ready", "col_squared",
                 "row_squared")
        sem = {n: s.sem(n) for n in names}
        adj_in = [s.sem(f"adj_in{b}") for b in range(GB)]
        x_stored = [s.sem(f"x_stored{b}") for b in range(GB)]
        ps_adj = [s.psum(f"ps_adj{i}", [P, NB, N]) for i in range(2)]
        ps_sd = [s.psum(f"ps_sd{i}", [P, NB, N]) for i in range(2)]
        ps_turn = [s.psum(f"ps_turn{i}", [P, NB, N]) for i in range(2)]
        ps_f = [s.psum(f"ps_f{i}", [P, 512]) for i in range(2)]
        ps_ahead = ps_adj + ps_turn
        block = stack.enter_context(nc.Block())


        @block.sync
        def _(sp):
            def load(g, b):
                sp.dma_start(adj[:, b], w["adj"][bass.ds(g * GB + b, 1)].rearrange(
                    "b (k p) j -> p (b k) j", p=P)).then_inc(adj_in[b], 16)

            def store(g):
                for b in range(GB):
                    sp.wait_ge(sem["x_ready"], g * GB + (b + 1))
                    sp.dma_start(out[bass.ds(g * GB + b, 1)].rearrange("b (k p) d -> p (b k) d", p=P),
                                 xout[:, b]).then_inc(x_stored[b], 16)

            for b in range(GB):
                load(0, b)
            with sp.Fori(0, GROUPS - 1) as g:
                for b in range(GB):
                    sp.wait_ge(sem["scaled"], g * GB + (b + 1))
                    sp.sem_inc(keep["held"], 1)
                    load(g + 1, b)
                store(g)
            store(GROUPS - 1)
            for b in range(GB):
                sp.wait_ge(x_stored[b], 16 * GROUPS)

        @block.gpsimd
        def _(pool):
            with pool.Fori(0, GROUPS) as g:
                done = pool.snap(g * GB)
                for b in range(GB):
                    pool.wait_ge(sem["clamped"], done + (b + 1))
                    nc.gpsimd.tensor_tensor(inv[:, b], clamped[:, b], neg_half[:, 0:2 * NB].rearrange(
                        "p (a k) -> p a k", a=2), ALU.pow).then_inc(sem["inv_ready"], 1)
                pool.wait_ge(sem["mv_ready"], (done + GB))
                pool.sem_inc(keep["held"], 1)
                nc.gpsimd.tensor_scalar(var[:], mv[:, :, :, 1], LN_EPS, 1.0, ALU.add, ALU.mult).then_inc(sem["var_ready"], 1)
                pool.wait_ge(sem["var_ready"], g + 1)
                nc.gpsimd.tensor_tensor(rstd[:], var[:], neg_half[:, 0:GB * NB].rearrange("p (b k) -> p b k", b=GB),
                                        ALU.pow).then_inc(sem["rstd_ready"], 1)

        @block.vector
        def _(dve):
            def nodes(g, b, k):
                return x[:, bass.ds(g * GB + b, 1), k].rearrange("p a d -> p (a d)")

            def prepare_stats(g, b):
                for k in range(NB):
                    ins = nc.vector.bn_stats(stats[:, b, k], nodes(g, b, k))
                ins.then_inc(sem["stats_ready"], 1)

            def prepare_mv(g, b):
                dve.wait_ge(sem["stats_ready"], g * GB + (b + 1))
                dve.sem_inc(keep["held"], 1)
                for k in range(NB):
                    ins = nc.vector.bn_aggr(mv[:, b, k], stats[:, b, k])
                ins.then_inc(sem["mv_ready"], 1)

            def prepare_norms(g, b):
                dve.wait_ge(sem["summed"], g * GB + (b + 1))
                nc.vector.tensor_scalar(clamped[:, b], sums[:, b], 1e-24, None, ALU.max).then_inc(sem["clamped"], 1)

            def prepare_scaled(g, b):
                dve.wait_ge(sem["norms_spread"], g * GB + (b + 1))
                dve.wait_ge(adj_in[b], g * 16 + 16)
                parity = bass.ds(g % 2, 1)
                for q, (dst, src) in enumerate(((rowT, adjT), (colA, adj))):
                    norms = ps_ahead[b][:, q].rearrange("p (a n) -> p a n", a=1).broadcast_to((P, NB, N))
                    ins = nc.vector.tensor_tensor(dst[:, parity, b].rearrange("p a k n -> p (a k) n"), src[:, b], norms, ALU.mult)
                ins.then_inc(sem["scaled"], 1)

            def prepare_normed(g, b):
                if b == 0:
                    dve.wait_ge(sem["rstd_ready"], g + 1)
                for k in range(NB):
                    ins = nc.vector.tensor_scalar(normed[:, b, k], nodes(g, b, k), mv[:, b, k, 0:1],
                                                  rstd[:, b, k:k + 1], ALU.subtract, ALU.mult)
                ins.then_inc(sem["normed_ready"], 1)

            def prepare_h(g, b):
                dve.wait_ge(sem["normed_ready"], g * GB + (b + 1))
                nc.vector.tensor_scalar(h[:, b], normed[:, b], 0.0, None, ALU.max).then_inc(sem["h_ready"], 1)

            for step in (prepare_stats, prepare_mv, prepare_norms, prepare_scaled, prepare_normed, prepare_h):
                for b in range(GB):
                    step(0, b)

            def dve_group(g, last=False):
                steps = {1: (prepare_stats,), 2: (prepare_mv, prepare_norms), 3: (prepare_normed, prepare_scaled, prepare_h)}
                for l in range(4):
                    for b in range(GB):
                        n = g * (4 * GB) + (l * GB + b + 1)
                        dve.wait_ge(sem["sd_made"], n)
                        nc.vector.tensor_tensor(sd[:, b], ps_sd[b % 2][:],
                                                keep["l3_bsd"][:, l:l + 1, :].broadcast_to((P, NB, 2 * D)),
                                                ALU.add).then_inc(sem["sd_kept"], 1)
                        if not last and l:
                            for step in steps[l]:
                                step(g + 1, b)
                for b in range(GB):
                    dve.wait_ge(sem["f_turned"], g * GB + (b + 1))
                    nc.vector.tensor_tensor(xout[:, b], x[:, bass.ds(g * GB + b, 1)].rearrange("p a k d -> p (a k) d"),
                                            ps_turn[b % 2][:, 0, :].rearrange("p (k d) -> p k d", k=NB),
                                            ALU.add).then_inc(sem["x_ready"], 1)
                for b in range(GB):
                    dve.wait_ge(x_stored[b], g * 16 + 16)

            with dve.Fori(0, GROUPS - 1) as g:
                dve_group(g)
            dve_group(GROUPS - 1, last=True)

        @block.scalar
        def _(act):
            def prepare_squares(g, b):
                act.wait_ge(adj_in[b], g * 16 + 16)
                for k in range(NB):
                    ins = nc.scalar.activation(junk[:, b, 0], adj[:, b, k], ACT.Square, accum_out=sums[:, b, 0, k:k + 1])
                    ins.then_inc(sem["row_squared"], 1)
                    act.wait_ge(sem["row_squared"], g * (GB * NB) + (b * NB + k + 1))
                act.wait_ge(sem["adj_turned"], g * GB + (b + 1))
                for k in range(NB):
                    ins = nc.scalar.activation(junk[:, b, 1], ps_ahead[b][:, k], ACT.Square,
                                               accum_out=sums[:, b, 1, k:k + 1])
                    if k < NB - 1:
                        ins.then_inc(sem["col_squared"], 1)
                        act.wait_ge(sem["col_squared"], g * (GB * (NB - 1)) + (b * (NB - 1) + k + 1))
                ins.then_inc(sem["summed"], 1)
                nc.scalar.activation(adjT[:, b], ps_ahead[b][:], ACT.Copy).then_inc(sem["adjT_kept"], 1)

            for b in range(GB):
                prepare_squares(0, b)

            def act_group(g, last=False):
                for b in range(GB):
                    act.wait_ge(sem["h_turned"], g * GB + (b + 1))
                    nc.scalar.activation(fT[:, b, 0], ps_f[b % 2][:, 0:N], ACT.Copy).then_inc(sem["h_kept"], 1)
                for l in range(4):
                    for b in range(GB):
                        act.wait_ge(sem["f_made"], g * (4 * GB) + (l * GB + b + 1))
                        nc.scalar.activation(fT[:, b, l + 1], ps_f[b % 2][:, 0:N], ACT.Tanh,
                                             bias=keep["l3_c"][:, l:l + 1]).then_inc(sem["f_kept"], 1)
                        if not last and l == 1:
                            prepare_squares(g + 1, b)

            with act.Fori(0, GROUPS - 1) as g:
                act_group(g)
            act_group(GROUPS - 1, last=True)

        @block.tensor
        def _(pe):
            def turn(dst, src, last_sem):
                for kr in range(NB):
                    for kc in range(NB):
                        ins = nc.tensor.transpose(dst[:, kc, kr * P:(kr + 1) * P], src[:, kr, kc * P:(kc + 1) * P], ident[:])
                ins.then_inc(last_sem, 1)

            def prepare_turned(g, b):
                pe.wait_ge(adj_in[b], g * 16 + 16)
                turn(ps_ahead[b], adj[:, b], sem["adj_turned"])

            def prepare_norms(g, b):
                pe.wait_ge(sem["adjT_kept"], g * GB + (b + 1))
                pe.wait_ge(sem["inv_ready"], g * GB + (b + 1))
                for q in range(2):
                    for k in range(NB):
                        ins = nc.tensor.transpose(ps_ahead[b][:, q, k * P:(k + 1) * P],
                                                  inv[:, b, q, k:k + 1].broadcast_to((P, P)), ident[:])
                ins.then_inc(sem["norms_spread"], 1)

            def prepare_input(g):
                for b in range(GB):
                    pe.wait_ge(sem["h_ready"], g * GB + (b + 1))
                    if b >= 2:
                        pe.wait_ge(sem["h_kept"], g * GB + (b - 1))
                    for k in range(NB):
                        ins = nc.tensor.transpose(ps_f[b % 2][:, k * P:(k + 1) * P], h[:, b, k], ident[:])
                    ins.then_inc(sem["h_turned"], 1)

            for b in range(GB):
                prepare_turned(0, b)
            for b in range(GB):
                prepare_norms(0, b)
            prepare_input(0)

            def pe_group(g, last=False):
                done = pe.snap(g * GB)
                parity = bass.ds(g % 2, 1)
                for l in range(4):
                    for b in range(GB):
                        if l == 0:
                            pe.wait_ge(sem["h_kept"], done + (b + 1))
                        else:
                            pe.wait_ge(sem["f_kept"], g * (4 * GB) + ((l - 1) * GB + b + 1))
                        if l or b >= 2:
                            pe.wait_ge(sem["sd_kept"], g * (4 * GB) + (l * GB + b - 1))
                        for k in range(NB):
                            for t, f in enumerate(L3_ORDER[l]):
                                ins = nc.tensor.matmul(ps_sd[b % 2][:, k], fT[:, b, f, k * P:(k + 1) * P],
                                                       keep["l3_wsd"][:, sum(L3_IN[:l]) + t, :],
                                                       start=t == 0, stop=t == L3_IN[l] - 1)
                        ins.then_inc(sem["sd_made"], 1)
                    for b in range(GB):
                        pe.wait_ge(sem["sd_kept"], g * (4 * GB) + (l * GB + b + 1))
                        if l == 0:
                            pe.wait_ge(sem["h_kept"], done + GB)
                        if l or b >= 2:
                            pe.wait_ge(sem["f_kept"], g * (4 * GB) + (l * GB + b - 1))
                        acc = ps_f[b % 2][:, 0:N]
                        for t, f in enumerate(L3_ORDER[l]):
                            nc.tensor.matmul(acc, keep["l3_wn"][:, sum(L3_IN[:l]) + t, :], fT[:, b, f],
                                             start=t == 0, stop=False)
                        for k in range(NB):
                            nc.tensor.matmul(acc, sd[:, b, k, 0:D], rowT[:, parity, b, k].rearrange("p a n -> p (a n)"),
                                             start=False, stop=False)
                            ins = nc.tensor.matmul(acc, sd[:, b, k, D:2 * D], colA[:, parity, b, k].rearrange("p a n -> p (a n)"),
                                                   start=False, stop=k == NB - 1)
                        ins.then_inc(sem["f_made"], 1)
                        if not last and l == 0:
                            prepare_turned(g + 1, b)
                        if not last and l == 2:
                            prepare_norms(g + 1, b)
                if not last:
                    pe.wait_ge(sem["scaled"], done + 2 * GB)
                for b in range(GB):
                    pe.wait_ge(sem["f_kept"], g * (4 * GB) + (3 * GB + b + 1))
                    if b >= 2:
                        pe.wait_ge(sem["x_ready"], done + (b - 1))
                    for k in range(NB):
                        ins = nc.tensor.transpose(ps_turn[b % 2][:, 0, k * P:(k + 1) * P], fT[:, b, 4, k * P:(k + 1) * P], ident[:])
                    ins.then_inc(sem["f_turned"], 1)
                if not last:
                    prepare_input(g + 1)
                pe.wait_ge(sem["x_ready"], done + GB)

            with pe.Fori(0, GROUPS - 1) as g:
                pe_group(g)
            pe_group(GROUPS - 1, last=True)


def build(nc, w, out):
    with ExitStack() as stack:
        s = Scope(nc, stack, "all_")
        bc = {n: s.sb("bc_" + n, [P, D]) for n in ("L0_gnn_b", "L2_gnn_b1", "L2_gnn_g1", "L2_gnn_be1", "L2_gnn_b2",
                                                    "L2_gnn_g2", "L2_gnn_be2")}
        keep = {
            "x": s.sb("x", [P, B, NB, D]),
            "ident": s.sb("ident", [P, P]), "ones": s.sb("ones", [P, P]), "neg_half": s.sb("neg_half", [P, 16]),
            "broadcast": bc,
            "sign_sums": s.sb("sign_sums", [P, 2, B * NB]),
            "held": s.sem("held"),
            "W0": s.sb("W0", [P, D]), "att2": s.sb("att2", [P, 2]), "attb": s.sb("attb", [P, 1]),
            "W1": s.sb("W1", [P, 2, D]), "W2": s.sb("W2", [P, 2, D]),
            "l3_wsd": s.sb("l3_wsd", [P, sum(L3_IN), 2 * D]), "l3_wn": s.sb("l3_wn", [P, sum(L3_IN), D]),
            "l3_bsd": s.sb("l3_bsd", [P, 4, 2 * D]), "l3_c": s.sb("l3_c", [P, 4]),
        }
        prepare(nc, w, keep)
        layers01(nc, w, keep)
        layer2(nc, w, keep)
        layer3(nc, w, keep, out)


INPUTS = (["x", "adj", "L0_gnn_W", "L0_gnn_b", "L1_gnn_att_w", "L1_gnn_att_b"]
          + [f"L2_gnn_{n}" for n in ("W1", "b1", "g1", "be1", "W2", "b2", "g2", "be2")]
          + [f"L3_gnn_{n}{l}" for l in range(4) for n in ("ws", "bs", "wd", "bd", "wn", "bn", "wu", "bu")])


def kernel(**inputs):
    import numpy as np
    import concourse.bacc as bacc
    from concourse.bass_utils import run_bass_kernel_spmd

    nc = bacc.Bacc("TRN2", target_bir_lowering=False, num_devices=1)
    arrays, w = {}, {}
    for name in INPUTS:
        a = np.ascontiguousarray(inputs[name])
        if a.ndim == 0:
            a = a.reshape(1)
        arrays["in_" + name] = a
        w[name] = nc.dram_tensor("in_" + name, a.shape, mybir.dt.from_np(a.dtype), kind="ExternalInput").ap()
    out = nc.dram_tensor("out_x", (B, N, D), F32, kind="ExternalOutput").ap()
    build(nc, w, out)
    return run_bass_kernel_spmd(nc, [arrays], core_ids=[0]).results[0]["out_x"]
```
